# Optimizing a Trainium2 kernel written in Bass

```python
import numpy as np
import jax
import jax.numpy as jnp

def _softmax(x, axis=-1):
    return jax.nn.softmax(x, axis=axis)

def _gelu(x):
    return jax.nn.gelu(x, approximate=True)

def _silu(x):
    return jax.nn.silu(x)

def _sigmoid(x):
    return jax.nn.sigmoid(x)

def _layernorm(x, axis=-1, eps=1e-05):
    m = jnp.mean(x, axis=axis, keepdims=True)
    v = jnp.var(x, axis=axis, keepdims=True)
    return (x - m) / jnp.sqrt(v + eps)

def _scatter_add(tgt, idx, src, axis=0):
    return tgt.at[idx].add(src)

def _segment_sum(src, seg, n):
    return jax.ops.segment_sum(src, seg, n)
kernel_name = 'mk_decoder_postln_d1_seqx_r2_4d52a1'

def setup_inputs(seed: int=0):
    np.random.seed(seed)
    _w = jnp.asarray

    def _rec_inputs():
        import jax
        import jax.numpy as jnp
        _rk = jax.random.key(seed)
        x = -0.0003929 + 0.9999 * jax.random.normal(jax.random.fold_in(_rk, 1), (8, 100, 1024), jnp.float32)
        _lenS = 100 - jax.random.randint(jax.random.fold_in(_rk, 7), (8,), 0, max(1, 100 // 4) + 1, jnp.int32)
        _lenS2 = 722 - jax.random.randint(jax.random.fold_in(_rk, 8), (8,), 0, max(1, 722 // 4) + 1, jnp.int32)
        _ctx_2048P = jax.random.normal(jax.random.fold_in(_rk, 11), (8, 16, 1024), jnp.float32)
        _ctx_2048c = jax.random.dirichlet(jax.random.fold_in(_rk, 511), 0.3 * jnp.ones((16,), jnp.float32), (8, 722))
        _ctx_2048t = jnp.einsum('bsk,bkd->bsd', _ctx_2048c, _ctx_2048P)
        _ctx_2048t = _ctx_2048t * jax.lax.rsqrt(jnp.mean(jnp.square(_ctx_2048t)) + 1e-12) * 0.953939
        ctx_2048 = -1.39393e-06 + 0.999914 * (_ctx_2048t + 0.3 * jax.random.normal(jax.random.fold_in(_rk, 611), (8, 722, 1024), jnp.float32))
        itok_BxS_0_1023 = jax.random.randint(jax.random.fold_in(_rk, 12), (8, 100), 0, 512, jnp.int32)
        return (x, ctx_2048, itok_BxS_0_1023)
    x, ctx_2048, itok_BxS_0_1023 = _rec_inputs()

    def _L0_attn_setup():
        import jax, jax.numpy as jnp
        import numpy as np
        L, N, E, H = (1024, 2, 1024, 16)
        DH = E // H
        SCALE = DH ** (-0.5)
        key = jax.random.key(seed)
        k1, k2, k3 = jax.random.split(key, 3)
        x = jax.random.normal(k1, (L, N, E), dtype=jnp.float32)
        weight_qkv = jax.random.normal(k2, (3 * E, E), dtype=jnp.float32) * 0.02
        weight_out = jax.random.normal(k3, (E, E), dtype=jnp.float32) * 0.02
        return {'x': x, 'weight_qkv': weight_qkv, 'weight_out': weight_out}
    _L0_attn_all = _L0_attn_setup()
    _L0_attn_in = {k: v for k, v in _L0_attn_all.items() if k in ('weight_qkv', 'weight_out')}
    del _L0_attn_all

    def _L0_xattn_setup():
        import jax, jax.numpy as jnp
        import numpy as np
        B, Lq, Lk = (2, 2048, 512)
        Q_DIM, KV_DIM = (1024, 1024)
        H, HD = (16, 128)
        KVC, QC, R = (256, 384, 64)
        LOOKBACK = 8
        NEG = -1e+30

        def _rope(x, L):
            half = x.shape[-1] // 2
            inv_freq = 1.0 / 10000.0 ** (jnp.arange(half, dtype=jnp.float32) / half)
            ang = jnp.arange(L, dtype=jnp.float32)[:, None] * inv_freq
            cos, sin = (jnp.cos(ang), jnp.sin(ang))
            x1, x2 = (x[..., :half], x[..., half:])
            return jnp.concatenate([x1 * cos - x2 * sin, x1 * sin + x2 * cos], axis=-1)
        key = jax.random.key(seed)
        ks = jax.random.split(key, 11)

        def w(k, shape, fan_in):
            return jax.random.normal(k, shape, jnp.float32) / np.sqrt(fan_in).astype(np.float32)
        return {'q': jax.random.normal(ks[0], (B, Lq, Q_DIM), jnp.float32), 'kv': jax.random.normal(ks[1], (B, Lk, KV_DIM), jnp.float32), 'seg_id': jnp.sort(jax.random.randint(ks[2], (B, Lq), 0, Lk), axis=-1), 'W_kvc': w(ks[3], (KV_DIM, KVC), KV_DIM), 'W_dq': w(ks[4], (Q_DIM, QC), Q_DIM), 'W_uq': w(ks[5], (QC, H * HD), QC), 'W_qr': w(ks[6], (QC, H * R), QC), 'W_uk': w(ks[7], (KVC, H * HD), KVC), 'W_kr': w(ks[8], (KVC, R), KVC), 'W_uv': w(ks[9], (KVC, H * HD), KVC), 'W_o': w(ks[10], (H * HD, Q_DIM), H * HD)}
    _L0_xattn_all = _L0_xattn_setup()
    _L0_xattn_in = {k: v for k, v in _L0_xattn_all.items() if k in ('W_kvc', 'W_dq', 'W_uq', 'W_qr', 'W_uk', 'W_kr', 'W_uv', 'W_o')}
    del _L0_xattn_all

    def _L0_ffn_setup():
        import jax, jax.numpy as jnp
        import numpy as np
        B_, S, D = (2, 1024, 1024)
        F_ = 4096
        R = 16
        H = 16
        HD = D // H
        MOD_SCALE = 0.1
        EPS = 1e-06

        def _rmsnorm(x, w):
            v = jnp.mean(x * x, axis=-1, keepdims=True)
            return x * jax.lax.rsqrt(v + EPS) * w

        def _attention(x, Wq, Wk, Wv, Wo):
            b, s, d = x.shape
            q = (x @ Wq.T).reshape(b, s, H, HD)
            k = (x @ Wk.T).reshape(b, s, H, HD)
            v = (x @ Wv.T).reshape(b, s, H, HD)
            scores = jnp.einsum('bqhd,bkhd->bhqk', q, k) / np.sqrt(HD).astype(np.float32)
            causal = jnp.tril(jnp.ones((s, s), bool))
            scores = jnp.where(causal, scores, jnp.finfo(scores.dtype).min)
            probs = jax.nn.softmax(scores, axis=-1)
            out = jnp.einsum('bhqk,bkhd->bqhd', probs, v).reshape(b, s, d)
            return out @ Wo.T
        key = jax.random.key(seed)
        ks = jax.random.split(key, 12)
        sd = 0.02
        return {'hidden_states': jax.random.normal(ks[0], (B_, S, D), jnp.float32), 'ln1_w': jnp.ones((D,), jnp.float32), 'ln2_w': jnp.ones((D,), jnp.float32), 'Wq': jax.random.normal(ks[1], (D, D), jnp.float32) * sd, 'Wk': jax.random.normal(ks[2], (D, D), jnp.float32) * sd, 'Wv': jax.random.normal(ks[3], (D, D), jnp.float32) * sd, 'Wo': jax.random.normal(ks[4], (D, D), jnp.float32) * sd, 'A': jax.random.normal(ks[5], (D, R), jnp.float32) * (0.01 / np.sqrt(D)), 'B': jax.random.normal(ks[6], (R, F_), jnp.float32) * (0.01 / np.sqrt(R)), 'W_in_base': jax.random.normal(ks[7], (F_, D), jnp.float32) * sd, 'W_up_base': jax.random.normal(ks[8], (F_, D), jnp.float32) * sd, 'W_down': jax.random.normal(ks[9], (D, F_), jnp.float32) * sd}
    _L0_ffn_all = _L0_ffn_setup()
    _L0_ffn_in = {k: v for k, v in _L0_ffn_all.items() if k in ('ln1_w', 'ln2_w', 'Wq', 'Wk', 'Wv', 'Wo', 'A', 'B', 'W_in_base', 'W_up_base', 'W_down')}
    del _L0_ffn_all
    return {'x': x, 'ctx_2048': ctx_2048, 'itok_BxS_0_1023': itok_BxS_0_1023, 'L0_attn_weight_qkv': _L0_attn_in['weight_qkv'], 'L0_attn_weight_out': _L0_attn_in['weight_out'], 'L0_xattn_W_kvc': _L0_xattn_in['W_kvc'], 'L0_xattn_W_dq': _L0_xattn_in['W_dq'], 'L0_xattn_W_uq': _L0_xattn_in['W_uq'], 'L0_xattn_W_qr': _L0_xattn_in['W_qr'], 'L0_xattn_W_uk': _L0_xattn_in['W_uk'], 'L0_xattn_W_kr': _L0_xattn_in['W_kr'], 'L0_xattn_W_uv': _L0_xattn_in['W_uv'], 'L0_xattn_W_o': _L0_xattn_in['W_o'], 'L0_ffn_ln1_w': _L0_ffn_in['ln1_w'], 'L0_ffn_ln2_w': _L0_ffn_in['ln2_w'], 'L0_ffn_Wq': _L0_ffn_in['Wq'], 'L0_ffn_Wk': _L0_ffn_in['Wk'], 'L0_ffn_Wv': _L0_ffn_in['Wv'], 'L0_ffn_Wo': _L0_ffn_in['Wo'], 'L0_ffn_A': _L0_ffn_in['A'], 'L0_ffn_B': _L0_ffn_in['B'], 'L0_ffn_W_in_base': _L0_ffn_in['W_in_base'], 'L0_ffn_W_up_base': _L0_ffn_in['W_up_base'], 'L0_ffn_W_down': _L0_ffn_in['W_down']}

def reference(x, ctx_2048, itok_BxS_0_1023, L0_attn_weight_qkv, L0_attn_weight_out, L0_xattn_W_kvc, L0_xattn_W_dq, L0_xattn_W_uq, L0_xattn_W_qr, L0_xattn_W_uk, L0_xattn_W_kr, L0_xattn_W_uv, L0_xattn_W_o, L0_ffn_ln1_w, L0_ffn_ln2_w, L0_ffn_Wq, L0_ffn_Wk, L0_ffn_Wv, L0_ffn_Wo, L0_ffn_A, L0_ffn_B, L0_ffn_W_in_base, L0_ffn_W_up_base, L0_ffn_W_down):
    import jax
    import jax.numpy as jnp

    def _L0_attn_ref(x, weight_qkv, weight_out):
        import jax, jax.numpy as jnp
        import numpy as np
        L, N, E, H = (1024, 2, 1024, 16)
        DH = E // H
        SCALE = DH ** (-0.5)
        l, n, e = x.shape
        h, dh = (H, DH)
        qkv = jnp.einsum('lne,fe->lnf', x, weight_qkv)
        q, k, v = jnp.split(qkv, 3, axis=-1)
        q = q.reshape(l, n, h, dh) * jnp.asarray(SCALE, x.dtype)
        k = k.reshape(l, n, h, dh)
        v = v.reshape(l, n, h, dh)
        attn = jnp.einsum('lnhd,mnhd->nhlm', q, k)
        causal = jnp.tril(jnp.ones((l, l), dtype=bool))
        attn = jnp.where(causal, attn, jnp.asarray(-jnp.inf, attn.dtype))
        attn = jax.nn.softmax(attn, axis=-1)
        out = jnp.einsum('nhlm,mnhd->lnhd', attn, v).reshape(l, n, e)
        return jnp.einsum('lne,fe->lnf', out, weight_out)

    def _L0_xattn_ref(q, kv, seg_id, W_kvc, W_dq, W_uq, W_qr, W_uk, W_kr, W_uv, W_o):
        import jax, jax.numpy as jnp
        import numpy as np
        B, Lq, Lk = (2, 2048, 512)
        Q_DIM, KV_DIM = (1024, 1024)
        H, HD = (16, 128)
        KVC, QC, R = (256, 384, 64)
        LOOKBACK = 8
        NEG = -1e+30

        def _rope(x, L):
            half = x.shape[-1] // 2
            inv_freq = 1.0 / 10000.0 ** (jnp.arange(half, dtype=jnp.float32) / half)
            ang = jnp.arange(L, dtype=jnp.float32)[:, None] * inv_freq
            cos, sin = (jnp.cos(ang), jnp.sin(ang))
            x1, x2 = (x[..., :half], x[..., half:])
            return jnp.concatenate([x1 * cos - x2 * sin, x1 * sin + x2 * cos], axis=-1)
        b, lq, _ = q.shape
        lk = kv.shape[1]
        kv_c = kv @ W_kvc
        q_c = q @ W_dq
        q_nope = (q_c @ W_uq).reshape(b, lq, H, HD).transpose(0, 2, 1, 3)
        q_rope = (q_c @ W_qr).reshape(b, lq, H, R).transpose(0, 2, 1, 3)
        k_nope = (kv_c @ W_uk).reshape(b, lk, H, HD)
        v = (kv_c @ W_uv).reshape(b, lk, H, HD)
        k_rope = kv_c @ W_kr
        q_rope = _rope(q_rope, lq)
        k_rope = _rope(k_rope, lk)
        scale = 1.0 / np.sqrt(HD + R).astype(np.float32)
        scores = (jnp.einsum('bhqd,bkhd->bhqk', q_nope, k_nope) + jnp.einsum('bhqr,bkr->bhqk', q_rope, k_rope)) * scale
        k_ids = jnp.arange(lk)[None, None, :]
        qs = seg_id[:, :, None]
        good = (k_ids <= qs) & (k_ids >= qs - LOOKBACK)
        scores = jnp.where(good[:, None, :, :], scores, NEG)
        attn = jax.nn.softmax(scores, axis=-1)
        out = jnp.einsum('bhqk,bkhd->bqhd', attn, v).reshape(b, lq, H * HD)
        return out @ W_o

    def _L0_ffn_ref(hidden_states, ln1_w, ln2_w, Wq, Wk, Wv, Wo, A, B, W_in_base, W_up_base, W_down):
        import jax, jax.numpy as jnp
        import numpy as np
        B_, S, D = (2, 1024, 1024)
        F_ = 4096
        R = 16
        H = 16
        HD = D // H
        MOD_SCALE = 0.1
        EPS = 1e-06

        def _rmsnorm(x, w):
            v = jnp.mean(x * x, axis=-1, keepdims=True)
            return x * jax.lax.rsqrt(v + EPS) * w

        def _attention(x, Wq, Wk, Wv, Wo):
            b, s, d = x.shape
            q = (x @ Wq.T).reshape(b, s, H, HD)
            k = (x @ Wk.T).reshape(b, s, H, HD)
            v = (x @ Wv.T).reshape(b, s, H, HD)
            scores = jnp.einsum('bqhd,bkhd->bhqk', q, k) / np.sqrt(HD).astype(np.float32)
            causal = jnp.tril(jnp.ones((s, s), bool))
            scores = jnp.where(causal, scores, jnp.finfo(scores.dtype).min)
            probs = jax.nn.softmax(scores, axis=-1)
            out = jnp.einsum('bhqk,bkhd->bqhd', probs, v).reshape(b, s, d)
            return out @ Wo.T
        residual = hidden_states
        x = _rmsnorm(hidden_states, ln1_w)
        attn = _attention(x, Wq, Wk, Wv, Wo)
        mod = MOD_SCALE * jnp.tanh(attn @ A)
        h = _rmsnorm(residual, ln2_w)
        gate_pre = h @ W_in_base.T + mod * (h @ A) @ B
        gate = jax.nn.silu(gate_pre)
        up = h @ W_up_base.T
        mlp_out = gate * up @ W_down.T
        return residual + mlp_out
    x = _layernorm(x + _L0_attn_ref(x, L0_attn_weight_qkv, L0_attn_weight_out), axis=-1)
    x = _layernorm(x + _L0_xattn_ref(x, ctx_2048, itok_BxS_0_1023, L0_xattn_W_kvc, L0_xattn_W_dq, L0_xattn_W_uq, L0_xattn_W_qr, L0_xattn_W_uk, L0_xattn_W_kr, L0_xattn_W_uv, L0_xattn_W_o), axis=-1)
    x = _layernorm(x + _L0_ffn_ref(x, L0_ffn_ln1_w, L0_ffn_ln2_w, L0_ffn_Wq, L0_ffn_Wk, L0_ffn_Wv, L0_ffn_Wo, L0_ffn_A, L0_ffn_B, L0_ffn_W_in_base, L0_ffn_W_up_base, L0_ffn_W_down), axis=-1)
    return x

_drawn_inputs = setup_inputs


def setup_inputs(seed=0):
    import zlib

    import numpy as np

    out = dict(_drawn_inputs(seed))
    spreads = {'L0_ffn_ln1_w': (1.0, 0.6), 'L0_ffn_ln2_w': (1.0, 0.2)}
    factors = {'L0_ffn_Wq': 200.0,
     'L0_ffn_Wk': 200.0,
     'L0_ffn_Wv': 200.0,
     'L0_ffn_Wo': 200.0,
     'L0_ffn_A': 200.0,
     'L0_ffn_B': 200.0}
    for name, (base, spread) in spreads.items():
        noise = np.random.default_rng([zlib.crc32(name.encode()), seed]).standard_normal(out[name].shape)
        drawn = base * np.exp(spread * noise) if base else spread * noise
        out[name] = jnp.asarray(drawn.astype(out[name].dtype))
    for name, factor in factors.items():
        out[name] = (out[name] * factor).astype(out[name].dtype)
    return out
```

```python
from contextlib import ExitStack

import numpy as np
import concourse.bass as bass
from concourse import mybir

F32 = mybir.dt.float32
F32R = mybir.dt.float32r
I32 = mybir.dt.int32
U32 = mybir.dt.uint32
ALU = mybir.AluOpType
ACT = mybir.ActivationFunctionType
AX = mybir.AxisListType

P = 128
D = 1024
KC = D // P
NB, NS = 8, 100
T = NB * NS
HT = T // 2
H = 16
HP = H // 2
LK = 722
KT = -(-LK // P)
KPAD = KT * P
KVC, QC, RR = 256, 384, 64
ROW = KVC + 2 * RR
WIN = 10
GQ = 8
GK = GQ * WIN
NG = T // GQ
UG = 2
UH = NG // 2 // UG
FF = 4096
FB, FM = 4, 8
RA = 16
NEG = -1e30
SN = 13
ST = NB * SN
EPS_LN, EPS_RMS = 1e-5, 1e-6

N_SELF, N_OUT, N_KV, N_DQ, N_PAIR, N_UV, N_WO, N_QK, N_MLP = 32, 16, NB * KT, 3, 16, 4, 16, 16, 96
N_HALF = N_PAIR + N_UV + N_WO
S_SELF = 0
S_OUT = S_SELF + N_SELF
S_KV = S_OUT + N_OUT
S_DQ = S_KV + N_KV
S_HALF = S_DQ + N_DQ
S_QK = S_HALF + 2 * N_HALF
S_MLP = S_QK + N_QK
N_STRIPES = S_MLP + N_MLP

C_IDENT = 0
C_ONES = C_IDENT + P
C_PERM = C_ONES + P
C_SMASK = C_PERM + P
C_FMASK = C_SMASK + ST
C_BMASK = C_FMASK + NS
C_QCOS = C_BMASK + GK
C_QSIN = C_QCOS + NS
C_KCOS = C_QSIN + NS
C_KSIN = C_KCOS + KT * RR
C_SHIFT = C_KSIN + KT * RR
C_ISMEAN = C_SHIFT + 1
C_ROW0 = C_ISMEAN + 1
C_MEANROW = C_ROW0 + NG
C_LN1 = C_MEANROW + NG
C_LN2 = C_LN1 + KC
C_WSHIFT = C_LN2 + KC
C_BATCH = C_WSHIFT + WIN
C_ZERO = C_BATCH + NB * NB
N_CONST = C_ZERO + P


def self_group(g):
    return min(SN * g, NS - SN)


(P_SET, P_SELF, P_OUT, P_KV, P_DQ, P_PA, P_SA, P_OA, P_PB, P_SB, P_OB, P_FP, P_FA, P_FU, P_FM) = range(15)
MK = 2 * 32 + RA
RING = 10
HALF = ((P_PA, P_SA, P_OA), (P_PB, P_SB, P_OB))


class Buffers:

    def __init__(m, sb):
        m.con = sb("con", [P, N_CONST], F32)
        m.raw = [sb(f"raw{i}", [P, KC, P], F32) for i in range(2)]
        m.whi = [sb(f"whi{i}", [P, KC, P], F32R) for i in range(2)]
        m.wlo = [sb(f"wlo{i}", [P, KC, P], F32R) for i in range(2)]
        m.sums = sb("sums", [P, 2, T], F32)
        m.square = sb("square", [P, 2, HT], F32)
        m.mean = sb("mean", [P, 2, HT], F32)
        m.rstd = sb("rstd", [P, 2, HT], F32)
        m.x_raw = sb("x_raw", [P, KC, T], F32, P_SET, P_SET)
        m.xh = sb("xh", [P, KC, T], F32R, P_SET, P_KV)
        m.xl = sb("xl", [P, KC, T], F32R, P_SET, P_OUT)
        m.aoh = sb("aoh", [P, HP, NB, NS], F32R, P_SELF, P_OUT)
        m.aol = sb("aol", [P, HP, NB, NS], F32R, P_SELF, P_OUT)
        m.ah = sb("ah", [P, KC, RA], F32R)
        m.al = sb("al", [P, KC, RA], F32R)
        m.a_raw = sb("a_raw", [P, KC, RA], F32, P_SET, P_SET)
        m.wah = sb("wah", [P, HP, 2 * RA], F32R, P_SET, P_OUT)
        m.wal = sb("wal", [P, HP, 2 * RA], F32R, P_SET, P_OUT)
        m.g_raw = sb("g_raw", [P, KC, H * RA], F32, P_OUT, P_OUT)
        m.kvh = sb("kvh", [P, KC, KVC + RR], F32R, P_SET, P_KV)
        m.kvl = sb("kvl", [P, KC, KVC + RR], F32R, P_SET, P_KV)
        m.qkv = [sb(n, [P, NS, NB], F32, P_SELF, P_SELF) for n in ("q_self", "k_self", "v_self")]
        m.v_tok = sb("v_tok", [ST, 8, P], F32, P_SELF, P_SELF)
        m.probs = sb("probs", [ST, 4, 4 * ST], F32, P_SELF, P_SELF)
        m.probs_t = sb("probs_t", [ST, 4, 4 * ST], F32, P_SELF, P_SELF)
        m.peak = sb("peak", [ST, 4, 4], F32)
        m.total = sb("total", [ST, 4, 4], F32)
        m.share = sb("share", [ST, 4, 4], F32)
        m.kv_raw = sb("kv_raw", [P, KC, KVC], F32, P_SET, P_SET)
        m.y1 = sb("y1", [P, KC, T], F32, at="xh")
        m.x1h = sb("x1h", [P, KC, T], F32R, P_KV, P_DQ)
        m.x1l = sb("x1l", [P, KC, T], F32R, P_KV, P_DQ)
        m.kvc_t = sb("kvc_t", [P, 2, D], F32, P_SET, P_SET)
        m.kr_raw = sb("kr_raw", [P, 2, RR], F32, P_SET, P_SET)
        m.row = [sb(f"row{i}", [P, ROW], F32, P_KV, P_KV) for i in range(2)]
        m.rot = [sb(f"rot{i}", [P, 2, RR], F32, P_KV, P_KV) for i in range(2)]
        m.kv_sum = sb("kv_sum", [P, NB, KVC], F32, P_KV, P_KV)
        m.mean_row = sb("mean_row", [NB, ROW], F32, P_KV, P_KV)
        m.segk_i = sb("segk_i", [GK, NG], I32, P_SET, P_SET)
        m.segr_i = sb("segr_i", [P, NG], I32, P_SET, P_SET)
        m.segk = sb("segk", [GK, NG], F32, P_SET, P_SET)
        m.segr = sb("segr", [P, NG], F32, P_SET, P_SET)
        m.keyf = sb("keyf", [GK, NG], F32, P_SET, P_SET)
        m.keyi = sb("keyi", [GK, NG], U32, P_SET, P_SB)
        m.seen = sb("seen", [P, NG, WIN], F32, P_SET, P_SET)
        m.hide = sb("hide", [P, NG, WIN], F32, P_SET, P_SB)
        m.qch = [sb(f"qch{hf}", [P, 3, HT], F32R, P_DQ, (P_PA, P_PB)[hf]) for hf in range(2)]
        m.qcl = [sb(f"qcl{hf}", [P, 3, HT], F32R, P_DQ, (P_PA, P_PB)[hf]) for hf in range(2)]
        m.qa = sb("qa", [P, 2, NG // 2, H, GQ], F32, P_PA, P_OB)
        m.qr = sb("qr", [P, 2, NG // 2, H, GQ], F32, P_PA, P_OB)
        m.lath = sb("lath", [P, 2, NG // 2, H, GQ], F32R, at="qa")
        m.latl = sb("latl", [P, 2, NG // 2, H, GQ], F32R, at="qr")
        m.y2 = [sb(f"y2_{hf}", [P, KC, HT], F32, (P_OA, P_OB)[hf], P_FM) for hf in range(2)]
        m.ve = sb("ve", [P, HT], F32)
        m.root = sb("root", [P, HT], F32)
        m.tmp = sb("tmp", [P, HT], F32)
        m.qn = {}
        for ph, x in ((P_PA, "a"), (P_PB, "b")):
            m.qn[ph] = dict(
                h=sb(f"qnh_{x}", [P, 2, HT], F32R, ph, ph), l=sb(f"qnl_{x}", [P, 2, HT], F32R, ph, ph),
                r=sb(f"qraw_{x}", [P, HT], F32, ph, ph), c=sb(f"qcos_{x}", [P, HT], F32, ph, ph),
                s=sb(f"qsin_{x}", [P, HT], F32, ph, ph))
        m.sp = {}
        for ph, x in ((P_SA, "a"), (P_SB, "b")):
            m.sp[ph] = dict(
                win=[sb(f"win{i}{x}", [GK, ROW], F32, ph, ph) for i in range(RING)],
                wt=[sb(f"wt{i}{x}", [P, UG * 3, GK], F32, ph, ph) for i in range(2)],
                pr=[sb(f"pr{i}{x}", [P, UG, GK], F32, ph, ph) for i in range(2)],
                pt=[sb(f"pt{i}{x}", [GK, UG, P], F32, ph, ph) for i in range(2)],
                mk=[sb(f"mk{i}{x}", [P, UG, GK], F32, ph, ph) for i in range(2)],
                st=[sb(f"st{i}{x}", [P, 3, UG], F32, ph, ph) for i in range(2)])
        m.x1t = {ph: [sb(f"x1t{i}_{ph}", [P, HT], F32, ph, ph) for i in range(2)] for ph in (P_OA, P_OB)}
        m.rms2 = sb("rms2", [P, 2, HT], F32, P_OA, P_FU)
        m.xah = sb("xah", [P, KC, T], F32R, P_FP, P_FA)
        m.xal = sb("xal", [P, KC, T], F32R, P_FP, P_FA)
        m.g_new = sb("g_new", [P, KC, H * RA], F32, P_FP, P_FA)
        m.gh = sb("gh", [P, KC, H * RA], F32R, P_FP, P_FA)
        m.gl = sb("gl", [P, KC, H * RA], F32R, P_FP, P_FA)
        m.xa32 = [sb(f"xa32_{i}", [P, HT], F32, P_FP, P_FU) for i in range(2)]
        m.z_tok = sb("z_tok", [NS, NB, H * RA], F32, P_FP, P_FA)
        m.hh = sb("hh", [P, KC, T], F32R, P_FU, P_FM)
        m.hl = sb("hl", [P, KC, T], F32R, P_FU, P_FM)
        m.qk = [sb(n, [P, T], F32, P_FA, P_FA) for n in ("q_ffn", "k_ffn")]
        m.fprobs = sb("fprobs", [NS, 4, 4 * NS], F32, P_FA, P_FA)
        m.fprobs_t = sb("fprobs_t", [NS, 4, 4 * NS], F32, P_FA, P_FA)
        m.m_tok = sb("m_tok", [NS, NB, RA], F32, P_FA, P_FU)
        m.tanh_m = sb("tanh_m", [RA, T], F32, P_FU, P_FU)
        m.u_raw = sb("u_raw", [RA, T], F32, P_FU, P_FU)
        m.ustk = sb("ustk", [MK, T], F32R, P_FU, P_FM)
        m.b_raw = sb("b_raw", [MK, FF], F32, P_FU, P_FM)
        m.bstk = sb("bstk", [MK, P], F32R, P_FM, P_FM)
        m.ffh = sb("ffh", [P, FM, T], F32R, P_FM, P_FM)
        m.ffl = sb("ffl", [P, FM, T], F32R, P_FM, P_FM)
        m.gate = [sb(f"gate{i}", [P, HT], F32, P_FM, P_FM) for i in range(2)]
        m.act32 = [sb(f"act32_{i}", [P, HT], F32, P_FM, P_FM) for i in range(2)]


def place(nc):
    wanted, placed = [], {}

    def note(name, shape, dt, first=P_SET, last=P_FM, at=None):
        if at is None:
            size = -(-int(np.prod(shape[1:])) * 4 // 64) * 64
            wanted.append((-size, name, first, last))

    Buffers(note)
    for less, name, first, last in sorted(wanted):
        size = -less
        at = -(-nc.sbuf_base // 64) * 64
        for a, b in sorted((a, b) for a, b, f, l in placed.values() if not (l < first or f > last)):
            if at + size > a and at < b:
                at = b
        placed[name] = (at, at + size, first, last)
        assert at + size <= nc.sbuf_usable_end, name

    def alloc(name, shape, dt, first=P_SET, last=P_FM, at=None):
        return nc.alloc_sbuf_tensor_at(name, shape, dt, offset=placed[at or name][0])

    return Buffers(alloc)


class Steps:

    def __init__(self):
        self.base, self.k = 0, 0

    def next(self):
        self.k += 1
        return 1

    def so_far(self):
        return self.base + self.k

    def loop(self, i, start, stop, per):
        self.base, self.k = self.base + self.k, 0
        self.after = self.base + (stop - start) * per
        self.base, self.per = self.base + (i - start) * per, per

    def close(self):
        assert self.k == self.per, self.k
        self.base, self.k = self.after, 0


SIGNALS = """
con_loaded aux_loaded seg_loaded x_raw_0 x_raw_1 x_raw_2 x_raw_3 raw_loaded_0 raw_loaded_1
w_hi w_lo dve_step 
set_hi set_lo key_index wa_zero fold_done
self_q self_k self_v self_s self_vt self_pt self_pv self_wo
q_evac k_evac v_evac s_taken s_centered s_exp s_probs vt_evac pt_evac ao_hi ao_lo wa_hi wa_lo
out_done wv_done y1_read y1_done square_done square_added g_evac g_stored
stat_sums stat_taken stat_var stat_root stat_rstd 
kv_done kv_copied kv_read row_ready row_stored_0 row_stored_1 ln1_z ln1_hi ln1_lo x1_stored mean_done mean_ready
mean_stored
dq_done qc_hi qc_lo
uq_done qr_done ukA_done ukB_done qr_half perm_done qn_hi qn_lo qr_raw qa_act qa_dve q_rot qr_zero
gathered_0 gathered_1 gathered_2 gathered_3 gathered_4 gathered_5 gathered_6 gathered_7 gathered_8 gathered_9
wt_done wt_evac win_mask win_s win_taken win_centered win_exp win_probs win_pt win_pt_evac win_lat lat_hi lat_lo
uv_done vo_hi vo_lo wo_half wo_done x1_back_0 x1_back_1 y2_done x2_done
g_back g_hi g_lo in_ready in_hi in_lo z_done z_evac
fq_done fk_done f_s f_pt f_pv fq_evac fk_evac f_taken f_centered f_exp f_probs f_pt_evac 
m_evac mt_done m_tanh ha_done u_ready u_hi u_lo y_twice b_loaded b_hi b_lo b_zero u_zero
ff_gate ff_up silu_done ff_prod ff_hi ff_lo down_done down_added final_done out_stored
""".split()



def ao_parts(t, C, a):
    last = self_group(7) + SN - 7 * SN
    parts = []
    for bank, first, stop, n0 in ((0, 0, 4 * SN, 0), (1, 0, 3 * SN, 4 * SN), (1, 4 * SN - last, 4 * SN, 7 * SN)):
        parts.append((t[:, a, :, n0:n0 + stop - first],
                      C[bank][:, NB * first:NB * stop].rearrange("p (n l) -> p l n", l=NB)))
    return parts


def lat_parts(t, C, u):
    src = C[u % 2][:, :].rearrange("p (g c r) -> p c g r", g=UG, c=2)
    return [(t[:, c, UG * u:UG * u + UG, :, :].rearrange("p g h q -> p g (h q)"), src[:, c]) for c in range(2)]


def build(nc, xT, stripes, w_kvc, w_kvcT, w_kr, mod_a, mod_b, seg_rows, seg_keys, const, key_table,
          x1_dram, g_dram, out):
    with ExitStack() as ctx:
        m = place(nc)
        bank = [ctx.enter_context(nc.psum_tensor(f"bank{i}", [P, 512], F32)) for i in range(8)]
        G, A, C = bank[0:2], bank[2:6], bank[6:8]
        sem = {n: ctx.enter_context(nc.semaphore(n)) for n in SIGNALS}
        con, raw, whi, wlo = m.con, m.raw, m.whi, m.wlo
        ident = con[:, C_IDENT:C_IDENT + P]
        ones = con[:, C_ONES:C_ONES + P]

        def positive(n):
            return not isinstance(n, int) or n > 0

        def half(t, hf):
            return t[:, hf * HT:(hf + 1) * HT]

        def grouped(t):
            return t.rearrange("p (g q) -> p g q", q=GQ)

        block = ctx.enter_context(nc.Block())

        @block.sync
        def _(sp):
            for c in range(4):
                sp.dma_start(m.x_raw[:, 2 * c:2 * c + 2, :], xT[:, 2 * c:2 * c + 2, :]).then_inc(sem[f"x_raw_{c}"], 16)
                if c < 2:
                    sp.dma_start(raw[c][:, :, :], stripes[c]).then_inc(sem[f"raw_loaded_{c}"], 16)
            with sp.Fori(1, N_STRIPES // 2) as j:
                for i in range(2):
                    sp.wait_ge(sem["w_lo"], 2 * j - 1 + i)
                    sp.dma_start(raw[i][:, :, :], stripes[2 * j + i]).then_inc(sem[f"raw_loaded_{i}"], 16)
            if N_STRIPES % 2:
                sp.wait_ge(sem["w_lo"], N_STRIPES - 2)
                sp.dma_start(raw[0][:, :, :], stripes[N_STRIPES - 1]).then_inc(sem["raw_loaded_0"], 16)
            for kc in range(KC):
                for u in range(2):
                    sp.wait_ge(sem["final_done"], 2 * kc + u + 1)
                    sp.dma_start(half(out[:, kc, :], u), m.y2[u][:, kc, :]).then_inc(sem["out_stored"], 16)
            sp.wait_ge(sem["out_stored"], 32 * KC)

        @block.gpsimd
        def _(pool):
            def low(s, slot):
                pool.wait_ge(sem["w_hi"], s + 1)
                pool.tensor_tensor(wlo[slot][:, :, :], raw[slot][:, :, :], whi[slot][:, :, :].bitcast(F32),
                                   ALU.subtract).then_inc(sem["w_lo"], 1)

            def lows(first, n):
                if n < 4:
                    for s in range(first, first + n):
                        low(s, s % 2)
                    return
                with pool.Fori(0, n // 2) as j:
                    for i in range(2):
                        low(2 * j + first + i, (first + i) % 2)
                if n % 2:
                    low(first + n - 1, (first + n - 1) % 2)

            lows(0, S_HALF)
            for hf in range(2):
                p_pair, p_win, _ = HALF[hf]
                s0 = S_HALF + hf * N_HALF
                pool.wait_ge(sem["dq_done"], 6)
                if positive(HP * hf):
                    pool.wait_ge(sem["wo_done"], HP * hf)
                turned = m.qr[:, 0, :, :, :].rearrange("p g (h e) q -> p g h e q", e=2)
                pool.wait_ge(sem["w_lo"], s0)
                for e in range(2):
                    pool.memset(turned[64 - 64 * e:128 - 64 * e, :, :, e, :], 0.0).then_inc(sem["qr_zero"], 1)
                    pool.wait_ge(sem["qr_zero"], 2 * hf + e + 1)
                with pool.Fori(0, HP) as hp:
                    for i in range(2):
                        low(2 * hp + s0 + i, (s0 + i) % 2)
                if hf == 0:
                    pool.wait_ge(sem["row_stored_0"], 16 * N_KV // 2)
                    pool.wait_ge(sem["row_stored_1"], 16 * N_KV // 2)
                    pool.wait_ge(sem["mean_stored"], 16)
                    pool.wait_ge(sem["key_index"], 1)
                pool.wait_ge(sem["perm_done"], HP * (hf + 1))
                pool.wait_ge(sem["q_rot"], 2 * HP * (hf + 1))
                w = m.sp[p_win]
                for u in range(UH):
                    if u >= RING // UG:
                        pool.wait_ge(sem["win_lat"], UH * hf + u - RING // UG + 1)
                    for gi in range(UG):
                        g = hf * NG // 2 + UG * u + gi
                        r = (UG * u + gi) % RING
                        pool.indirect_dma_start(
                            out=w["win"][r][:, :], out_offset=None, in_=key_table,
                            in_offset=bass.IndirectOffsetOnAxis(ap=m.keyi[:, g:g + 1], axis=0),
                        ).then_inc(sem[f"gathered_{r}"], 16)
                    if u >= 2:
                        pool.wait_ge(sem["win_taken"], UH * hf + u - 1)
                    for gi in range(UG):
                        g = hf * NG // 2 + UG * u + gi
                        ins = pool.tensor_tensor(
                            w["mk"][u % 2][:, gi, :].rearrange("p (q j) -> p q j", j=WIN),
                            con[:, C_BMASK:C_BMASK + GK].rearrange("p (q j) -> p q j", j=WIN),
                            m.hide[:, g, :].unsqueeze(1).to_broadcast([P, GQ, WIN]), ALU.add)
                    ins.then_inc(sem["win_mask"], 1)
                lows(s0 + N_PAIR, N_UV + N_WO)
            lows(S_QK, N_QK + N_MLP)

        @block.scalar
        def _(act):
            def high(k, i, per):
                act.wait_ge(sem[f"raw_loaded_{k % 2}"], 16 * (k // 2 + 1) + 8 * per * i)
                act.activation(whi[k % 2][:, :, :], raw[k % 2][:, :, :], ACT.Copy).then_inc(sem["w_hi"], 1)

            for dst, src in ((con[:, :], const), (m.a_raw[:, :, :], mod_a), (m.kv_raw[:, :, :], w_kvc),
                             (m.kvc_t[:, :, :], w_kvcT), (m.kr_raw[:, :, :], w_kr)):
                act.dma_start(dst, src).then_inc(sem["con_loaded" if src is const else "aux_loaded"], 16)
            act.dma_start(m.segk_i[:, :], seg_keys).then_inc(sem["seg_loaded"], 16)
            act.dma_start(m.segr_i[:, :], seg_rows).then_inc(sem["seg_loaded"], 16)
            for c in range(4):
                act.wait_ge(sem[f"x_raw_{c}"], 16)
                act.activation(m.xh[:, 2 * c:2 * c + 2, :], m.x_raw[:, 2 * c:2 * c + 2, :], ACT.Copy)\
                   .then_inc(sem["set_hi"], 1)
                if c == 0:
                    high(0, 0, 0)
            act.wait_ge(sem["aux_loaded"], 64)
            act.activation(m.ah[:, :, :], m.a_raw[:, :, :], ACT.Copy).then_inc(sem["set_hi"], 1)
            act.activation(m.kvh[:, :, 0:KVC], m.kv_raw[:, :, :], ACT.Copy).then_inc(sem["set_hi"], 1)

            def self_act(i, product, attn):
                a = i - 1

                def exps(j):
                    act.wait_ge(sem["s_centered"], 4 * a + j + 1)
                    act.activation(m.probs[:, j, :], m.probs[:, j, :], ACT.Exp).then_inc(sem["s_exp"], 1)

                def evac(u, done, t, name):
                    act.wait_ge(sem[done], 2 * i + u + 1)
                    act.activation(t[:, :, u * NB // 2:(u + 1) * NB // 2].rearrange("p n b -> p b n"), G[u][:, 0:HT].rearrange("p (b n) -> p b n", n=NS), ACT.Copy)\
                       .then_inc(sem[name], 1)

                if product:
                    if positive(i):
                        act.wait_ge(sem["self_wo"], i)
                    high(S_SELF + 1, i, 4)
                if attn:
                    exps(0)
                    exps(1)
                if product:
                    evac(0, "self_q", m.qkv[0][:, :, :], "q_evac")
                if attn:
                    exps(2)
                    exps(3)
                if product:
                    evac(1, "self_q", m.qkv[0][:, :, :], "q_evac")
                    act.wait_ge(sem["self_q"], 2 * i + 2)
                    high(S_SELF + 2, i, 4)
                    for u in range(2):
                        evac(u, "self_k", m.qkv[1][:, :, :], "k_evac")
                    act.wait_ge(sem["self_k"], 2 * i + 2)
                    high(S_SELF + 3, i, 4)
                if attn:
                    for j in range(4):
                        act.wait_ge(sem["self_pt"], 4 * a + j + 1)
                        act.activation(m.probs_t[:, j, :], A[j][0:ST, 0:4 * ST], ACT.Copy).then_inc(sem["pt_evac"], 1)
                if product:
                    for u in range(2):
                        evac(u, "self_v", m.qkv[2][:, :, :], "v_evac")
                    act.wait_ge(sem["self_v"], 2 * i + 2)
                    high(S_SELF + 4, i, 4)
                if attn:
                    for dst, src in ao_parts(m.aoh, C, a):
                        act.wait_ge(sem["self_pv"], a + 1)
                        act.activation(dst, src, ACT.Copy).then_inc(sem["ao_hi"], 1)
                if product:
                    act.wait_ge(sem["self_wo"], i + 1)
                    act.wait_ge(sem["wa_zero"], 2)
                    for e in range(2):
                        act.activation(m.wah[64 * e:64 * e + 64, i, RA * e:RA * e + RA], G[0][64 * e:64 * e + 64, 0:RA], ACT.Copy)\
                           .then_inc(sem["wa_hi"], 1)

            self_act(0, True, False)
            act.wait_ge(sem["fold_done"], 1)
            act.activation(m.kvh[:, :, KVC:KVC + RR], C[0][:, :].rearrange("p (k r) -> p k r", r=RR), ACT.Copy)\
               .then_inc(sem["set_hi"], 1)
            self_act(1, True, True)
            with act.Fori(2, HP) as i:
                self_act(i, True, True)
            self_act(HP, False, True)

            def out_act(i):
                if isinstance(i, int) and i == 0:
                    act.wait_ge(sem["self_wo"], HP)
                    high(S_OUT + 1, i, 2)
                else:
                    act.wait_ge(sem["wv_done"], i)
                    high(S_OUT + 1, i, 2)
                act.wait_ge(sem["out_done"], 2 * i + 2)
                high(S_OUT + 2, i, 2)
                for u in range(2):
                    act.wait_ge(sem["y1_done"], 2 * i + u + 1)
                    if positive(2 * i + u - 1 if not isinstance(i, int) or i else 0):
                        act.wait_ge(sem["square_added"], 2 * i + u - 1 if not isinstance(i, int) or i else 0)
                    act.activation(m.square[:, u, :], half(m.y1[:, i, :], u), ACT.Square).then_inc(sem["square_done"], 1)
                act.wait_ge(sem["wv_done"], i + 1)
                act.activation(m.g_raw[:, :, bass.ds(2 * RA * i, 2 * RA)], G[0][:, 0:KC * 2 * RA].rearrange("p (k r) -> p k r", r=2 * RA), ACT.Copy)\
                   .then_inc(sem["g_evac"], 1)

            out_act(0)
            with act.Fori(1, HP) as i:
                out_act(i)
            act.wait_ge(sem["g_evac"], HP)
            act.dma_start(g_dram, m.g_raw[:, :, :]).then_inc(sem["g_stored"], 16)

            def root(n):
                act.wait_ge(sem["stat_var"], n)
                act.activation(m.root[:, :], m.ve[:, :], ACT.Sqrt).then_inc(sem["stat_root"], 1)

            root(1)
            root(2)

            def store_row(n, i):
                act.wait_ge(sem["row_ready"], n + 1 + KT * i)
                act.wait_ge(sem["kv_copied"], n + 1 + KT * i)
                act.dma_start(key_table[bass.ds((n + KT * i) * P, P), :] if not isinstance(i, int)
                              else key_table[(n + KT * i) * P:(n + KT * i + 1) * P, :],
                              m.row[n % 2][:, :]).then_inc(sem[f"row_stored_{n % 2}"], 16)

            def kv_act(b):
                first = isinstance(b, int) and b == 0
                for ti in range(KT):
                    if first and ti == 0:
                        act.wait_ge(sem["wv_done"], HP)
                        high(S_KV + 1, 0, 0)
                    else:
                        act.wait_ge(sem["kv_done"], KT * b + ti)
                        high(S_KV + ti + 1, b, KT)
                    act.wait_ge(sem["kv_done"], KT * b + ti + 1)
                    if not (first and ti < 2):
                        act.wait_ge(sem[f"row_stored_{ti % 2}"], 16 * (KT // 2 * b + ti // 2))
                    act.activation(m.row[ti % 2][:, 0:KVC], G[ti % 2][:, 0:KVC], ACT.Copy)\
                       .then_inc(sem["kv_copied"], 1)
                    if not (first and ti == 0):
                        if ti:
                            store_row(ti - 1, b)
                        else:
                            store_row(KT - 1, b - 1)
                    if ti == 0:
                        for u in range(2):
                            act.wait_ge(sem["ln1_z"], 2 * b + u + 1)
                            act.activation(half(m.x1h[:, b, :], u), half(m.y1[:, b, :], u), ACT.Copy)\
                               .then_inc(sem["ln1_hi"], 1)
                        act.dma_start(x1_dram[:, b, :], m.y1[:, b, :]).then_inc(sem["x1_stored"], 16)

            kv_act(0)
            with act.Fori(1, NB) as b:
                kv_act(b)
            store_row(KT - 1, NB - 1)
            act.wait_ge(sem["mean_done"], 1)
            act.activation(m.mean_row[:, 0:KVC], G[0][0:NB, 0:KVC], ACT.Copy, scale=1.0 / LK).then_inc(sem["mean_ready"], 1)
            act.wait_ge(sem["mean_ready"], 2)
            act.dma_start(key_table[NB * KPAD:NB * KPAD + NB, :], m.mean_row[:, :]).then_inc(sem["mean_stored"], 16)

            for k in range(3):
                act.wait_ge(sem["dq_done" if k else "kv_done"], 2 * k if k else N_KV)
                high(S_DQ + k + 1, 0, 0)
                for u in range(2):
                    act.wait_ge(sem["dq_done"], 2 * k + u + 1)
                    act.activation(m.qch[u][:, k, :], G[u][:, 0:HT], ACT.Copy).then_inc(sem["qc_hi"], 1)

            for hf in range(2):
                p_pair, p_win, p_out = HALF[hf]
                s0 = S_HALF + hf * N_HALF
                q = m.qn[p_pair]

                def pair_act(hp):
                    n = HP * hf + hp
                    if isinstance(hp, int) and hp == 0:
                        act.wait_ge(sem["wo_done" if hf else "dq_done"], HP if hf else 6)
                        high(s0 + 1, 0, 0)
                    else:
                        act.wait_ge(sem["ukB_done"], 2 * n)
                        high(s0 + 1, hp, 2)
                    for u in range(2):
                        act.wait_ge(sem["uq_done"], 2 * n + u + 1)
                        act.activation(q["h"][:, u, :], G[u][:, 0:HT], ACT.Copy).then_inc(sem["qn_hi"], 1)
                    act.wait_ge(sem["qr_done"], n + 1)
                    if positive(2 * n):
                        act.wait_ge(sem["q_rot"], 2 * n)
                    act.activation(q["r"][:, :], A[0][:, 0:HT], ACT.Copy).then_inc(sem["qr_raw"], 1)
                    act.wait_ge(sem["qr_half"], n + 1)
                    high(s0 + 2, hp, 2)
                    for c in range(2):
                        act.wait_ge(sem["ukA_done"], 2 * n + c + 1)
                        act.activation(m.qa[:, c, :, 2 * hp, :], grouped(A[2 + c][:, 0:HT]), ACT.Copy)\
                           .then_inc(sem["qa_act"], 1)

                pair_act(0)
                with act.Fori(1, HP) as hp:
                    pair_act(hp)

                w = m.sp[p_win]
                for v in range(UH + 3):
                    if v < UH:
                        n = UH * hf + v
                        act.wait_ge(sem["wt_done"], n + 1)
                        if positive(n - 1):
                            act.wait_ge(sem["win_s"], n - 1)
                        act.activation(w["wt"][v % 2][:, :, :], G[v % 2][:, 0:UG * 3 * GK].rearrange("p (a k) -> p a k", k=GK), ACT.Copy)\
                           .then_inc(sem["wt_evac"], 1)
                    if 2 <= v < UH + 2:
                        u, n = v - 2, UH * hf + v - 2
                        act.wait_ge(sem["win_pt"], n + 1)
                        act.activation(w["pt"][u % 2][:, :, :], A[2 + u % 2][0:GK, 0:UG * P].rearrange("p (a k) -> p a k", k=P), ACT.Copy)\
                           .then_inc(sem["win_pt_evac"], 1)
                    if 1 <= v < UH + 1:
                        u, n = v - 1, UH * hf + v - 1
                        act.wait_ge(sem["win_centered"], n + 1)
                        act.activation(w["pr"][u % 2][:, :, :], w["pr"][u % 2][:, :, :], ACT.Exp)\
                           .then_inc(sem["win_exp"], 1)
                    if v >= 3:
                        u, n = v - 3, UH * hf + v - 3
                        act.wait_ge(sem["win_lat"], n + 1)
                        for dst, src in lat_parts(m.lath, C, u):
                            act.activation(dst, src, ACT.Copy).then_inc(sem["lat_hi"], 1)

                for i in range(N_UV):
                    act.wait_ge(sem["uv_done" if i else "ukB_done"], H * hf + 4 * i if i else H * (hf + 1))
                    high(s0 + N_PAIR + i + 1, 0, 0)
                    for h in range(4 * i, 4 * i + 4):
                        act.wait_ge(sem["uv_done"], H * hf + h + 1)
                        act.activation(m.lath[:, 0, :, h, :], grouped(G[h % 2][:, 0:HT]), ACT.Copy)\
                           .then_inc(sem["vo_hi"], 1)

                x1t = m.x1t[p_out]

                def fetch(k, i):
                    if positive(HP * hf + k + 2 * i - 1):
                        act.wait_ge(sem["y2_done"], HP * hf + k + 2 * i - 1)
                    act.dma_start(x1t[k % 2][:, :], half(x1_dram[:, k + 2 * i, :], hf)).then_inc(sem[f"x1_back_{k % 2}"], 16)

                act.wait_ge(sem["x1_stored"], 16 * KC)
                fetch(0, 0)
                fetch(1, 0)

                def wo_act(i):
                    first = isinstance(i, int) and i == 0
                    for k in range(2):
                        n = HP * hf + 2 * i + k
                        if first and k == 0:
                            act.wait_ge(sem["uv_done"], H * (hf + 1))
                            high(s0 + N_PAIR + N_UV + 1, 0, 0)
                        else:
                            act.wait_ge(sem["wo_done"], n)
                            high(s0 + N_PAIR + N_UV + 2 * k + 1, i, 4)
                        act.wait_ge(sem["wo_half"], n + 1)
                        high(s0 + N_PAIR + N_UV + 2 * k + 2, i, 4)
                        act.wait_ge(sem["y2_done"], n + 1)
                        if not (hf == 0 and first):
                            act.wait_ge(sem["square_added"], 2 * HP + n - 1)
                        act.activation(m.square[:, k, :], m.y2[hf][:, 2 * i + k, :], ACT.Square)\
                           .then_inc(sem["square_done"], 1)
                        if not (isinstance(i, int) and i == HP // 2 - 1):
                            fetch(2 + k, i)

                wo_act(0)
                with act.Fori(1, HP // 2 - 1) as i:
                    wo_act(i)
                wo_act(HP // 2 - 1)
                root(3 + 2 * hf)
                root(4 + 2 * hf)

            act.wait_ge(sem["g_stored"], 16)
            act.dma_start(m.g_new[:, :, :], g_dram).then_inc(sem["g_back"], 16)
            for n in range(2 * KC):
                u, kc = n // KC, n % KC
                act.wait_ge(sem["in_ready"], n + 1)
                act.activation(half(m.xah[:, kc, :], u), m.xa32[n % 2][:, :], ACT.Copy).then_inc(sem["in_hi"], 1)
            act.wait_ge(sem["g_back"], 16)
            act.activation(m.gh[:, :, :], m.g_new[:, :, :], ACT.Copy).then_inc(sem["g_hi"], 1)

            def ffn_act(i, product, attn, pt=True):
                a = i - 1

                def exps(j):
                    act.wait_ge(sem["f_centered"], 4 * a + j + 1)
                    act.activation(m.fprobs[:, j, :], m.fprobs[:, j, :], ACT.Exp).then_inc(sem["f_exp"], 1)

                def evac(u, done, t, name):
                    act.wait_ge(sem[done], 2 * i + u + 1)
                    act.activation(half(t[:, :], u), G[u][:, 0:HT], ACT.Copy).then_inc(sem[name], 1)

                if product:
                    if isinstance(i, int) and i == 0:
                        act.wait_ge(sem["wo_done"], 2 * HP)
                        high(S_QK + 1, i, 2)
                    else:
                        act.wait_ge(sem["fk_done"], 2 * i)
                        high(S_QK + 1, i, 2)
                if attn:
                    exps(0)
                    exps(1)
                if product:
                    evac(0, "fq_done", m.qk[0], "fq_evac")
                if attn:
                    exps(2)
                    exps(3)
                if product:
                    evac(1, "fq_done", m.qk[0], "fq_evac")
                    act.wait_ge(sem["fq_done"], 2 * i + 2)
                    high(S_QK + 2, i, 2)
                    evac(0, "fk_done", m.qk[1], "fk_evac")
                if attn:
                    for j in range(4):
                        act.wait_ge(sem["f_pt"], 4 * a + j + 1)
                        act.activation(m.fprobs_t[:, j, :], A[j][0:NS, 0:4 * NS], ACT.Copy)\
                           .then_inc(sem["f_pt_evac"], 1)
                if product:
                    evac(1, "fk_done", m.qk[1], "fk_evac")

            ffn_act(0, True, False)
            act.wait_ge(sem["z_done"], NB)
            ffn_act(1, True, True)
            with act.Fori(2, HP) as i:
                ffn_act(i, True, True)
            ffn_act(HP, False, True)
            act.wait_ge(sem["f_pv"], HP)
            act.activation(m.m_tok[:, :, :], C[0][0:NS, 0:NB * RA].rearrange("p (b r) -> p b r", r=RA), ACT.Copy)\
               .then_inc(sem["m_evac"], 1)
            for n in range(2 * KC):
                u, kc = n // KC, n % KC
                act.wait_ge(sem["in_ready"], 2 * KC + n + 1)
                act.activation(half(m.hh[:, kc, :], u), m.xa32[n % 2][:, :], ACT.Copy).then_inc(sem["in_hi"], 1)
                if n == 0:
                    act.wait_ge(sem["b_zero"], 1)
                    for r in range(3):
                        act.dma_start(m.b_raw[32 * r:32 * r + RA, :], mod_b).then_inc(sem["b_loaded"], 16)
            for u in range(2):
                act.wait_ge(sem["mt_done"], 2)
                act.activation(half(m.tanh_m[:, :], u), A[u][0:RA, 0:HT], ACT.Tanh).then_inc(sem["m_tanh"], 1)
            act.wait_ge(sem["u_zero"], 1)
            for u in range(2):
                act.wait_ge(sem["u_ready"], u + 1)
                for r in (0, 64):
                    act.activation(half(m.ustk[r:r + RA, :], u), half(m.u_raw[:, :], u), ACT.Copy)\
                       .then_inc(sem["u_hi"], 1)

            def b_high(f):
                if positive(2 * f):
                    act.wait_ge(sem["ff_gate"], 2 * f)
                act.activation(m.bstk[:, :], m.b_raw[:, bass.ds(f * P, P)] if not isinstance(f, int)
                     else m.b_raw[:, f * P:(f + 1) * P], ACT.Copy).then_inc(sem["b_hi"], 1)

            act.wait_ge(sem["b_loaded"], 48)

            def up_act(fb, fm):
                f = FM * fb + fm
                b_high(f)
                if isinstance(f, int) and f == 0:
                    act.wait_ge(sem["fk_done"], 2 * HP)
                    high(S_MLP + 1, 0, 0)
                elif isinstance(fm, int) and fm == 0:
                    act.wait_ge(sem["down_done"], 2 * FM * fb)
                    high(S_MLP + 1, fb, 24)
                else:
                    act.wait_ge(sem["ff_up"], 2 * f)
                    high2(S_MLP + 1, fb, fm)
                for u in range(2):
                    act.wait_ge(sem["ff_gate"], 2 * f + u + 1)
                    if not (isinstance(f, int) and f == 0):
                        act.wait_ge(sem["ff_prod"], 2 * f + u - 1)
                    act.activation(m.gate[u][:, :], G[u][:, 0:HT], ACT.Silu).then_inc(sem["silu_done"], 1)
                act.wait_ge(sem["ff_gate"], 2 * f + 2)
                high2(S_MLP + 2, fb, fm)
                for u in range(2):
                    act.wait_ge(sem["ff_prod"], 2 * f + u + 1)
                    act.activation(half(m.ffh[:, fm, :], u), m.act32[u][:, :], ACT.Copy).then_inc(sem["ff_hi"], 1)

            def high2(k, fb, fm):
                act.wait_ge(sem[f"raw_loaded_{k % 2}"], 16 * (k // 2 + 1) + 16 * 12 * fb + 16 * fm)
                act.activation(whi[k % 2][:, :, :], raw[k % 2][:, :, :], ACT.Copy).then_inc(sem["w_hi"], 1)

            def down_act(fb, c, i, last):
                n = FM * fb + c + 2 * i
                if not (last and isinstance(i, int) and i == KC // 2 - 1 and c == 1):
                    k = S_MLP + 2 * FM + c + 1
                    if c == 0 and isinstance(i, int) and i == 0:
                        act.wait_ge(sem["ff_up"], 2 * FM * (fb + 1))
                        high2(k, fb, i)
                    else:
                        act.wait_ge(sem["down_done"], 2 * n)
                        high2(k, fb, i)
                if last:
                    for u in range(2):
                        n3 = 2 * (c + 2 * i) + u
                        act.wait_ge(sem["down_added"], 2 * n + u + 1)
                        if not (isinstance(i, int) and i == 0 and c == 0):
                            act.wait_ge(sem["square_added"], 4 * HP + n3 - 1)
                        act.activation(m.square[:, u, :], m.y2[u][:, c + 2 * i, :], ACT.Square)\
                           .then_inc(sem["square_done"], 1)

            def block_act(fb, last):
                up_act(fb, 0)
                with act.Fori(1, FM) as fm:
                    up_act(fb, fm)
                for c in range(2):
                    down_act(fb, c, 0, last)
                with act.Fori(1, KC // 2 - 1) as i:
                    for c in range(2):
                        down_act(fb, c, i, last)
                for c in range(2):
                    down_act(fb, c, KC // 2 - 1, last)

            block_act(0, False)
            with act.Fori(1, FB - 1) as fb:
                block_act(fb, False)
            block_act(FB - 1, True)
            root(7)
            root(8)

        @block.vector
        def _(dve):
            steps = Steps()

            dve.memset(m.sums[:, :, :], 0.0).then_inc(sem["dve_step"], steps.next())
            dve.memset(m.wah[:, :, :].bitcast(F32), 0.0).then_inc(sem["wa_zero"], 1)
            dve.memset(m.wal[:, :, :].bitcast(F32), 0.0).then_inc(sem["wa_zero"], 1)
            for kc in range(KC):
                dve.wait_ge(sem[f"x_raw_{kc // 2}"], 16)
                dve.wait_ge(sem["set_hi"], kc // 2 + 1)
                dve.tensor_tensor(m.xl[:, kc, :], m.x_raw[:, kc, :], m.xh[:, kc, :].bitcast(F32), ALU.subtract)\
                   .then_inc(sem["set_lo"], 1)
            dve.wait_ge(sem["set_hi"], 5)
            dve.wait_ge(sem["aux_loaded"], 64)
            dve.tensor_tensor(m.al[:, :, :], m.a_raw[:, :, :], m.ah[:, :, :].bitcast(F32), ALU.subtract)\
               .then_inc(sem["set_lo"], 1)
            dve.wait_ge(sem["set_hi"], 6)
            dve.tensor_tensor(m.kvl[:, :, 0:KVC], m.kv_raw[:, :, :], m.kvh[:, :, 0:KVC].bitcast(F32), ALU.subtract)\
               .then_inc(sem["set_lo"], 1)
            dve.wait_ge(sem["fold_done"], 1)
            dve.wait_ge(sem["set_hi"], 7)
            dve.tensor_tensor(m.kvl[:, :, KVC:KVC + RR], C[0][:, :].rearrange("p (k r) -> p k r", r=RR), m.kvh[:, :, KVC:KVC + RR].bitcast(F32), ALU.subtract)\
               .then_inc(sem["set_lo"], 1)
            dve.wait_ge(sem["con_loaded"], 16)
            dve.wait_ge(sem["seg_loaded"], 32)
            dve.tensor_copy(m.segk[:, :], m.segk_i[:, :]).then_inc(sem["dve_step"], steps.next())
            dve.tensor_copy(m.segr[:, :], m.segr_i[:, :]).then_inc(sem["dve_step"], steps.next())
            dve.wait_ge(sem["dve_step"], steps.so_far())
            dve.tensor_scalar(m.keyf[:, :], m.segk[:, :], con[0:GK, C_SHIFT:C_SHIFT + 1], 0.0, ALU.add, ALU.max)\
               .then_inc(sem["dve_step"], steps.next())
            dve.wait_ge(sem["dve_step"], steps.so_far())
            dve.tensor_scalar(m.keyf[:, :], m.keyf[:, :], float(LK - 1), None, ALU.min)\
               .then_inc(sem["dve_step"], steps.next())
            dve.wait_ge(sem["dve_step"], steps.so_far())
            dve.tensor_tensor(m.keyf[:, :], m.keyf[:, :], con[0:GK, C_ROW0:C_ROW0 + NG], ALU.add)\
               .then_inc(sem["dve_step"], steps.next())
            dve.wait_ge(sem["dve_step"], steps.so_far())
            dve.tensor_tensor(m.segk[:, :], con[0:GK, C_MEANROW:C_MEANROW + NG], m.keyf[:, :], ALU.subtract)\
               .then_inc(sem["dve_step"], steps.next())
            dve.wait_ge(sem["dve_step"], steps.so_far())
            dve.scalar_tensor_tensor(m.keyf[:, :], m.segk[:, :], con[0:GK, C_ISMEAN:C_ISMEAN + 1], m.keyf[:, :],
                                          ALU.mult, ALU.add).then_inc(sem["dve_step"], steps.next())
            dve.wait_ge(sem["dve_step"], steps.so_far())
            dve.tensor_copy(m.keyi[:, :], m.keyf[:, :]).then_inc(sem["key_index"], 1)
            key = m.seen[:, :, 0:WIN - 1]
            dve.tensor_tensor(key, m.segr[:, :].unsqueeze(2).to_broadcast([P, NG, WIN - 1]),
                                   con[:, C_WSHIFT:C_WSHIFT + WIN - 1].unsqueeze(1).to_broadcast([P, NG, WIN - 1]), ALU.add)\
               .then_inc(sem["dve_step"], steps.next())
            dve.wait_ge(sem["dve_step"], steps.so_far())
            dve.tensor_scalar(m.hide[:, :, 0:WIN - 1], key, 0.0, NEG, ALU.is_lt, ALU.mult)\
               .then_inc(sem["dve_step"], steps.next())
            dve.wait_ge(sem["dve_step"], steps.so_far())
            dve.tensor_scalar(key, key, float(LK - 1), NEG, ALU.is_gt, ALU.mult)\
               .then_inc(sem["dve_step"], steps.next())
            dve.wait_ge(sem["dve_step"], steps.so_far())
            dve.tensor_tensor(m.hide[:, :, 0:WIN - 1], m.hide[:, :, 0:WIN - 1], key, ALU.add)\
               .then_inc(sem["dve_step"], steps.next())
            dve.wait_ge(sem["dve_step"], steps.so_far())
            dve.tensor_scalar(m.seen[:, :, 0], m.segr[:, :], 0.0, -NEG, ALU.is_lt, ALU.mult)\
               .then_inc(sem["dve_step"], steps.next())
            dve.wait_ge(sem["dve_step"], steps.so_far())
            dve.tensor_scalar(m.seen[:, :, 1], m.segr[:, :], float(LK - 1 + WIN - 2), -NEG, ALU.is_gt, ALU.mult)\
               .then_inc(sem["dve_step"], steps.next())
            dve.wait_ge(sem["dve_step"], steps.so_far())
            dve.tensor_tensor(m.seen[:, :, 0], m.seen[:, :, 0], m.seen[:, :, 1], ALU.add)\
               .then_inc(sem["dve_step"], steps.next())
            dve.wait_ge(sem["dve_step"], steps.so_far())
            dve.tensor_scalar(m.hide[:, :, WIN - 1], m.seen[:, :, 0], NEG, None, ALU.add)\
               .then_inc(sem["dve_step"], steps.next())
            dve.wait_ge(sem["dve_step"], steps.so_far())

            def soften(pr, rows, width, mask, banks, scale, a, full, taken, centered, exp, done):
                for jj in (0, 2):
                    for j in (jj, jj + 1):
                        v = pr[:, j, :].rearrange("p (g k) -> p g k", k=width)
                        dve.wait_ge(sem[full], 4 * a + j + 1)
                        dve.scalar_tensor_tensor(
                            v, banks[j][0:rows, 0:4 * width].rearrange("p (g k) -> p g k", k=width), scale,
                            mask.unsqueeze(1).to_broadcast([rows, 4, width]), ALU.mult, ALU.add).then_inc(sem[taken], 1)
                    for j in (jj, jj + 1):
                        v = pr[:, j, :].rearrange("p (g k) -> p g k", k=width)
                        dve.wait_ge(sem[taken], 4 * a + j + 1)
                        dve.tensor_reduce(m.peak[0:rows, j, :], v, AX.X, ALU.max)\
                           .then_inc(sem["dve_step"], steps.next())
                    dve.wait_ge(sem["dve_step"], steps.so_far())
                    for j in (jj, jj + 1):
                        v = pr[:, j, :].rearrange("p (g k) -> p g k", k=width)
                        dve.tensor_tensor(v, v, m.peak[0:rows, j, :].unsqueeze(2).to_broadcast([rows, 4, width]), ALU.subtract)\
                           .then_inc(sem[centered], 1)
                for jj in (0, 2):
                    for j in (jj, jj + 1):
                        v = pr[:, j, :].rearrange("p (g k) -> p g k", k=width)
                        dve.wait_ge(sem[exp], 4 * a + j + 1)
                        dve.tensor_reduce(m.total[0:rows, j, :], v, AX.X, ALU.add)\
                           .then_inc(sem["dve_step"], steps.next())
                    dve.wait_ge(sem["dve_step"], steps.so_far())
                    dve.reciprocal(m.share[0:rows, jj:jj + 2, :], m.total[0:rows, jj:jj + 2, :])\
                       .then_inc(sem["dve_step"], steps.next())
                    dve.wait_ge(sem["dve_step"], steps.so_far())
                    for j in (jj, jj + 1):
                        v = pr[:, j, :].rearrange("p (g k) -> p g k", k=width)
                        dve.tensor_tensor(v, v, m.share[0:rows, j, :].unsqueeze(2).to_broadcast([rows, 4, width]), ALU.mult)\
                           .then_inc(sem[done], 1)

            def self_dve(i, product, attn):
                a = i - 1
                if attn:
                    soften(m.probs, ST, ST, con[0:ST, C_SMASK:C_SMASK + ST], A, 64 ** -0.5, a,
                           "self_s", "s_taken", "s_centered", "s_exp", "s_probs")
                    for u in range(2):
                        dve.wait_ge(sem["self_vt"], 2 * a + u + 1)
                        dve.tensor_copy(m.v_tok[:, 4 * u:4 * u + 4, :],
                                        C[u][0:ST, :].rearrange("p (g f) -> p g f", f=P)).then_inc(sem["vt_evac"], 1)
                    for k, ((dst, src), (hi, _)) in enumerate(zip(ao_parts(m.aol, C, a), ao_parts(m.aoh, C, a))):
                        dve.wait_ge(sem["ao_hi"], 3 * a + (3 if k else 1))
                        dve.tensor_tensor(dst, src, hi.bitcast(F32), ALU.subtract).then_inc(sem["ao_lo"], 1)
                if product:
                    for e in range(2):
                        r = slice(64 * e, 64 * e + 64)
                        dve.wait_ge(sem["wa_hi"], 2 * i + 2)
                        dve.tensor_tensor(m.wal[r, i, RA * e:RA * e + RA], G[0][r, 0:RA], m.wah[r, i, RA * e:RA * e + RA].bitcast(F32), ALU.subtract)\
                           .then_inc(sem["wa_lo"], 1)

            self_dve(0, True, False)
            self_dve(1, True, True)
            with dve.Fori(2, HP) as i:
                steps.loop(i, 2, HP, 10)
                self_dve(i, True, True)
            steps.close()
            self_dve(HP, False, True)

            def out_dve(i):
                for u in range(2):
                    n = 2 * i + u + 1
                    y = half(m.y1[:, i, :], u)
                    dve.wait_ge(sem["out_done"], n)
                    dve.tensor_tensor(y, G[u][:, 0:HT], half(m.xh[:, i, :], u).bitcast(F32), ALU.add)\
                       .then_inc(sem["y1_read"], 1)
                    dve.wait_ge(sem["y1_read"], n)
                    dve.tensor_tensor(y, y, half(m.xl[:, i, :], u).bitcast(F32), ALU.add).then_inc(sem["y1_done"], 1)
                    dve.wait_ge(sem["y1_done"], n)
                    dve.tensor_tensor(half(m.sums[:, 0, :], u), half(m.sums[:, 0, :], u), y, ALU.add)\
                       .then_inc(sem["dve_step"], steps.next())
                    dve.wait_ge(sem["square_done"], n)
                    dve.tensor_tensor(half(m.sums[:, 1, :], u), half(m.sums[:, 1, :], u), m.square[:, u, :], ALU.add)\
                       .then_inc(sem["square_added"], 1)
                dve.wait_ge(sem["dve_step"], steps.so_far())
                dve.wait_ge(sem["square_added"], 2 * i + 2)

            with dve.Fori(0, HP) as i:
                steps.loop(i, 0, HP, 2)
                out_dve(i)
            steps.close()

            def rsqrt_of(r, n):
                dve.wait_ge(sem["stat_root"], n)
                dve.reciprocal(r, m.root[:, :]).then_inc(sem["dve_step"], steps.next())
                dve.wait_ge(sem["dve_step"], steps.so_far())
                dve.tensor_tensor(m.tmp[:, :], r, r, ALU.mult).then_inc(sem["dve_step"], steps.next())
                dve.wait_ge(sem["dve_step"], steps.so_far())
                dve.tensor_tensor(m.tmp[:, :], m.tmp[:, :], m.ve[:, :], ALU.mult)\
                   .then_inc(sem["dve_step"], steps.next())
                dve.wait_ge(sem["dve_step"], steps.so_far())
                dve.tensor_scalar(m.tmp[:, :], m.tmp[:, :], -0.5, 1.5, ALU.mult, ALU.add)\
                   .then_inc(sem["dve_step"], steps.next())
                dve.wait_ge(sem["dve_step"], steps.so_far())
                dve.tensor_tensor(r, r, m.tmp[:, :], ALU.mult).then_inc(sem["stat_rstd"], 1)
                dve.wait_ge(sem["stat_rstd"], n)

            def statistics(q, n, u, b0, b1):
                dve.wait_ge(sem["stat_sums"], q)
                dve.tensor_copy(m.mean[:, u, :], b0[:, 0:HT]).then_inc(sem["dve_step"], steps.next())
                dve.wait_ge(sem["dve_step"], steps.so_far())
                dve.tensor_tensor(m.tmp[:, :], m.mean[:, u, :], m.mean[:, u, :], ALU.mult)\
                   .then_inc(sem["dve_step"], steps.next())
                dve.wait_ge(sem["dve_step"], steps.so_far())
                dve.tensor_tensor(m.ve[:, :], b1[:, 0:HT], m.tmp[:, :], ALU.subtract).then_inc(sem["stat_taken"], 1)
                dve.wait_ge(sem["stat_taken"], q)
                dve.tensor_scalar(m.ve[:, :], m.ve[:, :], 0.0, EPS_LN, ALU.max, ALU.add).then_inc(sem["stat_var"], 1)
                dve.memset(half(m.sums[:, 0, :], u), 0.0).then_inc(sem["dve_step"], steps.next())
                dve.memset(half(m.sums[:, 1, :], u), 0.0).then_inc(sem["dve_step"], steps.next())
                dve.wait_ge(sem["dve_step"], steps.so_far())
                dve.wait_ge(sem["stat_var"], n)
                rsqrt_of(m.rstd[:, u, :], n)

            def second_norm(n, u):
                dve.tensor_scalar(m.ve[:, :], m.ve[:, :], -EPS_LN, None, ALU.add)\
                   .then_inc(sem["dve_step"], steps.next())
                dve.wait_ge(sem["dve_step"], steps.so_far())
                dve.tensor_tensor(m.ve[:, :], m.ve[:, :], m.rstd[:, u, :], ALU.mult)\
                   .then_inc(sem["dve_step"], steps.next())
                dve.wait_ge(sem["dve_step"], steps.so_far())
                dve.tensor_tensor(m.ve[:, :], m.ve[:, :], m.rstd[:, u, :], ALU.mult)\
                   .then_inc(sem["dve_step"], steps.next())
                dve.wait_ge(sem["dve_step"], steps.so_far())
                dve.tensor_scalar(m.ve[:, :], m.ve[:, :], EPS_RMS, None, ALU.add).then_inc(sem["stat_var"], 1)
                dve.wait_ge(sem["stat_var"], n)
                rsqrt_of(m.rms2[:, u, :], n)

            statistics(1, 1, 0, A[0], A[1])
            statistics(2, 2, 1, A[2], A[3])

            def norm(y, u, name):
                dve.tensor_tensor(y, y, m.mean[:, u, :], ALU.subtract).then_inc(sem["dve_step"], steps.next())
                dve.wait_ge(sem["dve_step"], steps.so_far())
                dve.tensor_tensor(y, y, m.rstd[:, u, :], ALU.mult).then_inc(sem[name], 1)

            def kv_dve(b):
                first = isinstance(b, int) and b == 0
                for u in range(2):
                    norm(half(m.y1[:, b, :], u), u, "ln1_z")
                for ti in range(KT):
                    n, s, bk = KT * b + ti, ti % 2, G[ti % 2]
                    kc, ks = C_KCOS + ti * RR, C_KSIN + ti * RR
                    dve.wait_ge(sem["kv_copied"], n + 1)
                    if not (first and ti < 2):
                        dve.wait_ge(sem["row_ready"], n - 1)
                    dve.tensor_tensor(m.rot[s][:, 0, :], bk[:, KVC:KVC + RR], con[:, kc:kc + RR], ALU.mult)\
                       .then_inc(sem["dve_step"], steps.next())
                    dve.tensor_tensor(m.rot[s][:, 1, 0:32], bk[:, KVC + 32:KVC + 64], con[:, ks:ks + 32], ALU.mult)\
                       .then_inc(sem["dve_step"], steps.next())
                    dve.tensor_tensor(m.rot[s][:, 1, 32:64], bk[:, KVC:KVC + 32], con[:, ks + 32:ks + 64], ALU.mult)\
                       .then_inc(sem["dve_step"], steps.next())
                    if ti == 0:
                        dve.tensor_copy(m.kv_sum[:, b, :], bk[:, 0:KVC]).then_inc(sem["kv_read"], 1)
                    else:
                        dve.wait_ge(sem["kv_read"], n)
                        dve.tensor_tensor(m.kv_sum[:, b, :], bk[:, 0:KVC], m.kv_sum[:, b, :], ALU.add)\
                           .then_inc(sem["kv_read"], 1)
                    dve.wait_ge(sem["dve_step"], steps.so_far())
                    if not (first and ti < 2):
                        dve.wait_ge(sem[f"row_stored_{s}"], 16 * (KT // 2 * b + ti // 2))
                    dve.tensor_tensor(m.row[s][:, KVC:ROW].rearrange("p (c r) -> p c r", r=RR), m.rot[s][:, 0, :].unsqueeze(1).to_broadcast([P, 2, RR]), m.rot[s][:, 1, :].unsqueeze(1).to_broadcast([P, 2, RR]), ALU.add)\
                       .then_inc(sem["row_ready"], 1)
                    if ti == 2:
                        for u in range(2):
                            dve.wait_ge(sem["ln1_hi"], 2 * b + u + 1)
                            dve.tensor_tensor(half(m.x1l[:, b, :], u), half(m.y1[:, b, :], u), half(m.x1h[:, b, :], u).bitcast(F32), ALU.subtract)\
                               .then_inc(sem["ln1_lo"], 1)

            kv_dve(0)
            with dve.Fori(1, NB) as b:
                steps.loop(b, 1, NB, 2 + 3 * KT)
                kv_dve(b)
            steps.close()
            dve.memset(m.mean_row[:, KVC:ROW], 0.0).then_inc(sem["mean_ready"], 1)

            for k in range(3):
                for u in range(2):
                    dve.wait_ge(sem["qc_hi"], 2 * k + u + 1)
                    dve.tensor_tensor(m.qcl[u][:, k, :], G[u][:, 0:HT], m.qch[u][:, k, :].bitcast(F32), ALU.subtract)\
                       .then_inc(sem["qc_lo"], 1)

            for hf in range(2):
                p_pair, p_win, p_out = HALF[hf]
                q = m.qn[p_pair]

                def pair_dve(hp):
                    n = HP * hf + hp
                    for u in range(2):
                        dve.wait_ge(sem["qn_hi"], 2 * n + u + 1)
                        if not (isinstance(hp, int) and hp == 0):
                            dve.wait_ge(sem["ukB_done"], 2 * n)
                        dve.tensor_tensor(q["l"][:, u, :], G[u][:, 0:HT], q["h"][:, u, :].bitcast(F32), ALU.subtract)\
                           .then_inc(sem["qn_lo"], 1)
                    dve.wait_ge(sem["qr_raw"], n + 1)

                    def turned(dst, src, at):
                        return dve.tensor_tensor(dst.rearrange("p (b s) -> p b s", s=NS),
                                                 src.rearrange("p (b s) -> p b s", s=NS),
                                                 con[:, at:at + NS].unsqueeze(1).to_broadcast([P, NB // 2, NS]), ALU.mult)

                    if hf == 1:
                        norm(m.y2[0][:, hp, :], 0, "x2_done")
                    turned(q["c"][:, :], q["r"][:, :], C_QCOS).then_inc(sem["dve_step"], steps.next())
                    for c in range(2):
                        dve.wait_ge(sem["ukB_done"], 2 * n + c + 1)
                        dve.tensor_copy(m.qa[:, c, :, 2 * hp + 1, :], grouped(C[c][:, 0:HT])).then_inc(sem["qa_dve"], 1)
                    dve.wait_ge(sem["perm_done"], n + 1)
                    turned(q["s"][:, :], A[1][:, 0:HT], C_QSIN).then_inc(sem["dve_step"], steps.next())
                    dve.wait_ge(sem["dve_step"], steps.so_far())
                    for e in range(2):
                        r = slice(64 * e, 64 * e + 64)
                        dve.tensor_tensor(m.qr[r, 0, :, 2 * hp + e, :], grouped(q["c"][r, :]), grouped(q["s"][r, :]), ALU.add)\
                           .then_inc(sem["q_rot"], 1)
                    dve.wait_ge(sem["q_rot"], 2 * n + 2)

                with dve.Fori(0, HP) as hp:
                    steps.loop(hp, 0, HP, 3 if hf else 2)
                    pair_dve(hp)
                steps.close()

                w = m.sp[p_win]
                scale = float(np.float32(1.0) / np.sqrt(np.float32(P + RR)))
                for v in range(1, UH + 4):
                    if v < UH + 1:
                        u, n = v - 1, UH * hf + v - 1
                        pr, st = w["pr"][u % 2], w["st"][u % 2]
                        dve.wait_ge(sem["win_s"], n + 1)
                        dve.wait_ge(sem["win_mask"], n + 1)
                        if positive(n - 1):
                            dve.wait_ge(sem["win_pt"], n - 1)
                        dve.scalar_tensor_tensor(pr[:, :, :], A[u % 2][:, 0:UG * GK].rearrange("p (g k) -> p g k", k=GK),
                                                 scale, w["mk"][u % 2][:, :, :], ALU.mult, ALU.add)\
                           .then_inc(sem["win_taken"], 1)
                        dve.wait_ge(sem["win_taken"], n + 1)
                        dve.tensor_reduce(st[:, 0, :], pr[:, :, :], AX.X, ALU.max)\
                           .then_inc(sem["dve_step"], steps.next())
                        dve.wait_ge(sem["dve_step"], steps.so_far())
                        dve.tensor_tensor(pr[:, :, :], pr[:, :, :], st[:, 0, :].unsqueeze(2).to_broadcast([P, UG, GK]), ALU.subtract)\
                           .then_inc(sem["win_centered"], 1)
                    if v >= 4:
                        u, n = v - 4, UH * hf + v - 4
                        for c, ((dst, src), (hi, _)) in enumerate(zip(lat_parts(m.latl, C, u), lat_parts(m.lath, C, u))):
                            dve.wait_ge(sem["lat_hi"], 2 * n + 2)
                            dve.tensor_tensor(dst, src, hi.bitcast(F32), ALU.subtract).then_inc(sem["lat_lo"], 1)
                    if v < UH + 1:
                        u, n = v - 1, UH * hf + v - 1
                        pr, st = w["pr"][u % 2], w["st"][u % 2]
                        dve.wait_ge(sem["win_exp"], n + 1)
                        dve.tensor_reduce(st[:, 1, :], pr[:, :, :], AX.X, ALU.add)\
                           .then_inc(sem["dve_step"], steps.next())
                        dve.wait_ge(sem["dve_step"], steps.so_far())
                        dve.reciprocal(st[:, 2, :], st[:, 1, :]).then_inc(sem["dve_step"], steps.next())
                        dve.wait_ge(sem["dve_step"], steps.so_far())
                        dve.tensor_tensor(pr[:, :, :], pr[:, :, :], st[:, 2, :].unsqueeze(2).to_broadcast([P, UG, GK]), ALU.mult)\
                           .then_inc(sem["win_probs"], 1)

                for h in range(H):
                    dve.wait_ge(sem["vo_hi"], H * hf + h + 1)
                    dve.tensor_tensor(m.latl[:, 0, :, h, :], grouped(G[h % 2][:, 0:HT]), m.lath[:, 0, :, h, :].bitcast(F32), ALU.subtract)\
                       .then_inc(sem["vo_lo"], 1)

                with dve.Fori(0, HP // 2) as i:
                    steps.loop(i, 0, HP // 2, 2)
                    for k in range(2):
                        n = HP * hf + 2 * i + k + 1
                        dve.wait_ge(sem["wo_done"], n)
                        dve.wait_ge(sem[f"x1_back_{k}"], 16 * (HP // 2 * hf + i + 1))
                        y = m.y2[hf][:, 2 * i + k, :]
                        dve.tensor_tensor(y, G[k][:, 0:HT], m.x1t[p_out][k][:, :], ALU.add).then_inc(sem["y2_done"], 1)
                        dve.wait_ge(sem["y2_done"], n)
                        dve.tensor_tensor(half(m.sums[:, 0, :], hf), half(m.sums[:, 0, :], hf), y, ALU.add)\
                           .then_inc(sem["dve_step"], steps.next())
                        dve.wait_ge(sem["dve_step"], steps.so_far())
                        dve.wait_ge(sem["square_done"], 2 * HP + n)
                        dve.tensor_tensor(half(m.sums[:, 1, :], hf), half(m.sums[:, 1, :], hf), m.square[:, k, :], ALU.add)\
                           .then_inc(sem["square_added"], 1)
                        dve.wait_ge(sem["square_added"], 2 * HP + n)
                steps.close()
                statistics(3 + hf, 3 + 2 * hf, hf, A[0], A[1])
                second_norm(4 + 2 * hf, hf)

            dve.wait_ge(sem["x2_done"], KC)
            for n in range(2 * KC + 1):
                if n < 2 * KC:
                    u, kc = n // KC, n % KC
                    y = m.y2[u][:, kc, :]
                    if u:
                        norm(y, 1, "x2_done")
                        dve.wait_ge(sem["x2_done"], KC + kc + 1)
                    if positive(n - 1):
                        dve.wait_ge(sem["in_hi"], n - 1)
                    if positive(n - 1):
                        dve.wait_ge(sem["in_lo"], n - 1)
                    dve.scalar_tensor_tensor(m.xa32[n % 2][:, :], y, con[:, C_LN1 + kc:C_LN1 + kc + 1],
                                             m.rms2[:, u, :], ALU.mult, ALU.mult).then_inc(sem["in_ready"], 1)
                if n:
                    u, kc = (n - 1) // KC, (n - 1) % KC
                    dve.wait_ge(sem["in_hi"], n)
                    dve.tensor_tensor(half(m.xal[:, kc, :], u), m.xa32[(n - 1) % 2][:, :], half(m.xah[:, kc, :], u).bitcast(F32), ALU.subtract)\
                       .then_inc(sem["in_lo"], 1)
            dve.wait_ge(sem["g_hi"], 1)
            dve.tensor_tensor(m.gl[:, :, :], m.g_new[:, :, :], m.gh[:, :, :].bitcast(F32), ALU.subtract)\
               .then_inc(sem["g_lo"], 1)

            def ffn_dve(i):
                soften(m.fprobs, NS, NS, con[0:NS, C_FMASK:C_FMASK + NS], A, 64 ** -0.5, i - 1,
                       "f_s", "f_taken", "f_centered", "f_exp", "f_probs")

            for b in range(NB):
                dve.wait_ge(sem["z_done"], b + 1)
                dve.tensor_copy(m.z_tok[:, b, :], G[b % 2][0:NS, 0:H * RA]).then_inc(sem["z_evac"], 1)
            ffn_dve(1)
            with dve.Fori(2, HP + 1) as i:
                steps.loop(i, 2, HP + 1, 10)
                ffn_dve(i)
            steps.close()

            dve.memset(m.b_raw[:, :], 0.0).then_inc(sem["dve_step"], steps.next())
            dve.wait_ge(sem["dve_step"], steps.so_far())
            dve.memset(m.tmp[:, 0:1], 0.0).then_inc(sem["b_zero"], 1)
            dve.memset(m.ustk[:, :].bitcast(F32), 0.0).then_inc(sem["dve_step"], steps.next())
            for n in range(2 * KC + 1):
                if n < 2 * KC:
                    u, kc = n // KC, n % KC
                    y = m.y2[u][:, kc, :]
                    dve.wait_ge(sem["in_hi"], 2 * KC + n - 1)
                    dve.wait_ge(sem["in_lo"], 2 * KC + n - 1)
                    dve.scalar_tensor_tensor(m.xa32[n % 2][:, :], y, con[:, C_LN2 + kc:C_LN2 + kc + 1],
                                             m.rms2[:, u, :], ALU.mult, ALU.mult).then_inc(sem["in_ready"], 1)
                if n:
                    u, kc = (n - 1) // KC, (n - 1) % KC
                    dve.wait_ge(sem["in_hi"], 2 * KC + n)
                    dve.tensor_tensor(half(m.hl[:, kc, :], u), m.xa32[(n - 1) % 2][:, :], half(m.hh[:, kc, :], u).bitcast(F32), ALU.subtract)\
                       .then_inc(sem["in_lo"], 1)
            dve.wait_ge(sem["dve_step"], steps.so_far())
            dve.memset(m.tmp[:, 1:2], 0.0).then_inc(sem["u_zero"], 1)
            dve.wait_ge(sem["in_ready"], 4 * KC)
            for u in range(2):
                dve.wait_ge(sem["m_tanh"], u + 1)
                dve.wait_ge(sem["ha_done"], u + 1)
                dve.scalar_tensor_tensor(half(m.u_raw[:, :], u), half(m.tanh_m[:, :], u), 0.1, G[u][0:RA, 0:HT],
                                         ALU.mult, ALU.mult).then_inc(sem["u_ready"], 1)
            for u in range(2):
                dve.wait_ge(sem["u_hi"], 2 * u + 2)
                dve.tensor_tensor(half(m.ustk[32:32 + RA, :], u), half(m.u_raw[:, :], u), half(m.ustk[0:RA, :], u).bitcast(F32), ALU.subtract)\
                   .then_inc(sem["u_lo"], 1)
            for u in range(2):
                dve.tensor_scalar(m.y2[u][:, :, :], m.y2[u][:, :, :], 2.0, None, ALU.mult).then_inc(sem["y_twice"], 1)
            dve.wait_ge(sem["y_twice"], 2)

            def up_dve(fb, fm):
                f = FM * fb + fm
                dve.wait_ge(sem["b_hi"], f + 1)
                dve.tensor_tensor(m.bstk[64:64 + RA, :], m.b_raw[64:64 + RA, bass.ds(f * P, P)] if not isinstance(f, int)
                    else m.b_raw[64:64 + RA, f * P:(f + 1) * P], m.bstk[64:64 + RA, :].bitcast(F32), ALU.subtract)\
                   .then_inc(sem["b_lo"], 1)
                for u in range(2):
                    dve.wait_ge(sem["silu_done"], 2 * f + u + 1)
                    dve.wait_ge(sem["ff_up"], 2 * f + u + 1)
                    dve.tensor_tensor(m.act32[u][:, :], m.gate[u][:, :], A[u][:, 0:HT], ALU.mult)\
                       .then_inc(sem["ff_prod"], 1)
                for u in range(2):
                    dve.wait_ge(sem["ff_hi"], 2 * f + u + 1)
                    dve.tensor_tensor(half(m.ffl[:, fm, :], u), m.act32[u][:, :], half(m.ffh[:, fm, :], u).bitcast(F32), ALU.subtract)\
                       .then_inc(sem["ff_lo"], 1)
                dve.wait_ge(sem["ff_lo"], 2 * f + 2)

            def down_dve(fb, c, last):
                n = FM * fb + c
                for u in range(2):
                    y = m.y2[u][:, c, :]
                    dve.wait_ge(sem["down_done"], 2 * n + u + 1)
                    dve.tensor_tensor(y, C[u][:, 0:HT], y, ALU.add).then_inc(sem["down_added"], 1)
                    if last:
                        dve.wait_ge(sem["down_added"], 2 * n + u + 1)
                        dve.tensor_tensor(half(m.sums[:, 0, :], u), half(m.sums[:, 0, :], u), y, ALU.add)\
                           .then_inc(sem["dve_step"], steps.next())
                        dve.wait_ge(sem["dve_step"], steps.so_far())
                        dve.wait_ge(sem["square_done"], 4 * HP + 2 * c + u + 1)
                        dve.tensor_tensor(half(m.sums[:, 1, :], u), half(m.sums[:, 1, :], u), m.square[:, u, :], ALU.add)\
                           .then_inc(sem["square_added"], 1)
                        dve.wait_ge(sem["square_added"], 4 * HP + 2 * c + u + 1)
                dve.wait_ge(sem["down_added"], 2 * n + 2)

            with dve.Fori(0, FB - 1) as fb:
                with dve.Fori(0, FM) as fm:
                    up_dve(fb, fm)
                with dve.Fori(0, KC) as c:
                    down_dve(fb, c, False)
            with dve.Fori(0, FM) as fm:
                up_dve(FB - 1, fm)
            with dve.Fori(0, KC) as c:
                steps.loop(c, 0, KC, 2)
                down_dve(FB - 1, c, True)
            steps.close()
            statistics(5, 7, 0, A[0], A[1])
            statistics(6, 8, 1, A[2], A[3])
            for kc in range(KC):
                for u in range(2):
                    norm(m.y2[u][:, kc, :], u, "final_done")

        @block.tensor
        def _(pe):
            def three(dst, w, xh, xl, first, last):
                pe.matmul(dst, w[0], xh, start=first, stop=False)
                pe.matmul(dst, w[0], xl, start=False, stop=False)
                return pe.matmul(dst, w[1], xh, start=False, stop=last)

            def tile(k, j):
                return whi[k % 2][:, j, :], wlo[k % 2][:, j, :]

            def stripe(k, i=0, per=0):
                pe.wait_ge(sem["w_lo"], k + per * i + 1)

            def chunks(dst, k, xh, xl, u):
                for kc in range(KC):
                    ins = three(dst, tile(k, kc), half(xh[:, kc, :], u), half(xl[:, kc, :], u), kc == 0, kc == KC - 1)
                return ins

            x_h, x_l = m.xh, m.xl
            q_s, k_s, v_s = m.qkv

            def self_product(j, i, done, evac, n_evac):
                stripe(S_SELF + j, i, 4)
                for u in range(2):
                    if evac:
                        if positive(n_evac[u]):
                            pe.wait_ge(sem[evac[u]], n_evac[u])
                    for kc in range(KC):
                        if isinstance(i, int) and i == 0 and j == 0:
                            pe.wait_ge(sem["set_lo"], kc + 1)
                        ins = three(G[u][:, 0:HT], tile(j, kc), half(x_h[:, kc, :], u), half(x_l[:, kc, :], u),
                                    kc == 0, kc == KC - 1)
                    ins.then_inc(sem[done], 1)

            def self_pe(i, product, attn):
                a = i - 1
                if attn:
                    pe.wait_ge(sem["q_evac"], 2 * a + 2)
                    pe.wait_ge(sem["k_evac"], 2 * a + 2)
                    for j in range(4):
                        e, gh = j // 2, j % 2
                        if not (isinstance(a, int) and a == 0):
                            pe.wait_ge(sem["pt_evac"], 4 * a - 3 + j)
                        for g4 in range(4):
                            n0 = self_group(4 * gh + g4)
                            rows = slice(64 * e, 64 * e + 64)
                            ins = pe.matmul(A[j][0:ST, g4 * ST:(g4 + 1) * ST], q_s[rows, n0:n0 + SN, :].rearrange("p n b -> p (n b)"),
                                            k_s[rows, n0:n0 + SN, :].rearrange("p n b -> p (n b)"), start=True, stop=True)
                        ins.then_inc(sem["self_s"], 1)
                if product:
                    self_product(0, i, "self_q", ("wa_lo", "v_evac"), (2 * i, 2 * i))
                if attn:
                    pe.wait_ge(sem["v_evac"], 2 * a + 2)
                    for u in range(2):
                        if not (isinstance(a, int) and a == 0):
                            pe.wait_ge(sem["ao_lo"], 3 * a)
                        else:
                            pe.wait_ge(sem["set_lo"], KC + 3)
                        for g4 in range(4):
                            n0 = self_group(4 * u + g4)
                            ins = pe.transpose(C[u][0:ST, g4 * P:(g4 + 1) * P], v_s[:, n0:n0 + SN, :].rearrange("p n b -> p (n b)"), ident)
                        ins.then_inc(sem["self_vt"], 1)
                if product:
                    self_product(1, i, "self_k", ("q_evac", "q_evac"), (2 * i + 1, 2 * i + 2))
                if attn:
                    for j in range(4):
                        pe.wait_ge(sem["s_probs"], 4 * a + j + 1)
                        for g4 in range(4):
                            ins = pe.transpose(A[j][0:ST, g4 * ST:(g4 + 1) * ST],
                                               m.probs[:, j, g4 * ST:(g4 + 1) * ST], con[0:ST, C_IDENT:C_IDENT + ST])
                        ins.then_inc(sem["self_pt"], 1)
                if product:
                    self_product(2, i, "self_v", ("k_evac", "k_evac"), (2 * i + 1, 2 * i + 2))
                if attn:
                    pe.wait_ge(sem["vt_evac"], 2 * a + 2)
                    for gh in range(2):
                        for e in range(2):
                            j = 2 * e + gh
                            pe.wait_ge(sem["pt_evac"], 4 * a + j + 1)
                            for g4 in range(4):
                                ins = pe.matmul(C[gh][64 * e:64 * e + 64, g4 * ST:(g4 + 1) * ST],
                                                m.v_tok[:, 4 * gh + g4, 64 * e:64 * e + 64],
                                                m.probs_t[:, j, g4 * ST:(g4 + 1) * ST], start=True, stop=True)
                    ins.then_inc(sem["self_pv"], 1)
                if product:
                    stripe(S_SELF + 3, i, 4)
                    pe.wait_ge(sem["set_lo"], KC + 1)
                    pe.wait_ge(sem["v_evac"], 2 * i + 1)
                    for kc in range(KC):
                        ins = three(G[0][:, 0:RA], tile(3, kc), m.ah[:, kc, :], m.al[:, kc, :], kc == 0, kc == KC - 1)
                    ins.then_inc(sem["self_wo"], 1)

            pe.wait_ge(sem["con_loaded"], 16)
            self_pe(0, True, False)
            pe.wait_ge(sem["aux_loaded"], 64)
            for kc in range(KC):
                for c in range(2):
                    ins = pe.matmul(C[0][:, kc * RR:(kc + 1) * RR], m.kvc_t[:, c, kc * P:(kc + 1) * P],
                                    m.kr_raw[:, c, :], start=(c == 0), stop=(c == 1))
            ins.then_inc(sem["fold_done"], 1)
            self_pe(1, True, True)
            with pe.Fori(2, HP) as i:
                self_pe(i, True, True)
            self_pe(HP, False, True)

            pe.wait_ge(sem["ao_lo"], 3 * HP)
            pe.wait_ge(sem["wa_lo"], 2 * HP)
            aoh, aol = m.aoh.rearrange("p k b s -> p k (b s)"), m.aol.rearrange("p k b s -> p k (b s)")

            def out_pe(i):
                first = isinstance(i, int) and i == 0
                stripe(S_OUT, i, 2)
                for u in range(2):
                    if not first:
                        pe.wait_ge(sem[("g_evac", "y1_read")[u]], (i, 2 * i)[u])
                    chunks(G[u][:, 0:HT], S_OUT, aoh, aol, u).then_inc(sem["out_done"], 1)
                stripe(S_OUT + 1, i, 2)
                pe.wait_ge(sem["y1_read"], 2 * i + 1)
                for ec in range(KC):
                    ins = three(G[0][:, ec * 2 * RA:(ec + 1) * 2 * RA], tile(S_OUT + 1, ec), m.wah[:, i, :], m.wal[:, i, :],
                                True, True)
                ins.then_inc(sem["wv_done"], 1)

            out_pe(0)
            with pe.Fori(1, HP) as i:
                out_pe(i)

            def sum_up(u, b0, b1):
                pe.matmul(b0[:, 0:HT], ones, half(m.sums[:, 0, :], u), start=True, stop=True)
                pe.matmul(b1[:, 0:HT], ones, half(m.sums[:, 1, :], u), start=True, stop=True)\
                  .then_inc(sem["stat_sums"], 1)

            pe.wait_ge(sem["pt_evac"], 4 * HP)
            pe.wait_ge(sem["square_added"], 2 * HP)
            sum_up(0, A[0], A[1])
            pe.wait_ge(sem["square_added"], 2 * HP)
            sum_up(1, A[2], A[3])

            pe.wait_ge(sem["set_lo"], KC + 3)

            def kv_pe(b):
                for ti in range(KT):
                    k, n = S_KV + ti, KT * b + ti
                    stripe(k, b, KT)
                    if isinstance(b, int) and b == 0 and ti < 2:
                        pe.wait_ge(sem[("g_evac", "y1_read")[ti]], (HP, 2 * HP)[ti])
                    else:
                        pe.wait_ge(sem["kv_copied"], n - 1)
                        pe.wait_ge(sem["kv_read"], n - 1)
                    for kc in range(KC):
                        ins = three(G[ti % 2][:, 0:KVC + RR], tile(k, kc), m.kvh[:, kc, :], m.kvl[:, kc, :],
                                    kc == 0, kc == KC - 1)
                    ins.then_inc(sem["kv_done"], 1)

            kv_pe(0)
            with pe.Fori(1, NB) as b:
                kv_pe(b)
            pe.wait_ge(sem["kv_copied"], N_KV)
            pe.wait_ge(sem["kv_read"], N_KV)
            for b in range(NB):
                ins = pe.matmul(G[0][0:NB, 0:KVC], con[:, C_BATCH + NB * b:C_BATCH + NB * (b + 1)], m.kv_sum[:, b, :],
                                start=(b == 0), stop=(b == NB - 1))
            ins.then_inc(sem["mean_done"], 1)

            for k in range(3):
                stripe(S_DQ + k)
                for u in range(2):
                    n = 2 * k + u
                    if k == 0:
                        pe.wait_ge(sem["ln1_lo"], 2 * KC)
                        pe.wait_ge(sem["mean_ready"], 2 - u)
                    if positive(n - 1):
                        pe.wait_ge(sem["qc_lo"], n - 1)
                    chunks(G[u][:, 0:HT], S_DQ + k, m.x1h, m.x1l, u).then_inc(sem["dq_done"], 1)
            pe.wait_ge(sem["qc_lo"], 6)

            for hf in range(2):
                p_pair, p_win, p_out = HALF[hf]
                s0 = S_HALF + hf * N_HALF
                q = m.qn[p_pair]
                if hf:
                    pe.wait_ge(sem["lat_lo"], 2 * UH)
                    pe.wait_ge(sem["y2_done"], HP)
                    pe.wait_ge(sem["stat_taken"], 3)

                def pair_pe(hp):
                    n = HP * hf + hp
                    later = not (isinstance(n, int) and n == 0)
                    stripe(s0, hp, 2)
                    for u in range(2):
                        if later:
                            pe.wait_ge(sem["qn_lo"], 2 * n)
                        for c in range(3):
                            ins = three(G[u][:, 0:HT], tile(s0, 3 * u + c), m.qch[hf][:, c, :], m.qcl[hf][:, c, :],
                                        c == 0, c == 2)
                        ins.then_inc(sem["uq_done"], 1)
                    if later:
                        pe.wait_ge(sem["qr_raw"], n)
                    for c in range(2):
                        ins = three(A[0][:, 0:HT], tile(s0, 6 + c), m.qch[hf][:, c, :], m.qcl[hf][:, c, :], c == 0, False)
                    ins.then_inc(sem["qr_half"], 1)
                    stripe(s0 + 1, hp, 2)
                    three(A[0][:, 0:HT], tile(s0 + 1, 0), m.qch[hf][:, 2, :], m.qcl[hf][:, 2, :], False, True)\
                        .then_inc(sem["qr_done"], 1)
                    for e, banks, done, evac in ((0, A[2:4], "ukA_done", "qa_act"), (1, C, "ukB_done", "qa_dve")):
                        pe.wait_ge(sem["qn_lo"], 2 * n + e + 1)
                        if later:
                            pe.wait_ge(sem[evac], 2 * n)
                        for c in range(2):
                            three(banks[c][:, 0:HT], tile(s0 + 1, 1 + 2 * e + c), q["h"][:, e, :], q["l"][:, e, :],
                                  True, True).then_inc(sem[done], 1)
                    pe.wait_ge(sem["qr_raw"], n + 1)
                    if later:
                        pe.wait_ge(sem["q_rot"], 2 * n)
                    pe.matmul(A[1][:, 0:HT], con[:, C_PERM:C_PERM + P], q["r"][:, :], start=True, stop=True)\
                      .then_inc(sem["perm_done"], 1)

                pair_pe(0)
                with pe.Fori(1, HP) as hp:
                    pair_pe(hp)

                n = HP * (hf + 1)
                for name, count in (("qa_act", 2 * n), ("qa_dve", 2 * n), ("q_rot", 2 * n), ("qr_zero", 2 * hf + 2), ("qn_lo", 2 * n)):
                    pe.wait_ge(sem[name], count)
                w = m.sp[p_win]
                for v in range(UH + 3):
                    if v < UH:
                        u, n = v, UH * hf + v
                        if positive(n - 1):
                            pe.wait_ge(sem["wt_evac"], n - 1)
                        for gi in range(UG):
                            r = (UG * u + gi) % RING
                            pe.wait_ge(sem[f"gathered_{r}"], 16 * (NG // 2 // RING * hf + (UG * u + gi) // RING + 1))
                            for c in range(3):
                                at = (3 * gi + c) * GK
                                ins = pe.transpose(G[u % 2][:, at:at + GK], w["win"][r][:, c * P:(c + 1) * P],
                                                   con[0:GK, C_IDENT:C_IDENT + GK])
                        ins.then_inc(sem["wt_done"], 1)
                    if 1 <= v < UH + 1:
                        u, n = v - 1, UH * hf + v - 1
                        pe.wait_ge(sem["wt_evac"], n + 1)
                        if positive(n - 1):
                            pe.wait_ge(sem["win_taken"], n - 1)
                        for gi in range(UG):
                            for c, src in enumerate((m.qa[:, 0], m.qa[:, 1], m.qr[:, 0])):
                                src = src[:, UG * u + gi, :, :].rearrange("p h q -> p (h q)")
                                ins = pe.matmul(A[u % 2][:, gi * GK:(gi + 1) * GK], src, w["wt"][u % 2][:, 3 * gi + c, :],
                                                start=(c == 0), stop=(c == 2))
                        ins.then_inc(sem["win_s"], 1)
                    if 2 <= v < UH + 2:
                        u, n = v - 2, UH * hf + v - 2
                        pe.wait_ge(sem["win_probs"], n + 1)
                        if positive(n - 1):
                            pe.wait_ge(sem["win_pt_evac"], n - 1)
                        for gi in range(UG):
                            ins = pe.transpose(A[2 + u % 2][0:GK, gi * P:(gi + 1) * P], w["pr"][u % 2][:, gi, :], ident)
                        ins.then_inc(sem["win_pt"], 1)
                    if v >= 3:
                        u, n = v - 3, UH * hf + v - 3
                        pe.wait_ge(sem["win_pt_evac"], n + 1)
                        if positive(2 * (n - 1)):
                            pe.wait_ge(sem["lat_lo"], 2 * (n - 1))
                        for gi in range(UG):
                            for c in range(2):
                                at = (2 * gi + c) * P
                                ins = pe.matmul(C[u % 2][:, at:at + P],
                                                w["win"][(UG * u + gi) % RING][:, c * P:(c + 1) * P],
                                                w["pt"][u % 2][:, gi, :], start=True, stop=True)
                        ins.then_inc(sem["win_lat"], 1)

                pe.wait_ge(sem["lat_lo"], 2 * UH * (hf + 1))
                pe.wait_ge(sem["wt_evac"], UH * (hf + 1))
                for i in range(N_UV):
                    k = s0 + N_PAIR + i
                    stripe(k)
                    for h in range(4 * i, 4 * i + 4):
                        if h >= 2:
                            pe.wait_ge(sem["vo_lo"], H * hf + h - 1)
                        for c in range(2):
                            ins = three(G[h % 2][:, 0:HT], tile(k, 2 * (h % 4) + c), m.lath[:, c, :, h, :], m.latl[:, c, :, h, :],
                                        c == 0, c == 1)
                        ins.then_inc(sem["uv_done"], 1)

                def wo_pe(i):
                    first = isinstance(i, int) and i == 0
                    for k in range(2):
                        n = HP * hf + 2 * i + k
                        if first and k == 0:
                            pe.wait_ge(sem["vo_lo"], H * (hf + 1))
                        if not first:
                            pe.wait_ge(sem["y2_done"], n - 1)
                        for kk in range(2):
                            s = s0 + N_PAIR + N_UV + 2 * k + kk
                            stripe(s, i, 4)
                            for c in range(KC):
                                h = KC * kk + c
                                ins = three(G[k][:, 0:HT], tile(s, c), m.lath[:, 0, :, h, :], m.latl[:, 0, :, h, :],
                                            h == 0, h == H - 1)
                            ins.then_inc(sem[("wo_half", "wo_done")[kk]], 1)

                wo_pe(0)
                with pe.Fori(1, HP // 2) as i:
                    wo_pe(i)
                pe.wait_ge(sem["square_added"], 2 * HP + HP * (hf + 1))
                sum_up(hf, A[0], A[1])

            pe.wait_ge(sem["y2_done"], 2 * HP)

            def ffn_product(j, i, u):
                if u == 0:
                    stripe(S_QK + j, i, 2)
                first = isinstance(i, int) and i == 0
                if not (first and j == 0):
                    pe.wait_ge(sem[("fk_evac", "fq_evac")[j]], 2 * i + u + (1 if j else -1))
                for kc in range(KC):
                    if first and j == 0:
                        pe.wait_ge(sem["in_lo"], KC * u + kc + 1)
                    ins = three(G[u][:, 0:HT], tile(S_QK + j, kc), half(m.xah[:, kc, :], u), half(m.xal[:, kc, :], u),
                                kc == 0, kc == KC - 1)
                ins.then_inc(sem[("fq_done", "fk_done")[j]], 1)

            def values(a):
                for j in range(4):
                    e, gh = j // 2, j % 2
                    pe.wait_ge(sem["f_pt_evac"], 4 * a + j + 1)
                    for g4 in range(4):
                        g = 4 * gh + g4
                        at = bass.ds((2 * a + e) * RA, RA) if not isinstance(a, int) \
                            else slice((2 * a + e) * RA, (2 * a + e + 1) * RA)
                        ins = pe.matmul(C[0][0:NS, g * RA:(g + 1) * RA], m.fprobs_t[:, j, g4 * NS:(g4 + 1) * NS],
                                        m.z_tok[:, g, at], start=False, stop=False, skip_group_check=True)
                ins.then_inc(sem["f_pv"], 1)

            def ffn_pe(i, product, attn, average):
                a = i - 1
                if attn:
                    pe.wait_ge(sem["fq_evac"], 2 * a + 2)
                    pe.wait_ge(sem["fk_evac"], 2 * a + 2)
                    for j in range(4):
                        e, gh = j // 2, j % 2
                        rows = slice(64 * e, 64 * e + 64)
                        if isinstance(a, int) and a == 0:
                            pe.wait_ge(sem["stat_taken"], 4)
                        else:
                            pe.wait_ge(sem["f_pt_evac"], 4 * a - 3 + j)
                        for g4 in range(4):
                            t0 = NS * (4 * gh + g4)
                            ins = pe.matmul(A[j][0:NS, g4 * NS:(g4 + 1) * NS], m.qk[0][rows, t0:t0 + NS],
                                            m.qk[1][rows, t0:t0 + NS], start=True, stop=True)
                        ins.then_inc(sem["f_s"], 1)
                if product:
                    ffn_product(0, i, 0)
                    ffn_product(0, i, 1)
                if average:
                    values(i - 2)
                if product:
                    ffn_product(1, i, 0)
                if attn:
                    for j in range(4):
                        pe.wait_ge(sem["f_probs"], 4 * a + j + 1)
                        for g4 in range(4):
                            ins = pe.transpose(A[j][0:NS, g4 * NS:(g4 + 1) * NS], m.fprobs[:, j, g4 * NS:(g4 + 1) * NS],
                                               con[0:NS, C_IDENT:C_IDENT + NS])
                        ins.then_inc(sem["f_pt"], 1)
                if product:
                    ffn_product(1, i, 1)

            ffn_pe(0, True, False, False)
            pe.wait_ge(sem["g_lo"], 1)
            for b in range(NB):
                if b < 2:
                    pe.wait_ge(sem["fk_evac"], b + 1)
                else:
                    pe.wait_ge(sem["z_evac"], b - 1)
                for kc in range(KC):
                    t = slice(b * NS, (b + 1) * NS)
                    ins = three(G[b % 2][0:NS, 0:H * RA], (m.xah[:, kc, t], m.xal[:, kc, t]), m.gh[:, kc, :], m.gl[:, kc, :],
                                kc == 0, kc == KC - 1)
                ins.then_inc(sem["z_done"], 1)
            zero = con[:, C_ZERO:C_ZERO + P]
            pe.wait_ge(sem["lat_lo"], 4 * UH)
            pe.matmul(C[0][0:NS, 0:NB * RA], zero[:, 0:NS], zero, start=True, stop=True)
            pe.wait_ge(sem["z_evac"], NB)
            ffn_pe(1, True, True, False)
            with pe.Fori(2, HP) as i:
                ffn_pe(i, True, True, True)
            ffn_pe(HP, False, True, True)
            values(HP - 1)

            pe.wait_ge(sem["fk_evac"], 2 * HP)
            for u in range(2):
                for kc in range(KC):
                    pe.wait_ge(sem["in_lo"], 2 * KC + KC * u + kc + 1)
                    ins = three(G[u][0:RA, 0:HT], (m.ah[:, kc, :], m.al[:, kc, :]), half(m.hh[:, kc, :], u),
                                half(m.hl[:, kc, :], u), kc == 0, kc == KC - 1)
                ins.then_inc(sem["ha_done"], 1)
                if u == 0:
                    pe.wait_ge(sem["m_evac"], 1)
                    pe.wait_ge(sem["f_pt_evac"], 4 * HP)
                    for g in range(NB):
                        ins = pe.transpose(A[g // 4][0:RA, (g % 4) * NS:(g % 4 + 1) * NS], m.m_tok[:, g, :],
                                           con[0:NS, C_IDENT:C_IDENT + NS])
                        if g % 4 == 3:
                            ins.then_inc(sem["mt_done"], 1)

            def up_pe(fb, fm):
                f = FM * fb + fm
                first = isinstance(f, int) and f == 0
                k = S_MLP
                pe.wait_ge(sem["w_lo"], k + 24 * fb + 2 * fm + 1)
                for u in range(2):
                    if first:
                        pe.wait_ge(sem["u_ready"], 2)
                    else:
                        pe.wait_ge(sem["silu_done"], 2 * f - 1 + u)
                    for kc in range(KC):
                        three(G[u][:, 0:HT], tile(k, kc), half(m.hh[:, kc, :], u), half(m.hl[:, kc, :], u), kc == 0, False)
                    if first:
                        pe.wait_ge(sem["u_lo"], 2)
                    pe.wait_ge(sem["b_lo"], f + 1)
                    pe.matmul(G[u][:, 0:HT], m.bstk[:, :], half(m.ustk[:, :], u), start=False, stop=True)\
                      .then_inc(sem["ff_gate"], 1)
                pe.wait_ge(sem["w_lo"], k + 24 * fb + 2 * fm + 2)
                for u in range(2):
                    if first:
                        pe.wait_ge(sem["m_tanh"], 2)
                    else:
                        pe.wait_ge(sem["ff_prod"], 2 * f - 1 + u)
                    chunks(A[u][:, 0:HT], k + 1, m.hh, m.hl, u).then_inc(sem["ff_up"], 1)

            def down_pe(fb, i, c, static_first):
                n = FM * fb + 2 * i + c
                k = S_MLP + 2 * FM + c
                pe.wait_ge(sem["w_lo"], k + 24 * fb + 2 * i + 1)
                for u in range(2):
                    if isinstance(n, int) and n == 0:
                        pe.wait_ge(sem["m_evac"], 1)
                    else:
                        pe.wait_ge(sem["down_added"], 2 * n - 1 + u)
                    for kc in range(KC):
                        if static_first:
                            pe.wait_ge(sem["ff_lo"], 2 * (FM * fb + kc) + u + 1)
                        ins = three(C[u][:, 0:HT], tile(k, kc), half(m.ffh[:, kc, :], u), half(m.ffl[:, kc, :], u),
                                    kc == 0, kc == KC - 1)
                    ins.then_inc(sem["down_done"], 1)

            def block_pe(fb):
                up_pe(fb, 0)
                with pe.Fori(1, FM) as fm:
                    up_pe(fb, fm)
                down_pe(fb, 0, 0, True)
                down_pe(fb, 0, 1, False)
                with pe.Fori(1, KC // 2) as i:
                    for c in range(2):
                        down_pe(fb, i, c, False)

            block_pe(0)
            with pe.Fori(1, FB) as fb:
                block_pe(fb)
            pe.wait_ge(sem["square_added"], 4 * HP + 2 * KC)
            sum_up(0, A[0], A[1])
            pe.wait_ge(sem["square_added"], 4 * HP + 2 * KC)
            sum_up(1, A[2], A[3])


def tiles(w):
    k, n = w.shape
    return w.reshape(k // P, P, n // P, P).transpose(0, 2, 1, 3)


def stripe_of(ts):
    out = np.zeros((P, KC, P), np.float32)
    for i, t in enumerate(ts):
        out[:, i] = t
    return out


def constants(ln1, ln2):
    c = np.zeros((P, N_CONST), np.float32)
    c[:, C_IDENT:C_IDENT + P] = np.eye(P)
    c[:, C_ONES:C_ONES + P] = 1.0 / D
    r = np.arange(P)
    c[r, C_PERM + (r ^ 32)] = 1.0
    nq, lq = np.divmod(np.arange(ST), NB)
    ok = (nq[:, None] == nq[None]) & (lq[None] <= lq[:, None])
    c[:ST, C_SMASK:C_SMASK + ST] = np.where(ok, 0, NEG)
    t = np.arange(NS)
    c[:NS, C_FMASK:C_FMASK + NS] = np.where(t[None] <= t[:, None], 0, NEG)
    c[:, C_BMASK:C_BMASK + GK] = np.where((r % GQ)[:, None] == (np.arange(GK) // WIN)[None], 0, NEG)
    half_r = RR // 2
    freq = np.float32(1.0) / np.float32(10000.0) ** (np.arange(half_r, dtype=np.float32) / np.float32(half_r))
    ang = np.arange(KPAD, dtype=np.float32)[:, None] * freq
    cos, sin = np.cos(ang), np.sin(ang)
    f = r % half_r
    c[:, C_QCOS:C_QCOS + NS] = cos[:NS, f].T
    c[:, C_QSIN:C_QSIN + NS] = sin[:NS, f].T * np.where(r % RR < half_r, -1, 1)[:, None]
    c[:, C_KCOS:C_KCOS + KT * RR] = np.concatenate([cos, cos], 1).reshape(KT, P, RR).transpose(1, 0, 2).reshape(P, -1)
    c[:, C_KSIN:C_KSIN + KT * RR] = np.concatenate([-sin, sin], 1).reshape(KT, P, RR).transpose(1, 0, 2).reshape(P, -1)
    j = np.arange(GK) % WIN
    c[:GK, C_SHIFT] = j - (WIN - 2)
    c[:GK, C_ISMEAN] = j == WIN - 1
    batch = (np.arange(NG)[None] * GQ + (np.arange(GK) // WIN)[:, None]) // NS
    c[:GK, C_ROW0:C_ROW0 + NG] = batch * KPAD
    c[:GK, C_MEANROW:C_MEANROW + NG] = NB * KPAD + batch
    c[:, C_LN1:C_LN1 + KC] = ln1.reshape(KC, P).T
    c[:, C_LN2:C_LN2 + KC] = ln2.reshape(KC, P).T
    c[:, C_WSHIFT:C_WSHIFT + WIN] = np.arange(WIN) - (WIN - 2)
    for b in range(NB):
        c[:, C_BATCH + NB * b + b] = 1.0
    return c


def kernel(**inputs):
    import concourse.bacc as bacc
    from concourse.bass_utils import run_bass_kernel_spmd as run

    a = {k: np.asarray(v) for k, v in inputs.items()}
    x = a["x"].reshape(T, D)
    fm = lambda w: np.ascontiguousarray(w.reshape(-1, P, w.shape[1]).transpose(1, 0, 2))
    s = np.zeros((N_STRIPES, P, KC, P), np.float32)
    at = 0

    def put(ts):
        nonlocal at
        s[at] = stripe_of(ts)
        at += 1

    qkv, wo = tiles(a["L0_attn_weight_qkv"].T), tiles(a["L0_attn_weight_out"].T)
    ffo, ffv = tiles(a["L0_ffn_Wo"]), tiles(a["L0_ffn_Wv"])
    for i in range(HP):
        for part in range(3):
            put(qkv[:, KC * part + i])
        put(ffo[:, i])
    for i in range(HP):
        put(wo[:, i])
        put(ffv[i])
    c = a["ctx_2048"]
    pad = np.zeros((NB, KPAD, D), np.float32)
    pad[:, :LK] = c
    for b in range(NB):
        ct = tiles(pad[b].T)
        for ti in range(KT):
            put(ct[:, ti])
    dq, uq, qr = (tiles(a["L0_xattn_W_" + n]) for n in ("dq", "uq", "qr"))
    uk, uv, xo = tiles(a["L0_xattn_W_uk"].T), tiles(a["L0_xattn_W_uv"]), tiles(a["L0_xattn_W_o"])
    for i in range(3):
        put(dq[:, i])
    for hf in range(2):
        for hp in range(HP):
            put([*uq[:, 2 * hp], *uq[:, 2 * hp + 1], qr[0, hp], qr[1, hp]])
            put([qr[2, hp], *uk[2 * hp], *uk[2 * hp + 1]])
        for i in range(N_UV):
            put([uv[k, h] for h in range(4 * i, 4 * i + 4) for k in range(2)])
        for i in range(KC):
            put(xo[:KC, i])
            put(xo[KC:, i])
    fq, fk = tiles(a["L0_ffn_Wq"].T), tiles(a["L0_ffn_Wk"].T)
    for i in range(HP):
        put(fq[:, i])
        put(fk[:, i])
    fin, fup, fdn = (tiles(a["L0_ffn_" + n].T) for n in ("W_in_base", "W_up_base", "W_down"))
    for fb in range(FB):
        for i in range(FM):
            put(fin[:, FM * fb + i])
            put(fup[:, FM * fb + i])
        for i in range(KC):
            put(fdn[FM * fb:FM * (fb + 1), i])
    assert at == N_STRIPES

    seg = a["itok_BxS_0_1023"].reshape(NG, GQ).astype(np.int32)
    arrays = {
        "xT": fm(x.T), "stripes": s, "w_kvc": fm(a["L0_xattn_W_kvc"]), "w_kvcT": fm(a["L0_xattn_W_kvc"].T),
        "w_kr": fm(a["L0_xattn_W_kr"]), "mod_a": fm(a["L0_ffn_A"]), "mod_b": np.ascontiguousarray(a["L0_ffn_B"]),
        "seg_rows": np.ascontiguousarray(np.tile(seg.T, (H, 1))),
        "seg_keys": np.ascontiguousarray(np.repeat(seg.T, WIN, axis=0)),
        "const": constants(a["L0_ffn_ln1_w"], a["L0_ffn_ln2_w"]),
    }
    nc = bacc.Bacc("TRN2", target_bir_lowering=False, num_devices=1)
    args = [nc.dram_tensor(n, v.shape, mybir.dt.from_np(v.dtype), kind="ExternalInput").ap() for n, v in arrays.items()]
    args += [nc.dram_tensor(n, shape, F32, kind="Internal").ap() for n, shape in
             (("key_table", (NB * KPAD + NB, ROW)), ("x1_dram", (P, KC, T)), ("g_dram", (P, KC, H * RA)))]
    args.append(nc.dram_tensor("out", (P, KC, T), F32, kind="ExternalOutput").ap())
    build(nc, *args)
    r = run(nc, [arrays], core_ids=[0])
    return np.ascontiguousarray(r.results[0]["out"].transpose(2, 1, 0).reshape(NB, NS, D))
```

```python
from contextlib import ExitStack

import numpy as np
import concourse.bass as bass
from concourse import mybir

F32 = mybir.dt.float32
F32R = mybir.dt.float32r
I32 = mybir.dt.int32
U32 = mybir.dt.uint32
ALU = mybir.AluOpType
ACT = mybir.ActivationFunctionType
AX = mybir.AxisListType

P = 128
D = 1024
KC = D // P
NB, NS = 8, 100
T = NB * NS
HT = T // 2
H = 16
HP = H // 2
LK = 722
KT = -(-LK // P)
KPAD = KT * P
KVC, QC, RR = 256, 384, 64
ROW = KVC + 2 * RR
WIN = 10
GQ = 8
GK = GQ * WIN
NG = T // GQ
UG = 2
UH = NG // 2 // UG
FF = 4096
FB, FM = 4, 8
RA = 16
NEG = -1e30
SN = 13
ST = NB * SN
EPS_LN, EPS_RMS = 1e-5, 1e-6

N_SELF, N_OUT, N_KV, N_DQ, N_PAIR, N_UV, N_WO, N_QK, N_MLP = 32, 16, NB * KT, 3, 16, 4, 16, 16, 96
N_HALF = N_PAIR + N_UV + N_WO
S_SELF = 0
S_OUT = S_SELF + N_SELF
S_KV = S_OUT + N_OUT
S_DQ = S_KV + N_KV
S_HALF = S_DQ + N_DQ
S_QK = S_HALF + 2 * N_HALF
S_MLP = S_QK + N_QK
N_STRIPES = S_MLP + N_MLP

C_IDENT = 0
C_ONES = C_IDENT + P
C_PERM = C_ONES + P
C_SMASK = C_PERM + P
C_FMASK = C_SMASK + ST
C_BMASK = C_FMASK + NS
C_QCOS = C_BMASK + GK
C_QSIN = C_QCOS + NS
C_KCOS = C_QSIN + NS
C_KSIN = C_KCOS + KT * RR
C_SHIFT = C_KSIN + KT * RR
C_ISMEAN = C_SHIFT + 1
C_ROW0 = C_ISMEAN + 1
C_MEANROW = C_ROW0 + NG
C_LN1 = C_MEANROW + NG
C_LN2 = C_LN1 + KC
C_WSHIFT = C_LN2 + KC
C_BATCH = C_WSHIFT + WIN
C_ZERO = C_BATCH + NB * NB
N_CONST = C_ZERO + P


def self_group(g):
    return min(SN * g, NS - SN)


(P_SET, P_SELF, P_OUT, P_KV, P_DQ, P_PA, P_SA, P_OA, P_PB, P_SB, P_OB, P_FP, P_FA, P_FU, P_FM) = range(15)
MK = 2 * 32 + RA
EARLY = 2
POOL_LAST = 7
RING = 10
HALF = ((P_PA, P_SA, P_OA), (P_PB, P_SB, P_OB))


class Buffers:

    def __init__(m, sb):
        m.con = sb("con", [P, N_CONST], F32)
        m.raw = [sb(f"raw{i}", [P, KC, P], F32) for i in range(2)]
        m.whi = [sb(f"whi{i}", [P, KC, P], F32R) for i in range(2)]
        m.w32 = sb("w32", [P, KC, P], F32, at="whi1")
        m.wlo = [sb(f"wlo{i}", [P, KC, P], F32R) for i in range(2)]
        m.sums = sb("sums", [P, 2, T], F32)
        m.square = sb("square", [P, 2, HT], F32)
        m.mean = sb("mean", [P, 2, HT], F32)
        m.rstd = sb("rstd", [P, 2, HT], F32)
        m.x_raw = sb("x_raw", [P, KC, T], F32, P_SET, P_SET)
        m.xh = sb("xh", [P, KC, T], F32R, P_SET, P_KV)
        m.xl = sb("xl", [P, KC, T], F32R, P_SET, P_OUT)
        m.aoh = sb("aoh", [P, HP, NB, NS], F32R, P_SELF, P_OUT)
        m.aol = sb("aol", [P, HP, NB, NS], F32R, P_SELF, P_OUT)
        m.ah = sb("ah", [P, KC, RA], F32R)
        m.al = sb("al", [P, KC, RA], F32R)
        m.a_raw = sb("a_raw", [P, KC, RA], F32, P_SET, P_SELF)
        m.wa = sb("wa", [P, HP, 2 * RA], F32, P_SET, P_OUT)
        m.g_raw = sb("g_raw", [P, KC, H * RA], F32, P_OUT, P_OUT)
        m.kvh = sb("kvh", [P, KC, KVC + RR], F32R, P_SET, P_KV)
        m.kvl = sb("kvl", [P, KC, KVC + RR], F32R, P_SET, P_KV)
        m.qkv = [sb(n, [P, NS, NB], F32, P_SELF, P_SELF) for n in ("q_self", "k_self", "v_self")]
        m.v_tok = sb("v_tok", [ST, 8, P], F32, P_SELF, P_SELF)
        m.probs = sb("probs", [ST, 4, 4 * ST], F32, P_SELF, P_SELF)
        m.probs_t = sb("probs_t", [ST, 4, 4 * ST], F32, P_SELF, P_SELF)
        m.peak = sb("peak", [ST, 4, 4], F32)
        m.total = sb("total", [ST, 4, 4], F32)
        m.share = sb("share", [ST, 4, 4], F32)
        m.kv_raw = sb("kv_raw", [P, KC, KVC], F32, P_SET, P_SET)
        m.y1 = sb("y1", [P, KC, T], F32, at="xh")
        m.x1h = sb("x1h", [P, KC, T], F32R, P_KV, P_DQ)
        m.x1l = sb("x1l", [P, KC, T], F32R, P_KV, P_DQ)
        m.kvc_t = sb("kvc_t", [P, 2, D], F32, P_SET, P_SET)
        m.kr_raw = sb("kr_raw", [P, 2, RR], F32, P_SET, P_SET)
        m.row = [sb(f"row{i}", [P, ROW], F32, P_KV, P_KV) for i in range(2)]
        m.rot = [sb(f"rot{i}", [P, 2, RR], F32, P_KV, P_KV) for i in range(2)]
        m.kv_sum = sb("kv_sum", [P, NB, KVC], F32, P_KV, P_KV)
        m.mean_row = sb("mean_row", [NB, ROW], F32, P_KV, P_KV)
        m.segk_i = sb("segk_i", [GK, NG], I32, P_SET, P_SET)
        m.segr_i = sb("segr_i", [P, NG], I32, P_SET, P_SET)
        m.segk = sb("segk", [GK, NG], F32, P_SET, P_SET)
        m.segr = sb("segr", [P, NG], F32, P_SET, P_SET)
        m.keyf = sb("keyf", [GK, NG], F32, P_SET, P_SET)
        m.keyi = sb("keyi", [GK, NG], U32, P_SET, P_SB)
        m.seen = sb("seen", [P, NG, WIN], F32, P_SET, P_SET)
        m.hide = sb("hide", [P, NG, WIN], F32, P_SET, P_SB)
        m.qch = [sb(f"qch{hf}", [P, 3, HT], F32R, P_DQ, (P_PA, P_PB)[hf]) for hf in range(2)]
        m.qcl = [sb(f"qcl{hf}", [P, 3, HT], F32R, P_DQ, (P_PA, P_PB)[hf]) for hf in range(2)]
        m.qa = sb("qa", [P, 2, NG // 2, H, GQ], F32, P_PA, P_OB)
        m.qr = sb("qr", [P, 2, NG // 2, H, GQ], F32, P_PA, P_OB)
        m.lath = sb("lath", [P, 2, NG // 2, H, GQ], F32R, at="qa")
        m.latl = sb("latl", [P, 2, NG // 2, H, GQ], F32R, at="qr")
        m.y2 = [sb(f"y2_{hf}", [P, KC, HT], F32, (P_OA, P_OB)[hf], P_FM) for hf in range(2)]
        m.ve = sb("ve", [P, HT], F32)
        m.root = sb("root", [P, HT], F32)
        m.tmp = sb("tmp", [P, HT], F32)
        m.qn = {}
        for ph, x in ((P_PA, "a"), (P_PB, "b")):
            m.qn[ph] = dict(
                h=sb(f"qnh_{x}", [P, 2, HT], F32R, ph, ph), l=sb(f"qnl_{x}", [P, 2, HT], F32R, ph, ph),
                r=sb(f"qraw_{x}", [P, HT], F32, ph, ph), c=sb(f"qcos_{x}", [P, HT], F32, ph, ph),
                s=sb(f"qsin_{x}", [P, HT], F32, ph, ph))
        m.win = [sb(f"win{i}", [GK, ROW], F32, P_PA, P_SB) for i in range(EARLY)]
        m.sp = {}
        for ph, x in ((P_SA, "a"), (P_SB, "b")):
            m.sp[ph] = dict(
                win=m.win + [sb(f"win{i}{x}", [GK, ROW], F32, ph, ph) for i in range(EARLY, RING)],
                wt=[sb(f"wt{i}{x}", [P, UG * 3, GK], F32, ph, ph) for i in range(2)],
                pr=[sb(f"pr{i}{x}", [P, UG, GK], F32, ph, ph) for i in range(2)],
                pt=[sb(f"pt{i}{x}", [GK, UG, P], F32, ph, ph) for i in range(2)],
                mk=[sb(f"mk{i}{x}", [P, UG, GK], F32, ph, ph) for i in range(2)],
                st=[sb(f"st{i}{x}", [P, 3, UG], F32, ph, ph) for i in range(2)])
        m.x1t = {ph: [sb(f"x1t{i}_{ph}", [P, HT], F32, ph, ph) for i in range(2)] for ph in (P_OA, P_OB)}
        m.rms2 = sb("rms2", [P, 2, HT], F32, P_OA, P_FU)
        m.xah = sb("xah", [P, KC, T], F32R, P_FP, P_FA)
        m.xal = sb("xal", [P, KC, T], F32R, P_FP, P_FA)
        m.g_new = sb("g_new", [P, KC, H * RA], F32, P_FP, P_FA)
        m.gh = sb("gh", [P, KC, H * RA], F32R, P_FP, P_FA)
        m.gl = sb("gl", [P, KC, H * RA], F32R, P_FP, P_FA)
        m.xa32 = [sb(f"xa32_{i}", [P, HT], F32, P_FP, P_FU) for i in range(2)]
        m.z_tok = sb("z_tok", [NS, NB, H * RA], F32, P_FP, P_FU)
        m.hh = sb("hh", [P, KC, T], F32R, P_FU, P_FM)
        m.hl = sb("hl", [P, KC, T], F32R, P_FU, P_FM)
        m.qk = [sb(n, [P, T], F32, P_FA, P_FA) for n in ("q_ffn", "k_ffn")]
        m.fprobs = sb("fprobs", [NS, 4, 4 * NS], F32, P_FA, P_FA)
        m.fprobs_t = sb("fprobs_t", [NS, 4, 4 * NS], F32, P_FA, P_FU)
        m.m_tok = sb("m_tok", [NS, NB, RA], F32, P_FA, P_FU)
        m.tanh_m = sb("tanh_m", [RA, T], F32, P_FU, P_FU)
        m.u_raw = sb("u_raw", [RA, T], F32, P_FU, P_FU)
        m.ustk = sb("ustk", [MK, T], F32R, P_FU, P_FM)
        m.b_raw = sb("b_raw", [MK, FF], F32, P_FU, P_FM)
        m.bstk = sb("bstk", [MK, P], F32R, P_FM, P_FM)
        m.ffh = sb("ffh", [P, FM, T], F32R, P_FM, P_FM)
        m.ffl = sb("ffl", [P, FM, T], F32R, P_FM, P_FM)
        m.gate = [sb(f"gate{i}", [P, HT], F32, P_FM, P_FM) for i in range(2)]
        m.act32 = [sb(f"act32_{i}", [P, HT], F32, P_FM, P_FM) for i in range(2)]


def place(nc):
    wanted, placed = [], {}

    def note(name, shape, dt, first=P_SET, last=P_FM, at=None):
        if at is None:
            size = -(-int(np.prod(shape[1:])) * 4 // 64) * 64
            wanted.append((-size, name, first, last))

    Buffers(note)
    for less, name, first, last in sorted(wanted, key=lambda w: w[0]):
        size = -less
        at = -(-nc.sbuf_base // 64) * 64
        for a, b in sorted((a, b) for a, b, f, l in placed.values() if not (l < first or f > last)):
            if at + size > a and at < b:
                at = b
        placed[name] = (at, at + size, first, last)
        assert at + size <= nc.sbuf_usable_end, name

    def alloc(name, shape, dt, first=P_SET, last=P_FM, at=None):
        return nc.alloc_sbuf_tensor_at(name, shape, dt, offset=placed[at or name][0])

    return Buffers(alloc)


class Steps:

    def __init__(self):
        self.base, self.k = 0, 0

    def next(self):
        self.k += 1
        return 1

    def so_far(self):
        return self.base + self.k

    def loop(self, i, start, stop, per):
        self.base, self.k = self.base + self.k, 0
        self.after = self.base + (stop - start) * per
        self.base, self.per = self.base + (i - start) * per, per

    def close(self):
        assert self.k == self.per, self.k
        self.base, self.k = self.after, 0


SIGNALS = """
con_loaded aux_loaded seg_loaded x_raw_0 x_raw_1 x_raw_2 x_raw_3 raw_loaded_0 raw_loaded_1
w_hi w_lo dve_step 
set_hi set_lo key_index wa_zero fold_done
self_q self_k self_v self_s self_vt self_pt self_pv self_wo
q_evac k_evac v_evac s_taken s_centered s_exp s_probs vt_evac pt_evac ao_hi ao_lo wa_done
out_done wv_done y1_read y1_done square_done square_added g_evac g_stored
stat_sums stat_taken stat_var stat_root stat_rstd 
kv_done kv_copied kv_read row_ready row_stored_0 row_stored_1 ln1_z ln1_hi ln1_lo x1_stored mean_done mean_ready
mean_stored
dq_done qc_hi qc_lo
uq_done qr_done ukA_done ukB_done qr_half perm_done qn_hi qn_lo qr_raw qa_act qa_dve q_rot qr_zero
gathered_0 gathered_1 gathered_2 gathered_3 gathered_4 gathered_5 gathered_6 gathered_7 gathered_8 gathered_9
wt_done wt_evac win_mask win_s win_taken win_centered win_exp win_probs win_pt win_pt_evac win_lat lat_hi lat_lo
uv_done vo_hi vo_lo wo_half wo_done x1_back_0 x1_back_1 y2_done x2_done
g_back g_hi g_lo in_ready in_hi in_low_even in_low_odd z_done z_evac
fq_done fk_done f_s f_pt f_pv fq_evac fk_evac f_taken f_centered f_exp f_probs f_pt_evac 
m_evac mt_done m_tanh ha_done u_ready u_hi u_lo b_loaded b_hi b_lo u_zero
ff_gate ff_up silu_done ff_prod ff_hi ff_lo down_done down_added final_0 final_1 pool_step out_stored
""".split()



def ao_parts(t, C, a):
    last = self_group(7) + SN - 7 * SN
    parts = []
    for bank, first, stop, n0 in ((0, 0, 4 * SN, 0), (1, 0, 3 * SN, 4 * SN), (1, 4 * SN - last, 4 * SN, 7 * SN)):
        parts.append((t[:, a, :, n0:n0 + stop - first],
                      C[bank][:, NB * first:NB * stop].rearrange("p (n l) -> p l n", l=NB)))
    return parts


def lat_parts(t, C, u):
    src = C[u % 2][:, :].rearrange("p (g c r) -> p c g r", g=UG, c=2)
    return [(t[:, c, UG * u:UG * u + UG, :, :].rearrange("p g h q -> p g (h q)"), src[:, c]) for c in range(2)]


def build(nc, xT, stripes, w_kvc, w_kvcT, w_kr, mod_a, mod_b, seg_rows, seg_keys, const, key_table,
          x1_dram, g_dram, out):
    with ExitStack() as ctx:
        m = place(nc)
        bank = [ctx.enter_context(nc.psum_tensor(f"bank{i}", [P, 512], F32)) for i in range(8)]
        G, A, C = bank[0:2], bank[2:6], bank[6:8]
        sem = {n: ctx.enter_context(nc.semaphore(n)) for n in SIGNALS}
        con, raw, whi, wlo = m.con, m.raw, m.whi, m.wlo
        ident = con[:, C_IDENT:C_IDENT + P]
        ones = con[:, C_ONES:C_ONES + P]

        def positive(n):
            return not isinstance(n, int) or n > 0

        def half(t, hf):
            return t[:, hf * HT:(hf + 1) * HT]

        def grouped(t):
            return t.rearrange("p (g q) -> p g q", q=GQ)

        block = ctx.enter_context(nc.Block())

        @block.sync
        def _(sp):
            for c in range(4):
                sp.dma_start(m.x_raw[:, 2 * c:2 * c + 2, :], xT[:, 2 * c:2 * c + 2, :]).then_inc(sem[f"x_raw_{c}"], 16)
                if c == 0:
                    sp.dma_start(raw[0][:, :, :], stripes[0]).then_inc(sem["raw_loaded_0"], 16)
            sp.dma_start(raw[1][:, :, :], stripes[1]).then_inc(sem["raw_loaded_1"], 16)
            with sp.Fori(1, N_STRIPES // 2) as j:
                for i in range(2):
                    sp.wait_ge(sem["w_lo"], 4 * j - 2 + 2 * i)
                    sp.dma_start(raw[i][:, :, :], stripes[2 * j + i]).then_inc(sem[f"raw_loaded_{i}"], 16)
            if N_STRIPES % 2:
                sp.wait_ge(sem["w_lo"], 2 * (N_STRIPES - 2))
                sp.dma_start(raw[0][:, :, :], stripes[N_STRIPES - 1]).then_inc(sem["raw_loaded_0"], 16)
            last = [("final_1", kc, 1) for kc in range(KC)]
            for kc in range(POOL_LAST):
                last.insert(2 * kc, ("final_0", kc, 0))
            last += [("final_1", kc, 0) for kc in range(POOL_LAST, KC)]
            count = {"final_0": 0, "final_1": 0}
            for name, kc, u in last:
                count[name] += 1
                sp.wait_ge(sem[name], count[name])
                sp.dma_start(half(out[:, kc, :], u), m.y2[u][:, kc, :]).then_inc(sem["out_stored"], 16)
            sp.wait_ge(sem["out_stored"], 32 * KC)

        @block.gpsimd
        def _(pool):
            def low(s, slot):
                for part in range(2):
                    t = slice(KC // 2 * part, KC // 2 * (part + 1))
                    pool.wait_ge(sem["w_hi"], 2 * s + part + 1)
                    pool.tensor_tensor(wlo[slot][:, t, :], raw[slot][:, t, :], whi[slot][:, t, :].bitcast(F32),
                                       ALU.subtract).then_inc(sem["w_lo"], 1)

            def lows(first, n):
                if n < 4:
                    for s in range(first, first + n):
                        low(s, s % 2)
                    return
                with pool.Fori(0, n // 2) as j:
                    for i in range(2):
                        low(2 * j + first + i, (first + i) % 2)
                if n % 2:
                    low(first + n - 1, (first + n - 1) % 2)

            def taken(s):
                pool.wait_ge(sem["w_hi"], 2 * s + 2)
                pool.tensor_tensor(wlo[1][:, 0, 0:8], raw[1][:, 0, 0:8], m.w32[:, 0, 0:8], ALU.subtract)\
                    .then_inc(sem["w_lo"], 2)

            with pool.Fori(0, HP) as i:
                for j in range(3):
                    low(4 * i + S_SELF + j, j % 2)
                taken(4 * i + S_SELF + 3)
            with pool.Fori(0, HP) as i:
                low(2 * i + S_OUT, 0)
                taken(2 * i + S_OUT + 1)
            lows(S_KV, S_HALF - S_KV)
            for hf in range(2):
                p_pair, p_win, _ = HALF[hf]
                s0 = S_HALF + hf * N_HALF
                turned = m.qr[:, 0, :, :, :].rearrange("p g (h e) q -> p g h e q", e=2)
                for e in range(2):
                    for i in range(2):
                        low(s0 + 2 * e + i, (s0 + i) % 2)
                    pool.wait_ge(sem["dq_done"], 6)
                    if hf:
                        pool.wait_ge(sem["wo_done"], HP)
                    pool.wait_ge(sem["w_lo"], 2 * (s0 + 2 * e + 2))
                    pool.memset(turned[64 - 64 * e:128 - 64 * e, :, :, e, :], 0.0).then_inc(sem["qr_zero"], 1)
                    pool.wait_ge(sem["qr_zero"], 2 * hf + e + 1)
                with pool.Fori(2, HP) as hp:
                    for i in range(2):
                        low(2 * hp + s0 + i, (s0 + i) % 2)
                if hf == 0:
                    pool.wait_ge(sem["row_stored_0"], 16 * N_KV // 2)
                    pool.wait_ge(sem["row_stored_1"], 16 * N_KV // 2)
                    pool.wait_ge(sem["mean_stored"], 16)
                    pool.wait_ge(sem["key_index"], 1)
                w = m.sp[p_win]
                for u in range(UH):
                    if u == EARLY // UG:
                        pool.wait_ge(sem["perm_done"], HP * (hf + 1))
                        pool.wait_ge(sem["q_rot"], 2 * HP * (hf + 1))
                    if u >= RING // UG:
                        pool.wait_ge(sem["win_lat"], UH * hf + u - RING // UG + 1)
                    for gi in range(UG):
                        g = hf * NG // 2 + UG * u + gi
                        r = (UG * u + gi) % RING
                        pool.indirect_dma_start(
                            out=w["win"][r][:, :], out_offset=None, in_=key_table,
                            in_offset=bass.IndirectOffsetOnAxis(ap=m.keyi[:, g:g + 1], axis=0),
                        ).then_inc(sem[f"gathered_{r}"], 16)
                    if u < EARLY // UG:
                        continue
                    for v in (range(EARLY // UG + 1) if u == EARLY // UG else (u,)):
                        if v >= 2:
                            pool.wait_ge(sem["win_taken"], UH * hf + v - 1)
                        for gi in range(UG):
                            g = hf * NG // 2 + UG * v + gi
                            ins = pool.tensor_tensor(
                                w["mk"][v % 2][:, gi, :].rearrange("p (q j) -> p q j", j=WIN),
                                con[:, C_BMASK:C_BMASK + GK].rearrange("p (q j) -> p q j", j=WIN),
                                m.hide[:, g, :].unsqueeze(1).to_broadcast([P, GQ, WIN]), ALU.add)
                        ins.then_inc(sem["win_mask"], 1)
                lows(s0 + N_PAIR, N_UV + N_WO)
            lows(S_QK, 2)

            def input_low(t, th, first):
                for n in range(first + 1, first + 2 * KC, 2):
                    u, kc = n // KC % 2, n % KC
                    pool.wait_ge(sem["in_hi"], n + 1)
                    pool.tensor_tensor(half(t[:, kc, :], u), m.xa32[1][:, :], half(th[:, kc, :], u).bitcast(F32),
                                       ALU.subtract).then_inc(sem["in_low_odd"], 1)
                    if n == KC - 1:
                        pool.wait_ge(sem["g_hi"], 1)
                        pool.tensor_tensor(m.gl[:, :, :], m.g_new[:, :, :], m.gh[:, :, :].bitcast(F32), ALU.subtract)\
                            .then_inc(sem["g_lo"], 1)

            input_low(m.xal, m.xah, 0)
            lows(S_QK + 2, N_QK - 2)
            lows(S_MLP, 2)
            input_low(m.hl, m.hh, 2 * KC)
            lows(S_MLP + 2, N_MLP - 2)
            pool.wait_ge(sem["stat_rstd"], 7)
            for kc in range(POOL_LAST):
                y = m.y2[0][:, kc, :]
                pool.tensor_tensor(y, y, m.mean[:, 0, :], ALU.subtract).then_inc(sem["pool_step"], 1)
                pool.wait_ge(sem["pool_step"], kc + 1)
                pool.tensor_tensor(y, y, m.rstd[:, 0, :], ALU.mult).then_inc(sem["final_0"], 1)

        @block.scalar
        def _(act):
            def whole(k, i, per):
                act.wait_ge(sem["raw_loaded_1"], 16 * (k // 2 + 1) + 8 * per * i)
                act.activation(m.w32[:, :, :], raw[1][:, :, :], ACT.Copy).then_inc(sem["w_hi"], 2)

            def high(k, i, per):
                act.wait_ge(sem[f"raw_loaded_{k % 2}"], 16 * (k // 2 + 1) + 8 * per * i)
                for part in range(2):
                    t = slice(KC // 2 * part, KC // 2 * (part + 1))
                    act.activation(whi[k % 2][:, t, :], raw[k % 2][:, t, :], ACT.Copy).then_inc(sem["w_hi"], 1)

            for c in range(4):
                act.wait_ge(sem[f"x_raw_{c}"], 16)
                act.activation(m.xh[:, 2 * c:2 * c + 2, :], m.x_raw[:, 2 * c:2 * c + 2, :], ACT.Copy)\
                   .then_inc(sem["set_hi"], 1)
                if c == 0:
                    high(0, 0, 0)
                if c == 1:
                    act.dma_start(con[:, :], const).then_inc(sem["con_loaded"], 16)
                if c == 2:
                    for dst, src in ((m.a_raw[:, :, :], mod_a), (m.kv_raw[:, :, :], w_kvc),
                                     (m.kvc_t[:, :, :], w_kvcT), (m.kr_raw[:, :, :], w_kr)):
                        act.dma_start(dst, src).then_inc(sem["aux_loaded"], 16)
                    act.dma_start(m.segk_i[:, :], seg_keys).then_inc(sem["seg_loaded"], 16)
                    act.dma_start(m.segr_i[:, :], seg_rows).then_inc(sem["seg_loaded"], 16)

            def aux_high():
                act.wait_ge(sem["aux_loaded"], 64)
                act.activation(m.ah[:, :, :], m.a_raw[:, :, :], ACT.Copy).then_inc(sem["set_hi"], 1)
                act.activation(m.kvh[:, :, 0:KVC], m.kv_raw[:, :, :], ACT.Copy).then_inc(sem["set_hi"], 1)

            def self_act(i, product, attn, beside=None):
                a = i - 1

                def exps(j):
                    act.wait_ge(sem["s_centered"], 4 * a + j + 1)
                    act.activation(m.probs[:, j, :], m.probs[:, j, :], ACT.Exp).then_inc(sem["s_exp"], 1)

                def evac(u, done, t, name):
                    act.wait_ge(sem[done], 2 * i + u + 1)
                    act.activation(t[:, :, u * NB // 2:(u + 1) * NB // 2].rearrange("p n b -> p b n"), G[u][:, 0:HT].rearrange("p (b n) -> p b n", n=NS), ACT.Copy)\
                       .then_inc(sem[name], 1)

                if product:
                    if positive(i):
                        act.wait_ge(sem["self_wo"], i)
                    high(S_SELF + 1, i, 4)
                if attn:
                    exps(0)
                    exps(1)
                if product:
                    evac(0, "self_q", m.qkv[0][:, :, :], "q_evac")
                if attn:
                    exps(2)
                    exps(3)
                if product:
                    evac(1, "self_q", m.qkv[0][:, :, :], "q_evac")
                    act.wait_ge(sem["self_q"], 2 * i + 2)
                    high(S_SELF + 2, i, 4)
                    if beside:
                        beside()
                    for u in range(2):
                        evac(u, "self_k", m.qkv[1][:, :, :], "k_evac")
                    act.wait_ge(sem["self_k"], 2 * i + 2)
                    whole(S_SELF + 3, i, 4)
                if attn:
                    for j in range(4):
                        act.wait_ge(sem["self_pt"], 4 * a + j + 1)
                        act.activation(m.probs_t[:, j, :], A[j][0:ST, 0:4 * ST], ACT.Copy).then_inc(sem["pt_evac"], 1)
                if product:
                    for u in range(2):
                        evac(u, "self_v", m.qkv[2][:, :, :], "v_evac")
                    act.wait_ge(sem["self_v"], 2 * i + 2)
                    high(S_SELF + 4, i, 4)
                if attn:
                    for dst, src in ao_parts(m.aoh, C, a):
                        act.wait_ge(sem["self_pv"], a + 1)
                        act.activation(dst, src, ACT.Copy).then_inc(sem["ao_hi"], 1)
                if product:
                    act.wait_ge(sem["self_wo"], i + 1)
                    act.wait_ge(sem["wa_zero"], 1)
                    for e in range(2):
                        rows = slice(64 * e, 64 * e + 64)
                        act.activation(m.wa[rows, i, RA * e:RA * e + RA], G[0][rows, 0:RA], ACT.Copy)\
                           .then_inc(sem["wa_done"], 1)

            self_act(0, True, False, aux_high)
            act.wait_ge(sem["fold_done"], 1)
            act.activation(m.kvh[:, :, KVC:KVC + RR], C[0][:, :].rearrange("p (k r) -> p k r", r=RR), ACT.Copy)\
               .then_inc(sem["set_hi"], 1)
            self_act(1, True, True)
            with act.Fori(2, HP) as i:
                self_act(i, True, True)
            self_act(HP, False, True)

            def out_act(i):
                first = isinstance(i, int) and i == 0
                act.wait_ge(sem["self_wo" if first else "wv_done"], HP if first else i)
                whole(S_OUT + 1, i, 2)
                for u in range(2):
                    act.wait_ge(sem["y1_done"], 2 * i + u + 1)
                    if not first:
                        act.wait_ge(sem["square_added"], 2 * i + u - 1)
                    act.activation(m.square[:, u, :], half(m.y1[:, i, :], u), ACT.Square).then_inc(sem["square_done"], 1)
                    if u == 0:
                        act.wait_ge(sem["out_done"], 2 * i + 2)
                        high(S_OUT + 2, i, 2)
                act.wait_ge(sem["wv_done"], i + 1)
                act.activation(m.g_raw[:, :, bass.ds(2 * RA * i, 2 * RA)],
                               A[3][:, 0:KC * 2 * RA].rearrange("p (k r) -> p k r", r=2 * RA), ACT.Copy)\
                   .then_inc(sem["g_evac"], 1)

            out_act(0)
            with act.Fori(1, HP) as i:
                out_act(i)
            act.wait_ge(sem["g_evac"], HP)
            act.dma_start(g_dram, m.g_raw[:, :, :]).then_inc(sem["g_stored"], 16)

            def root(n):
                act.wait_ge(sem["stat_var"], n)
                act.activation(m.root[:, :], m.ve[:, :], ACT.Sqrt).then_inc(sem["stat_root"], 1)

            act.wait_ge(sem["wv_done"], HP)
            high(S_KV + 1, 0, 0)
            act.wait_ge(sem["kv_done"], 1)
            high(S_KV + 2, 0, 0)
            def store_row(n, i):
                act.wait_ge(sem["row_ready"], n + 1 + KT * i)
                act.wait_ge(sem["kv_copied"], n + 1 + KT * i)
                act.dma_start(key_table[bass.ds((n + KT * i) * P, P), :] if not isinstance(i, int)
                              else key_table[(n + KT * i) * P:(n + KT * i + 1) * P, :],
                              m.row[n % 2][:, :]).then_inc(sem[f"row_stored_{n % 2}"], 16)

            def kv_act(b):
                first = isinstance(b, int) and b == 0
                for ti in range(KT):
                    act.wait_ge(sem["kv_done"], KT * b + ti + 1)
                    if not (first and ti == 0):
                        high(S_KV + ti + 2, b, KT)
                    if not (first and ti < 2):
                        act.wait_ge(sem[f"row_stored_{ti % 2}"], 16 * (KT // 2 * b + ti // 2))
                    act.activation(m.row[ti % 2][:, 0:KVC], G[ti % 2][:, 0:KVC], ACT.Copy)\
                       .then_inc(sem["kv_copied"], 1)
                    if first and ti in (0, 2):
                        root(ti // 2 + 1)
                    if not (first and ti == 0):
                        if ti:
                            store_row(ti - 1, b)
                        else:
                            store_row(KT - 1, b - 1)
                    if ti == (KT - 1 if first else 0):
                        for u in range(2):
                            act.wait_ge(sem["ln1_z"], 2 * b + u + 1)
                            act.activation(half(m.x1h[:, b, :], u), half(m.y1[:, b, :], u), ACT.Copy)\
                               .then_inc(sem["ln1_hi"], 1)
                        act.dma_start(x1_dram[:, b, :], m.y1[:, b, :]).then_inc(sem["x1_stored"], 16)

            kv_act(0)
            with act.Fori(1, NB) as b:
                kv_act(b)
            store_row(KT - 1, NB - 1)
            act.wait_ge(sem["mean_done"], 1)
            act.activation(m.mean_row[:, 0:KVC], G[0][0:NB, 0:KVC], ACT.Copy, scale=1.0 / LK).then_inc(sem["mean_ready"], 1)
            act.wait_ge(sem["mean_ready"], 2)
            act.dma_start(key_table[NB * KPAD:NB * KPAD + NB, :], m.mean_row[:, :]).then_inc(sem["mean_stored"], 16)

            for k in range(3):
                if k:
                    act.wait_ge(sem["dq_done"], 2 * k)
                    high(S_DQ + k + 1, 0, 0)
                for u in range(2):
                    act.wait_ge(sem["dq_done"], 2 * k + u + 1)
                    act.activation(m.qch[u][:, k, :], G[u][:, 0:HT], ACT.Copy).then_inc(sem["qc_hi"], 1)

            for hf in range(2):
                p_pair, p_win, p_out = HALF[hf]
                s0 = S_HALF + hf * N_HALF
                q = m.qn[p_pair]

                def pair_act(hp):
                    n = HP * hf + hp
                    if isinstance(hp, int) and hp == 0:
                        act.wait_ge(sem["wo_done" if hf else "dq_done"], HP if hf else 6)
                        high(s0 + 1, 0, 0)
                    else:
                        act.wait_ge(sem["ukB_done"], 2 * n)
                        high(s0 + 1, hp, 2)
                    for u in range(2):
                        act.wait_ge(sem["uq_done"], 2 * n + u + 1)
                        act.activation(q["h"][:, u, :], G[u][:, 0:HT], ACT.Copy).then_inc(sem["qn_hi"], 1)
                    act.wait_ge(sem["qr_done"], n + 1)
                    if positive(2 * n):
                        act.wait_ge(sem["q_rot"], 2 * n)
                    act.activation(q["r"][:, :], A[0][:, 0:HT], ACT.Copy).then_inc(sem["qr_raw"], 1)
                    act.wait_ge(sem["qr_half"], n + 1)
                    high(s0 + 2, hp, 2)
                    for c in range(2):
                        act.wait_ge(sem["ukA_done"], 2 * n + c + 1)
                        act.activation(m.qa[:, c, :, 2 * hp, :], grouped(A[2 + c][:, 0:HT]), ACT.Copy)\
                           .then_inc(sem["qa_act"], 1)

                pair_act(0)
                if hf == 0:
                    with act.Fori(1, HP) as hp:
                        pair_act(hp)
                else:
                    pair_act(1)
                    root(3)
                    for hp in range(2, 5):
                        pair_act(hp)
                    root(4)
                    with act.Fori(5, HP) as hp:
                        pair_act(hp)

                act.wait_ge(sem["ukB_done"], H * (hf + 1))
                high(s0 + N_PAIR + 1, 0, 0)

                w = m.sp[p_win]
                for v in range(UH + 3):
                    if v < UH:
                        n = UH * hf + v
                        act.wait_ge(sem["wt_done"], n + 1)
                        if positive(n - 1):
                            act.wait_ge(sem["win_s"], n - 1)
                        act.activation(w["wt"][v % 2][:, :, :], G[v % 2][:, 0:UG * 3 * GK].rearrange("p (a k) -> p a k", k=GK), ACT.Copy)\
                           .then_inc(sem["wt_evac"], 1)
                    if 2 <= v < UH + 2:
                        u, n = v - 2, UH * hf + v - 2
                        act.wait_ge(sem["win_pt"], n + 1)
                        act.activation(w["pt"][u % 2][:, :, :], A[2 + u % 2][0:GK, 0:UG * P].rearrange("p (a k) -> p a k", k=P), ACT.Copy)\
                           .then_inc(sem["win_pt_evac"], 1)
                    if 1 <= v < UH + 1:
                        u, n = v - 1, UH * hf + v - 1
                        act.wait_ge(sem["win_centered"], n + 1)
                        act.activation(w["pr"][u % 2][:, :, :], w["pr"][u % 2][:, :, :], ACT.Exp)\
                           .then_inc(sem["win_exp"], 1)
                    if v >= 3:
                        u, n = v - 3, UH * hf + v - 3
                        act.wait_ge(sem["win_lat"], n + 1)
                        for dst, src in lat_parts(m.lath, C, u):
                            act.activation(dst, src, ACT.Copy).then_inc(sem["lat_hi"], 1)

                for i in range(N_UV):
                    if i:
                        act.wait_ge(sem["uv_done"], H * hf + 4 * i)
                        high(s0 + N_PAIR + i + 1, 0, 0)
                    for h in range(4 * i, 4 * i + 4):
                        act.wait_ge(sem["uv_done"], H * hf + h + 1)
                        act.activation(m.lath[:, 0, :, h, :], grouped(A[h % 4][:, 0:HT]), ACT.Copy)\
                           .then_inc(sem["vo_hi"], 1)

                x1t = m.x1t[p_out]

                def fetch(k, i):
                    if positive(HP * hf + k + 2 * i - 1):
                        act.wait_ge(sem["y2_done"], HP * hf + k + 2 * i - 1)
                    act.dma_start(x1t[k % 2][:, :], half(x1_dram[:, k + 2 * i, :], hf)).then_inc(sem[f"x1_back_{k % 2}"], 16)

                act.wait_ge(sem["x1_stored"], 16 * KC)
                fetch(0, 0)
                fetch(1, 0)

                def square_of(k, i, more=True):
                    n = HP * hf + 2 * i + k
                    act.wait_ge(sem["y2_done"], n + 1)
                    if not (hf == 0 and isinstance(i, int) and i == 0):
                        act.wait_ge(sem["square_added"], 2 * HP + n - 1)
                    act.activation(m.square[:, k, :], m.y2[hf][:, 2 * i + k, :], ACT.Square)\
                       .then_inc(sem["square_done"], 1)
                    if more:
                        fetch(2 + k, i)

                def wo_act(i):
                    first = isinstance(i, int) and i == 0
                    for k in range(2):
                        n = HP * hf + 2 * i + k
                        more = not (k and isinstance(i, int) and i == HP // 2 - 1)
                        if first and k == 0:
                            act.wait_ge(sem["uv_done"], H * (hf + 1))
                            high(s0 + N_PAIR + N_UV + 1, 0, 0)
                        else:
                            act.wait_ge(sem["wo_done"], n)
                            high(s0 + N_PAIR + N_UV + 2 * k + 1, i, 4)
                            square_of(1 - k, i if k else i - 1, more)
                        act.wait_ge(sem["wo_half"], n + 1)
                        high(s0 + N_PAIR + N_UV + 2 * k + 2, i, 4)

                wo_act(0)
                with act.Fori(1, HP // 2 - 1) as i:
                    wo_act(i)
                wo_act(HP // 2 - 1)
                if hf == 0:
                    square_of(1, HP // 2 - 1, False)

            act.wait_ge(sem["wo_done"], 2 * HP)
            high(S_QK + 1, 0, 0)
            act.wait_ge(sem["y2_done"], 2 * HP)
            act.wait_ge(sem["square_added"], 4 * HP - 2)
            act.activation(m.square[:, 1, :], m.y2[1][:, KC - 1, :], ACT.Square).then_inc(sem["square_done"], 1)

            act.wait_ge(sem["g_stored"], 16)
            act.dma_start(m.g_new[:, :, :], g_dram).then_inc(sem["g_back"], 16)
            def xa_high(n):
                u, kc = n // KC, n % KC
                act.wait_ge(sem["in_ready"], n + 1)
                act.activation(half(m.xah[:, kc, :], u), m.xa32[n % 2][:, :], ACT.Copy).then_inc(sem["in_hi"], 1)

            def z_out(b):
                act.wait_ge(sem["z_done"], b + 1)
                act.activation(m.z_tok[:, b, :], G[b % 2][0:NS, 0:H * RA], ACT.Copy).then_inc(sem["z_evac"], 1)

            for n in range(KC):
                xa_high(n)
            act.wait_ge(sem["g_back"], 16)
            act.activation(m.gh[:, :, :], m.g_new[:, :, :], ACT.Copy).then_inc(sem["g_hi"], 1)
            act.wait_ge(sem["fq_done"], 1)
            act.activation(half(m.qk[0][:, :], 0), G[0][:, 0:HT], ACT.Copy).then_inc(sem["fq_evac"], 1)
            root(5)
            act.wait_ge(sem["fk_done"], 1)
            act.activation(half(m.qk[1][:, :], 0), G[1][:, 0:HT], ACT.Copy).then_inc(sem["fk_evac"], 1)
            root(6)
            z_out(0)
            z_out(1)
            for n in range(KC, 2 * KC):
                xa_high(n)
                if n == KC + 2:
                    z_out(2)
                if n == KC + 5:
                    z_out(3)
            act.wait_ge(sem["fq_done"], 2)
            act.activation(half(m.qk[0][:, :], 1), G[0][:, 0:HT], ACT.Copy).then_inc(sem["fq_evac"], 1)
            high(S_QK + 2, 0, 0)
            act.wait_ge(sem["fk_done"], 2)
            act.activation(half(m.qk[1][:, :], 1), G[1][:, 0:HT], ACT.Copy).then_inc(sem["fk_evac"], 1)

            def ffn_act(i, product, attn):
                a = i - 1

                def exps(j):
                    act.wait_ge(sem["f_centered"], 4 * a + j + 1)
                    act.activation(m.fprobs[:, j, :], m.fprobs[:, j, :], ACT.Exp).then_inc(sem["f_exp"], 1)

                def evac(u, done, t, name):
                    act.wait_ge(sem[done], 2 * i + u + 1)
                    act.activation(half(t[:, :], u), G[u][:, 0:HT], ACT.Copy).then_inc(sem[name], 1)

                if product:
                    act.wait_ge(sem["fk_done"], 2 * i)
                    high(S_QK + 1, i, 2)
                if attn:
                    exps(0)
                    exps(1)
                if product:
                    evac(0, "fq_done", m.qk[0], "fq_evac")
                if attn:
                    exps(2)
                    exps(3)
                if product:
                    evac(1, "fq_done", m.qk[0], "fq_evac")
                    act.wait_ge(sem["fq_done"], 2 * i + 2)
                    high(S_QK + 2, i, 2)
                    evac(0, "fk_done", m.qk[1], "fk_evac")
                if attn:
                    for j in range(4):
                        act.wait_ge(sem["f_pt"], 4 * a + j + 1)
                        act.activation(m.fprobs_t[:, j, :], A[j][0:NS, 0:4 * NS], ACT.Copy)\
                           .then_inc(sem["f_pt_evac"], 1)
                if product:
                    evac(1, "fk_done", m.qk[1], "fk_evac")

            ffn_act(1, True, True)
            with act.Fori(2, HP) as i:
                ffn_act(i, True, True)
            ffn_act(HP, False, True)
            act.wait_ge(sem["fk_done"], 2 * HP)
            high(S_MLP + 1, 0, 0)
            for n in range(2 * KC):
                u, kc = n // KC, n % KC
                act.wait_ge(sem["in_ready"], 2 * KC + n + 1)
                act.activation(half(m.hh[:, kc, :], u), m.xa32[n % 2][:, :], ACT.Copy).then_inc(sem["in_hi"], 1)
                if n == 3:
                    act.wait_ge(sem["f_pv"], HP)
                    act.activation(m.m_tok[:, :, :], C[0][0:NS, 0:NB * RA].rearrange("p (b r) -> p b r", r=RA), ACT.Copy)\
                       .then_inc(sem["m_evac"], 1)
                if n == 0:
                    for r in range(MK // RA):
                        act.dma_start(m.b_raw[RA * r:RA * r + RA, :], mod_b).then_inc(sem["b_loaded"], 16)
            for u in range(2):
                act.wait_ge(sem["mt_done"], 2)
                act.activation(half(m.tanh_m[:, :], u), A[u][0:RA, 0:HT], ACT.Tanh).then_inc(sem["m_tanh"], 1)
            act.wait_ge(sem["u_zero"], 1)
            for u in range(2):
                act.wait_ge(sem["u_ready"], u + 1)
                for r in (0, 64):
                    act.activation(half(m.ustk[r:r + RA, :], u), half(m.u_raw[:, :], u), ACT.Copy)\
                       .then_inc(sem["u_hi"], 1)

            def b_high(f):
                if positive(2 * f):
                    act.wait_ge(sem["ff_gate"], 2 * f)
                act.activation(m.bstk[:, :], m.b_raw[:, bass.ds(f * P, P)] if not isinstance(f, int)
                     else m.b_raw[:, f * P:(f + 1) * P], ACT.Copy).then_inc(sem["b_hi"], 1)

            act.wait_ge(sem["b_loaded"], 16 * MK // RA)

            def up_act(fb, fm):
                f = FM * fb + fm
                b_high(f)
                if isinstance(f, int) and f == 0:
                    pass
                elif isinstance(fm, int) and fm == 0:
                    act.wait_ge(sem["down_done"], 2 * FM * fb)
                    high(S_MLP + 1, fb, 24)
                else:
                    act.wait_ge(sem["ff_up"], 2 * f)
                    high2(S_MLP + 1, fb, fm)
                for u in range(2):
                    act.wait_ge(sem["ff_gate"], 2 * f + u + 1)
                    if not (isinstance(f, int) and f == 0):
                        act.wait_ge(sem["ff_prod"], 2 * f + u - 1)
                    act.activation(m.gate[u][:, :], G[u][:, 0:HT], ACT.Silu).then_inc(sem["silu_done"], 1)
                act.wait_ge(sem["ff_gate"], 2 * f + 2)
                high2(S_MLP + 2, fb, fm)
                for u in range(2):
                    act.wait_ge(sem["ff_prod"], 2 * f + u + 1)
                    act.activation(half(m.ffh[:, fm, :], u), m.act32[u][:, :], ACT.Copy).then_inc(sem["ff_hi"], 1)

            def high2(k, fb, fm):
                act.wait_ge(sem[f"raw_loaded_{k % 2}"], 16 * (k // 2 + 1) + 16 * 12 * fb + 16 * fm)
                for part in range(2):
                    t = slice(KC // 2 * part, KC // 2 * (part + 1))
                    act.activation(whi[k % 2][:, t, :], raw[k % 2][:, t, :], ACT.Copy).then_inc(sem["w_hi"], 1)

            def down_act(fb, c, i, last):
                n = FM * fb + c + 2 * i
                if not (last and isinstance(i, int) and i == KC // 2 - 1 and c == 1):
                    k = S_MLP + 2 * FM + c + 1
                    if c == 0 and isinstance(i, int) and i == 0:
                        act.wait_ge(sem["ff_up"], 2 * FM * (fb + 1))
                        high2(k, fb, i)
                    else:
                        act.wait_ge(sem["down_done"], 2 * n)
                        high2(k, fb, i)
                if last:
                    for u in range(2):
                        n3 = 2 * (c + 2 * i) + u
                        act.wait_ge(sem["down_added"], 2 * n + u + 1)
                        if not (isinstance(i, int) and i == 0 and c == 0):
                            act.wait_ge(sem["square_added"], 4 * HP + n3 - 1)
                        act.activation(m.square[:, u, :], m.y2[u][:, c + 2 * i, :], ACT.Square)\
                           .then_inc(sem["square_done"], 1)

            def block_act(fb, last):
                up_act(fb, 0)
                with act.Fori(1, FM) as fm:
                    up_act(fb, fm)
                for c in range(2):
                    down_act(fb, c, 0, last)
                with act.Fori(1, KC // 2 - 1) as i:
                    for c in range(2):
                        down_act(fb, c, i, last)
                for c in range(2):
                    down_act(fb, c, KC // 2 - 1, last)

            block_act(0, False)
            with act.Fori(1, FB - 1) as fb:
                block_act(fb, False)
            block_act(FB - 1, True)
            root(7)
            root(8)

        @block.vector
        def _(dve):
            steps = Steps()

            dve.memset(m.sums[:, :, :], 0.0).then_inc(sem["dve_step"], steps.next())
            dve.memset(m.wa[:, :, :], 0.0).then_inc(sem["wa_zero"], 1)
            for kc in range(KC):
                dve.wait_ge(sem[f"x_raw_{kc // 2}"], 16)
                dve.wait_ge(sem["set_hi"], kc // 2 + 1)
                dve.tensor_tensor(m.xl[:, kc, :], m.x_raw[:, kc, :], m.xh[:, kc, :].bitcast(F32), ALU.subtract)\
                   .then_inc(sem["set_lo"], 1)
            dve.wait_ge(sem["set_hi"], 5)
            dve.wait_ge(sem["aux_loaded"], 64)
            dve.tensor_tensor(m.al[:, :, :], m.a_raw[:, :, :], m.ah[:, :, :].bitcast(F32), ALU.subtract)\
               .then_inc(sem["set_lo"], 1)
            dve.wait_ge(sem["set_hi"], 6)
            dve.tensor_tensor(m.kvl[:, :, 0:KVC], m.kv_raw[:, :, :], m.kvh[:, :, 0:KVC].bitcast(F32), ALU.subtract)\
               .then_inc(sem["set_lo"], 1)
            dve.wait_ge(sem["fold_done"], 1)
            dve.wait_ge(sem["set_hi"], 7)
            dve.tensor_tensor(m.kvl[:, :, KVC:KVC + RR], C[0][:, :].rearrange("p (k r) -> p k r", r=RR), m.kvh[:, :, KVC:KVC + RR].bitcast(F32), ALU.subtract)\
               .then_inc(sem["set_lo"], 1)
            dve.wait_ge(sem["con_loaded"], 16)
            dve.wait_ge(sem["seg_loaded"], 32)
            dve.tensor_copy(m.segk[:, :], m.segk_i[:, :]).then_inc(sem["dve_step"], steps.next())
            dve.tensor_copy(m.segr[:, :], m.segr_i[:, :]).then_inc(sem["dve_step"], steps.next())
            dve.wait_ge(sem["dve_step"], steps.so_far())
            dve.tensor_scalar(m.keyf[:, :], m.segk[:, :], con[0:GK, C_SHIFT:C_SHIFT + 1], 0.0, ALU.add, ALU.max)\
               .then_inc(sem["dve_step"], steps.next())
            dve.wait_ge(sem["dve_step"], steps.so_far())
            dve.tensor_scalar(m.keyf[:, :], m.keyf[:, :], float(LK - 1), None, ALU.min)\
               .then_inc(sem["dve_step"], steps.next())
            dve.wait_ge(sem["dve_step"], steps.so_far())
            dve.tensor_tensor(m.keyf[:, :], m.keyf[:, :], con[0:GK, C_ROW0:C_ROW0 + NG], ALU.add)\
               .then_inc(sem["dve_step"], steps.next())
            dve.wait_ge(sem["dve_step"], steps.so_far())
            dve.tensor_tensor(m.segk[:, :], con[0:GK, C_MEANROW:C_MEANROW + NG], m.keyf[:, :], ALU.subtract)\
               .then_inc(sem["dve_step"], steps.next())
            dve.wait_ge(sem["dve_step"], steps.so_far())
            dve.scalar_tensor_tensor(m.keyf[:, :], m.segk[:, :], con[0:GK, C_ISMEAN:C_ISMEAN + 1], m.keyf[:, :],
                                          ALU.mult, ALU.add).then_inc(sem["dve_step"], steps.next())
            dve.wait_ge(sem["dve_step"], steps.so_far())
            dve.tensor_copy(m.keyi[:, :], m.keyf[:, :]).then_inc(sem["key_index"], 1)
            key = m.seen[:, :, 0:WIN - 1]
            dve.tensor_tensor(key, m.segr[:, :].unsqueeze(2).to_broadcast([P, NG, WIN - 1]),
                                   con[:, C_WSHIFT:C_WSHIFT + WIN - 1].unsqueeze(1).to_broadcast([P, NG, WIN - 1]), ALU.add)\
               .then_inc(sem["dve_step"], steps.next())
            dve.wait_ge(sem["dve_step"], steps.so_far())
            dve.tensor_scalar(m.hide[:, :, 0:WIN - 1], key, 0.0, NEG, ALU.is_lt, ALU.mult)\
               .then_inc(sem["dve_step"], steps.next())
            dve.wait_ge(sem["dve_step"], steps.so_far())
            dve.tensor_scalar(key, key, float(LK - 1), NEG, ALU.is_gt, ALU.mult)\
               .then_inc(sem["dve_step"], steps.next())
            dve.wait_ge(sem["dve_step"], steps.so_far())
            dve.tensor_tensor(m.hide[:, :, 0:WIN - 1], m.hide[:, :, 0:WIN - 1], key, ALU.add)\
               .then_inc(sem["dve_step"], steps.next())
            dve.wait_ge(sem["dve_step"], steps.so_far())
            dve.tensor_scalar(m.seen[:, :, 0], m.segr[:, :], 0.0, -NEG, ALU.is_lt, ALU.mult)\
               .then_inc(sem["dve_step"], steps.next())
            dve.wait_ge(sem["dve_step"], steps.so_far())
            dve.tensor_scalar(m.seen[:, :, 1], m.segr[:, :], float(LK - 1 + WIN - 2), -NEG, ALU.is_gt, ALU.mult)\
               .then_inc(sem["dve_step"], steps.next())
            dve.wait_ge(sem["dve_step"], steps.so_far())
            dve.tensor_tensor(m.seen[:, :, 0], m.seen[:, :, 0], m.seen[:, :, 1], ALU.add)\
               .then_inc(sem["dve_step"], steps.next())
            dve.wait_ge(sem["dve_step"], steps.so_far())
            dve.tensor_scalar(m.hide[:, :, WIN - 1], m.seen[:, :, 0], NEG, None, ALU.add)\
               .then_inc(sem["dve_step"], steps.next())
            dve.wait_ge(sem["dve_step"], steps.so_far())

            def soften(pr, rows, width, mask, banks, scale, a, full, taken, centered, exp, done):
                for jj in (0, 2):
                    for j in (jj, jj + 1):
                        v = pr[:, j, :].rearrange("p (g k) -> p g k", k=width)
                        dve.wait_ge(sem[full], 4 * a + j + 1)
                        dve.scalar_tensor_tensor(
                            v, banks[j][0:rows, 0:4 * width].rearrange("p (g k) -> p g k", k=width), scale,
                            mask.unsqueeze(1).to_broadcast([rows, 4, width]), ALU.mult, ALU.add).then_inc(sem[taken], 1)
                    for j in (jj, jj + 1):
                        v = pr[:, j, :].rearrange("p (g k) -> p g k", k=width)
                        dve.wait_ge(sem[taken], 4 * a + j + 1)
                        dve.tensor_reduce(m.peak[0:rows, j, :], v, AX.X, ALU.max)\
                           .then_inc(sem["dve_step"], steps.next())
                    dve.wait_ge(sem["dve_step"], steps.so_far())
                    for j in (jj, jj + 1):
                        v = pr[:, j, :].rearrange("p (g k) -> p g k", k=width)
                        dve.tensor_tensor(v, v, m.peak[0:rows, j, :].unsqueeze(2).to_broadcast([rows, 4, width]), ALU.subtract)\
                           .then_inc(sem[centered], 1)
                for jj in (0, 2):
                    for j in (jj, jj + 1):
                        v = pr[:, j, :].rearrange("p (g k) -> p g k", k=width)
                        dve.wait_ge(sem[exp], 4 * a + j + 1)
                        dve.tensor_reduce(m.total[0:rows, j, :], v, AX.X, ALU.add)\
                           .then_inc(sem["dve_step"], steps.next())
                    dve.wait_ge(sem["dve_step"], steps.so_far())
                    dve.reciprocal(m.share[0:rows, jj:jj + 2, :], m.total[0:rows, jj:jj + 2, :])\
                       .then_inc(sem["dve_step"], steps.next())
                    dve.wait_ge(sem["dve_step"], steps.so_far())
                    for j in (jj, jj + 1):
                        v = pr[:, j, :].rearrange("p (g k) -> p g k", k=width)
                        dve.tensor_tensor(v, v, m.share[0:rows, j, :].unsqueeze(2).to_broadcast([rows, 4, width]), ALU.mult)\
                           .then_inc(sem[done], 1)

            def self_dve(i):
                a = i - 1
                soften(m.probs, ST, ST, con[0:ST, C_SMASK:C_SMASK + ST], A, 64 ** -0.5, a,
                       "self_s", "s_taken", "s_centered", "s_exp", "s_probs")
                for u in range(2):
                    dve.wait_ge(sem["self_vt"], 2 * a + u + 1)
                    dve.tensor_copy(m.v_tok[:, 4 * u:4 * u + 4, :],
                                    C[u][0:ST, :].rearrange("p (g f) -> p g f", f=P)).then_inc(sem["vt_evac"], 1)
                for k, ((dst, src), (hi, _)) in enumerate(zip(ao_parts(m.aol, C, a), ao_parts(m.aoh, C, a))):
                    dve.wait_ge(sem["ao_hi"], 3 * a + (3 if k else 1))
                    dve.tensor_tensor(dst, src, hi.bitcast(F32), ALU.subtract).then_inc(sem["ao_lo"], 1)

            self_dve(1)
            with dve.Fori(2, HP + 1) as i:
                steps.loop(i, 2, HP + 1, 10)
                self_dve(i)
            steps.close()

            def out_dve(i):
                for u in range(2):
                    n = 2 * i + u + 1
                    y = half(m.y1[:, i, :], u)
                    dve.wait_ge(sem["out_done"], n)
                    dve.tensor_tensor(y, G[u][:, 0:HT], half(m.xh[:, i, :], u).bitcast(F32), ALU.add)\
                       .then_inc(sem["y1_read"], 1)
                    dve.wait_ge(sem["y1_read"], n)
                    dve.tensor_tensor(y, y, half(m.xl[:, i, :], u).bitcast(F32), ALU.add).then_inc(sem["y1_done"], 1)
                    dve.wait_ge(sem["y1_done"], n)
                    dve.tensor_tensor(half(m.sums[:, 0, :], u), half(m.sums[:, 0, :], u), y, ALU.add)\
                       .then_inc(sem["dve_step"], steps.next())
                    dve.wait_ge(sem["square_done"], n)
                    dve.tensor_tensor(half(m.sums[:, 1, :], u), half(m.sums[:, 1, :], u), m.square[:, u, :], ALU.add)\
                       .then_inc(sem["square_added"], 1)
                dve.wait_ge(sem["dve_step"], steps.so_far())
                dve.wait_ge(sem["square_added"], 2 * i + 2)

            with dve.Fori(0, HP) as i:
                steps.loop(i, 0, HP, 2)
                out_dve(i)
            steps.close()

            def rsqrt_of(r, n):
                inverse_root(r, n)
                newton(r, n)

            def inverse_root(r, n):
                dve.wait_ge(sem["stat_root"], n)
                dve.reciprocal(r, m.root[:, :]).then_inc(sem["dve_step"], steps.next())
                dve.wait_ge(sem["dve_step"], steps.so_far())

            def newton(r, n):
                dve.tensor_tensor(m.tmp[:, :], r, r, ALU.mult).then_inc(sem["dve_step"], steps.next())
                dve.wait_ge(sem["dve_step"], steps.so_far())
                dve.scalar_tensor_tensor(m.tmp[:, :], m.tmp[:, :], -0.5, m.ve[:, :], ALU.mult, ALU.mult)\
                   .then_inc(sem["dve_step"], steps.next())
                dve.wait_ge(sem["dve_step"], steps.so_far())
                dve.scalar_tensor_tensor(r, m.tmp[:, :], 1.5, r, ALU.add, ALU.mult).then_inc(sem["stat_rstd"], 1)
                dve.wait_ge(sem["stat_rstd"], n)

            def take_sums(q, u, b0, b1):
                dve.wait_ge(sem["stat_sums"], q)
                dve.tensor_copy(m.mean[:, u, :], b0[:, 0:HT]).then_inc(sem["dve_step"], steps.next())
                dve.wait_ge(sem["dve_step"], steps.so_far())
                dve.tensor_tensor(m.tmp[:, :], m.mean[:, u, :], m.mean[:, u, :], ALU.mult)\
                   .then_inc(sem["dve_step"], steps.next())
                dve.wait_ge(sem["dve_step"], steps.so_far())
                dve.tensor_tensor(m.ve[:, :], b1[:, 0:HT], m.tmp[:, :], ALU.subtract).then_inc(sem["stat_taken"], 1)

            def spread(n, u):
                variance(n, u)
                rsqrt_of(m.rstd[:, u, :], n)

            def variance(n, u):
                dve.wait_ge(sem["stat_taken"], (1, 2, 3, 0, 4, 0, 5, 6)[n - 1])
                dve.tensor_scalar(m.ve[:, :], m.ve[:, :], 0.0, EPS_LN, ALU.max, ALU.add).then_inc(sem["stat_var"], 1)
                if n < 7:
                    dve.memset(half(m.sums[:, 0, :], u), 0.0).then_inc(sem["dve_step"], steps.next())
                    dve.memset(half(m.sums[:, 1, :], u), 0.0).then_inc(sem["dve_step"], steps.next())
                    dve.wait_ge(sem["dve_step"], steps.so_far())
                dve.wait_ge(sem["stat_var"], n)

            def statistics(q, n, u, b0, b1):
                take_sums(q, u, b0, b1)
                spread(n, u)

            def second_norm(n, u):
                second_variance(n, u)
                rsqrt_of(m.rms2[:, u, :], n)

            def second_variance(n, u):
                dve.scalar_tensor_tensor(m.ve[:, :], m.ve[:, :], -EPS_LN, m.rstd[:, u, :], ALU.add, ALU.mult)\
                   .then_inc(sem["dve_step"], steps.next())
                dve.wait_ge(sem["dve_step"], steps.so_far())
                dve.tensor_tensor(m.ve[:, :], m.ve[:, :], m.rstd[:, u, :], ALU.mult)\
                   .then_inc(sem["dve_step"], steps.next())
                dve.wait_ge(sem["dve_step"], steps.so_far())
                dve.tensor_scalar(m.ve[:, :], m.ve[:, :], EPS_RMS, None, ALU.add).then_inc(sem["stat_var"], 1)
                dve.wait_ge(sem["stat_var"], n)

            def norm(y, u, name):
                dve.tensor_tensor(y, y, m.mean[:, u, :], ALU.subtract).then_inc(sem["dve_step"], steps.next())
                dve.wait_ge(sem["dve_step"], steps.so_far())
                dve.tensor_tensor(y, y, m.rstd[:, u, :], ALU.mult).then_inc(sem[name], 1)

            def kv_tile(b, ti):
                first = isinstance(b, int) and b == 0
                n, s, bk = KT * b + ti, ti % 2, G[ti % 2]
                kc, ks = C_KCOS + ti * RR, C_KSIN + ti * RR
                dve.wait_ge(sem["kv_copied"], n + 1)
                if not (first and ti < 2):
                    dve.wait_ge(sem["row_ready"], n - 1)
                dve.tensor_tensor(m.rot[s][:, 0, :], bk[:, KVC:KVC + RR], con[:, kc:kc + RR], ALU.mult)\
                   .then_inc(sem["dve_step"], steps.next())
                dve.tensor_tensor(m.rot[s][:, 1, 0:32], bk[:, KVC + 32:KVC + 64], con[:, ks:ks + 32], ALU.mult)\
                   .then_inc(sem["dve_step"], steps.next())
                dve.tensor_tensor(m.rot[s][:, 1, 32:64], bk[:, KVC:KVC + 32], con[:, ks + 32:ks + 64], ALU.mult)\
                   .then_inc(sem["dve_step"], steps.next())
                if ti == 0:
                    dve.tensor_copy(m.kv_sum[:, b, :], bk[:, 0:KVC]).then_inc(sem["kv_read"], 1)
                else:
                    dve.wait_ge(sem["kv_read"], n)
                    dve.tensor_tensor(m.kv_sum[:, b, :], bk[:, 0:KVC], m.kv_sum[:, b, :], ALU.add)\
                       .then_inc(sem["kv_read"], 1)
                dve.wait_ge(sem["dve_step"], steps.so_far())
                if not (first and ti < 2):
                    dve.wait_ge(sem[f"row_stored_{s}"], 16 * (KT // 2 * b + ti // 2))
                dve.tensor_tensor(m.row[s][:, KVC:ROW].rearrange("p (c r) -> p c r", r=RR), m.rot[s][:, 0, :].unsqueeze(1).to_broadcast([P, 2, RR]), m.rot[s][:, 1, :].unsqueeze(1).to_broadcast([P, 2, RR]), ALU.add)\
                   .then_inc(sem["row_ready"], 1)

            def x1_norm(b):
                for u in range(2):
                    norm(half(m.y1[:, b, :], u), u, "ln1_z")

            def x1_low(b):
                for u in range(2):
                    dve.wait_ge(sem["ln1_hi"], 2 * b + u + 1)
                    dve.tensor_tensor(half(m.x1l[:, b, :], u), half(m.y1[:, b, :], u),
                                      half(m.x1h[:, b, :], u).bitcast(F32), ALU.subtract).then_inc(sem["ln1_lo"], 1)

            take_sums(1, 0, A[0], A[1])
            kv_tile(0, 0)
            spread(1, 0)
            kv_tile(0, 1)
            take_sums(2, 1, A[2], A[3])
            kv_tile(0, 2)
            spread(2, 1)
            for ti in range(3, KT):
                kv_tile(0, ti)
            x1_norm(0)
            x1_low(0)

            with dve.Fori(1, NB) as b:
                steps.loop(b, 1, NB, 2 + 3 * KT)
                x1_norm(b)
                for ti in range(KT):
                    kv_tile(b, ti)
                    if ti == 2:
                        x1_low(b)
            steps.close()
            dve.memset(m.mean_row[:, KVC:ROW], 0.0).then_inc(sem["mean_ready"], 1)

            for k in range(3):
                for u in range(2):
                    dve.wait_ge(sem["qc_hi"], 2 * k + u + 1)
                    dve.tensor_tensor(m.qcl[u][:, k, :], G[u][:, 0:HT], m.qch[u][:, k, :].bitcast(F32), ALU.subtract)\
                       .then_inc(sem["qc_lo"], 1)

            for hf in range(2):
                p_pair, p_win, p_out = HALF[hf]
                q = m.qn[p_pair]

                def pair_dve(hp, take=False):
                    n = HP * hf + hp
                    for u in range(2):
                        dve.wait_ge(sem["qn_hi"], 2 * n + u + 1)
                        if not (isinstance(hp, int) and hp == 0):
                            dve.wait_ge(sem["ukB_done"], 2 * n)
                        dve.tensor_tensor(q["l"][:, u, :], G[u][:, 0:HT], q["h"][:, u, :].bitcast(F32), ALU.subtract)\
                           .then_inc(sem["qn_lo"], 1)
                    if take:
                        take_sums(3, 0, C[0], C[1])
                    dve.wait_ge(sem["qr_raw"], n + 1)

                    def turned(dst, src, at):
                        return dve.tensor_tensor(dst.rearrange("p (b s) -> p b s", s=NS),
                                                 src.rearrange("p (b s) -> p b s", s=NS),
                                                 con[:, at:at + NS].unsqueeze(1).to_broadcast([P, NB // 2, NS]), ALU.mult)

                    turned(q["c"][:, :], q["r"][:, :], C_QCOS).then_inc(sem["dve_step"], steps.next())
                    for c in range(2):
                        dve.wait_ge(sem["ukB_done"], 2 * n + c + 1)
                        dve.tensor_copy(m.qa[:, c, :, 2 * hp + 1, :], grouped(C[c][:, 0:HT])).then_inc(sem["qa_dve"], 1)
                    dve.wait_ge(sem["perm_done"], n + 1)
                    turned(q["s"][:, :], A[1][:, 0:HT], C_QSIN).then_inc(sem["dve_step"], steps.next())
                    dve.wait_ge(sem["dve_step"], steps.so_far())
                    for e in range(2):
                        r = slice(64 * e, 64 * e + 64)
                        dve.tensor_tensor(m.qr[r, 0, :, 2 * hp + e, :], grouped(q["c"][r, :]), grouped(q["s"][r, :]), ALU.add)\
                           .then_inc(sem["q_rot"], 1)
                    dve.wait_ge(sem["q_rot"], 2 * n + 2)

                if hf == 0:
                    with dve.Fori(0, HP) as hp:
                        steps.loop(hp, 0, HP, 2)
                        pair_dve(hp)
                    steps.close()
                else:
                    pair_dve(0, True)
                    variance(3, 0)
                    pair_dve(1)
                    inverse_root(m.rstd[:, 0, :], 3)
                    pair_dve(2)
                    newton(m.rstd[:, 0, :], 3)
                    pair_dve(3)
                    second_variance(4, 0)
                    pair_dve(4)
                    inverse_root(m.rms2[:, 0, :], 4)
                    pair_dve(5)
                    newton(m.rms2[:, 0, :], 4)
                    norm(m.y2[0][:, 0, :], 0, "x2_done")
                    for hp in (6, 7):
                        pair_dve(hp)
                        for kc in ((1, 2, 3, 4), (5, 6, 7))[hp - 6]:
                            norm(m.y2[0][:, kc, :], 0, "x2_done")

                w = m.sp[p_win]
                scale = float(np.float32(1.0) / np.sqrt(np.float32(P + RR)))
                for v in range(1, UH + 4):
                    if v < UH + 1:
                        u, n = v - 1, UH * hf + v - 1
                        pr, st = w["pr"][u % 2], w["st"][u % 2]
                        dve.wait_ge(sem["win_s"], n + 1)
                        dve.wait_ge(sem["win_mask"], n + 1)
                        if positive(n - 1):
                            dve.wait_ge(sem["win_pt"], n - 1)
                        dve.scalar_tensor_tensor(pr[:, :, :], A[u % 2][:, 0:UG * GK].rearrange("p (g k) -> p g k", k=GK),
                                                 scale, w["mk"][u % 2][:, :, :], ALU.mult, ALU.add)\
                           .then_inc(sem["win_taken"], 1)
                        dve.wait_ge(sem["win_taken"], n + 1)
                        dve.tensor_reduce(st[:, 0, :], pr[:, :, :], AX.X, ALU.max)\
                           .then_inc(sem["dve_step"], steps.next())
                        dve.wait_ge(sem["dve_step"], steps.so_far())
                        dve.tensor_tensor(pr[:, :, :], pr[:, :, :], st[:, 0, :].unsqueeze(2).to_broadcast([P, UG, GK]), ALU.subtract)\
                           .then_inc(sem["win_centered"], 1)
                    if v >= 4:
                        u, n = v - 4, UH * hf + v - 4
                        for c, ((dst, src), (hi, _)) in enumerate(zip(lat_parts(m.latl, C, u), lat_parts(m.lath, C, u))):
                            dve.wait_ge(sem["lat_hi"], 2 * n + 2)
                            dve.tensor_tensor(dst, src, hi.bitcast(F32), ALU.subtract).then_inc(sem["lat_lo"], 1)
                    if v < UH + 1:
                        u, n = v - 1, UH * hf + v - 1
                        pr, st = w["pr"][u % 2], w["st"][u % 2]
                        dve.wait_ge(sem["win_exp"], n + 1)
                        dve.tensor_reduce(st[:, 1, :], pr[:, :, :], AX.X, ALU.add)\
                           .then_inc(sem["dve_step"], steps.next())
                        dve.wait_ge(sem["dve_step"], steps.so_far())
                        dve.reciprocal(st[:, 2, :], st[:, 1, :]).then_inc(sem["dve_step"], steps.next())
                        dve.wait_ge(sem["dve_step"], steps.so_far())
                        dve.tensor_tensor(pr[:, :, :], pr[:, :, :], st[:, 2, :].unsqueeze(2).to_broadcast([P, UG, GK]), ALU.mult)\
                           .then_inc(sem["win_probs"], 1)

                for h in range(H):
                    dve.wait_ge(sem["vo_hi"], H * hf + h + 1)
                    dve.tensor_tensor(m.latl[:, 0, :, h, :], grouped(A[h % 4][:, 0:HT]), m.lath[:, 0, :, h, :].bitcast(F32), ALU.subtract)\
                       .then_inc(sem["vo_lo"], 1)

                with dve.Fori(0, HP // 2) as i:
                    steps.loop(i, 0, HP // 2, 2)
                    for k in range(2):
                        n = HP * hf + 2 * i + k + 1
                        dve.wait_ge(sem["wo_done"], n)
                        dve.wait_ge(sem[f"x1_back_{k}"], 16 * (HP // 2 * hf + i + 1))
                        y = m.y2[hf][:, 2 * i + k, :]
                        dve.tensor_tensor(y, G[k][:, 0:HT], m.x1t[p_out][k][:, :], ALU.add).then_inc(sem["y2_done"], 1)
                        dve.wait_ge(sem["y2_done"], n)
                        dve.tensor_tensor(half(m.sums[:, 0, :], hf), half(m.sums[:, 0, :], hf), y, ALU.add)\
                           .then_inc(sem["dve_step"], steps.next())
                        dve.wait_ge(sem["dve_step"], steps.so_far())
                        dve.wait_ge(sem["square_done"], 2 * HP + n)
                        dve.tensor_tensor(half(m.sums[:, 1, :], hf), half(m.sums[:, 1, :], hf), m.square[:, k, :], ALU.add)\
                           .then_inc(sem["square_added"], 1)
                        dve.wait_ge(sem["square_added"], 2 * HP + n)
                steps.close()

            dve.wait_ge(sem["x2_done"], KC)

            def xa_dve(first, stop):
                for n in range(first, stop + 1):
                    if n < stop:
                        u, kc = n // KC, n % KC
                        y = m.y2[u][:, kc, :]
                        if u:
                            norm(y, 1, "x2_done")
                            dve.wait_ge(sem["x2_done"], KC + kc + 1)
                        if n >= 2:
                            dve.wait_ge(sem["in_hi"], n - 1)
                            dve.wait_ge(sem["in_low_odd" if n % 2 else "in_low_even"], n // 2)
                        dve.scalar_tensor_tensor(m.xa32[n % 2][:, :], y, con[:, C_LN1 + kc:C_LN1 + kc + 1],
                                                 m.rms2[:, u, :], ALU.mult, ALU.mult).then_inc(sem["in_ready"], 1)
                    if n > first and n % 2:
                        u, kc = (n - 1) // KC, (n - 1) % KC
                        dve.wait_ge(sem["in_hi"], n)
                        dve.tensor_tensor(half(m.xal[:, kc, :], u), m.xa32[(n - 1) % 2][:, :],
                                          half(m.xah[:, kc, :], u).bitcast(F32), ALU.subtract)\
                           .then_inc(sem["in_low_even"], 1)

            xa_dve(0, KC)
            statistics(4, 5, 1, A[0], A[1])
            second_norm(6, 1)
            xa_dve(KC, 2 * KC)

            def ffn_dve(i):
                soften(m.fprobs, NS, NS, con[0:NS, C_FMASK:C_FMASK + NS], A, 64 ** -0.5, i - 1,
                       "f_s", "f_taken", "f_centered", "f_exp", "f_probs")

            for b in range(NB // 2, NB):
                dve.wait_ge(sem["z_done"], b + 1)
                dve.tensor_copy(m.z_tok[:, b, :], G[b % 2][0:NS, 0:H * RA]).then_inc(sem["z_evac"], 1)
            ffn_dve(1)
            with dve.Fori(2, HP + 1) as i:
                steps.loop(i, 2, HP + 1, 10)
                ffn_dve(i)
            steps.close()

            dve.memset(m.ustk[:, :].bitcast(F32), 0.0).then_inc(sem["u_zero"], 1)
            for n in range(2 * KC + 1):
                if n < 2 * KC:
                    u, kc = n // KC, n % KC
                    y = m.y2[u][:, kc, :]
                    dve.wait_ge(sem["in_hi"], 2 * KC + n - 1)
                    dve.wait_ge(sem["in_low_odd" if n % 2 else "in_low_even"], KC + n // 2)
                    dve.scalar_tensor_tensor(m.xa32[n % 2][:, :], y, con[:, C_LN2 + kc:C_LN2 + kc + 1],
                                             m.rms2[:, u, :], ALU.mult, ALU.mult).then_inc(sem["in_ready"], 1)
                if n % 2:
                    u, kc = (n - 1) // KC, (n - 1) % KC
                    dve.wait_ge(sem["in_hi"], 2 * KC + n)
                    dve.tensor_tensor(half(m.hl[:, kc, :], u), m.xa32[(n - 1) % 2][:, :], half(m.hh[:, kc, :], u).bitcast(F32), ALU.subtract)\
                       .then_inc(sem["in_low_even"], 1)
            dve.wait_ge(sem["in_ready"], 4 * KC)
            for u in range(2):
                dve.wait_ge(sem["m_tanh"], u + 1)
                dve.wait_ge(sem["ha_done"], u + 1)
                dve.scalar_tensor_tensor(half(m.u_raw[:, :], u), half(m.tanh_m[:, :], u), 0.1, G[u][0:RA, 0:HT],
                                         ALU.mult, ALU.mult).then_inc(sem["u_ready"], 1)
            for u in range(2):
                dve.wait_ge(sem["u_hi"], 2 * u + 2)
                dve.tensor_tensor(half(m.ustk[32:32 + RA, :], u), half(m.u_raw[:, :], u), half(m.ustk[0:RA, :], u).bitcast(F32), ALU.subtract)\
                   .then_inc(sem["u_lo"], 1)
            def up_dve(fb, fm):
                f = FM * fb + fm
                dve.wait_ge(sem["b_hi"], f + 1)
                dve.tensor_tensor(m.bstk[64:64 + RA, :], m.b_raw[64:64 + RA, bass.ds(f * P, P)] if not isinstance(f, int)
                    else m.b_raw[64:64 + RA, f * P:(f + 1) * P], m.bstk[64:64 + RA, :].bitcast(F32), ALU.subtract)\
                   .then_inc(sem["b_lo"], 1)
                for u in range(2):
                    dve.wait_ge(sem["silu_done"], 2 * f + u + 1)
                    dve.wait_ge(sem["ff_up"], 2 * f + u + 1)
                    dve.tensor_tensor(m.act32[u][:, :], m.gate[u][:, :], A[u][:, 0:HT], ALU.mult)\
                       .then_inc(sem["ff_prod"], 1)
                for u in range(2):
                    dve.wait_ge(sem["ff_hi"], 2 * f + u + 1)
                    dve.tensor_tensor(half(m.ffl[:, fm, :], u), m.act32[u][:, :], half(m.ffh[:, fm, :], u).bitcast(F32), ALU.subtract)\
                       .then_inc(sem["ff_lo"], 1)
                dve.wait_ge(sem["ff_lo"], 2 * f + 2)

            def down_dve(fb, c, first, last):
                n = FM * fb + c
                for u in range(2):
                    y = m.y2[u][:, c, :]
                    dve.wait_ge(sem["down_done"], 2 * n + u + 1)
                    dve.scalar_tensor_tensor(y, y, 2.0 if first else 1.0, C[u][:, 0:HT], ALU.mult, ALU.add)\
                       .then_inc(sem["down_added"], 1)
                    if last:
                        dve.wait_ge(sem["down_added"], 2 * n + u + 1)
                        dve.tensor_tensor(half(m.sums[:, 0, :], u), half(m.sums[:, 0, :], u), y, ALU.add)\
                           .then_inc(sem["dve_step"], steps.next())
                        dve.wait_ge(sem["dve_step"], steps.so_far())
                        dve.wait_ge(sem["square_done"], 4 * HP + 2 * c + u + 1)
                        dve.tensor_tensor(half(m.sums[:, 1, :], u), half(m.sums[:, 1, :], u), m.square[:, u, :], ALU.add)\
                           .then_inc(sem["square_added"], 1)
                        dve.wait_ge(sem["square_added"], 4 * HP + 2 * c + u + 1)
                dve.wait_ge(sem["down_added"], 2 * n + 2)

            with dve.Fori(0, FM) as fm:
                up_dve(0, fm)
            with dve.Fori(0, KC) as c:
                down_dve(0, c, True, False)
            with dve.Fori(1, FB - 1) as fb:
                with dve.Fori(0, FM) as fm:
                    up_dve(fb, fm)
                with dve.Fori(0, KC) as c:
                    down_dve(fb, c, False, False)
            with dve.Fori(0, FM) as fm:
                up_dve(FB - 1, fm)
            with dve.Fori(0, KC) as c:
                steps.loop(c, 0, KC, 2)
                down_dve(FB - 1, c, False, True)
            steps.close()
            statistics(5, 7, 0, A[0], A[1])
            statistics(6, 8, 1, A[2], A[3])
            for kc in range(KC):
                norm(m.y2[1][:, kc, :], 1, "final_1")
            for kc in range(POOL_LAST, KC):
                norm(m.y2[0][:, kc, :], 0, "final_1")

        @block.tensor
        def _(pe):
            def three(dst, w, xh, xl, first, last):
                pe.matmul(dst, w[0], xh, start=first, stop=False)
                pe.matmul(dst, w[0], xl, start=False, stop=False)
                return pe.matmul(dst, w[1], xh, start=False, stop=last)

            def tile(k, j):
                return whi[k % 2][:, j, :], wlo[k % 2][:, j, :]

            def stripe(k, i=0, per=0, part=0):
                pe.wait_ge(sem["w_lo"], 2 * k + 2 * per * i + part + 1)

            def chunks(dst, k, i, per, xh, xl, u):
                for kc in range(KC):
                    if u == 0 and kc == KC // 2:
                        stripe(k, i, per, 1)
                    ins = three(dst, tile(k, kc), half(xh[:, kc, :], u), half(xl[:, kc, :], u), kc == 0, kc == KC - 1)
                return ins

            x_h, x_l = m.xh, m.xl
            q_s, k_s, v_s = m.qkv

            def self_product(j, i, done, evac, n_evac):
                stripe(S_SELF + j, i, 4)
                for u in range(2):
                    if evac:
                        if positive(n_evac[u]):
                            pe.wait_ge(sem[evac[u]], n_evac[u])
                    for kc in range(KC):
                        if isinstance(i, int) and i == 0 and j == 0:
                            pe.wait_ge(sem["set_lo"], kc + 1)
                        if u == 0 and kc == KC // 2:
                            stripe(S_SELF + j, i, 4, 1)
                        ins = three(G[u][:, 0:HT], tile(j, kc), half(x_h[:, kc, :], u), half(x_l[:, kc, :], u),
                                    kc == 0, kc == KC - 1)
                    ins.then_inc(sem[done], 1)

            def self_pe(i, product, attn):
                a = i - 1
                if attn:
                    pe.wait_ge(sem["q_evac"], 2 * a + 2)
                    pe.wait_ge(sem["k_evac"], 2 * a + 2)
                    for j in range(4):
                        e, gh = j // 2, j % 2
                        if not (isinstance(a, int) and a == 0):
                            pe.wait_ge(sem["pt_evac"], 4 * a - 3 + j)
                        for g4 in range(4):
                            n0 = self_group(4 * gh + g4)
                            rows = slice(64 * e, 64 * e + 64)
                            ins = pe.matmul(A[j][0:ST, g4 * ST:(g4 + 1) * ST], q_s[rows, n0:n0 + SN, :].rearrange("p n b -> p (n b)"),
                                            k_s[rows, n0:n0 + SN, :].rearrange("p n b -> p (n b)"), start=True, stop=True)
                        ins.then_inc(sem["self_s"], 1)
                if product:
                    self_product(0, i, "self_q", ("wa_done", "v_evac"), (2 * i, 2 * i))
                if attn:
                    pe.wait_ge(sem["v_evac"], 2 * a + 2)
                    for u in range(2):
                        if not (isinstance(a, int) and a == 0):
                            pe.wait_ge(sem["ao_lo"], 3 * a)
                        else:
                            pe.wait_ge(sem["set_lo"], KC + 3)
                        for g4 in range(4):
                            n0 = self_group(4 * u + g4)
                            ins = pe.transpose(C[u][0:ST, g4 * P:(g4 + 1) * P], v_s[:, n0:n0 + SN, :].rearrange("p n b -> p (n b)"), ident)
                        ins.then_inc(sem["self_vt"], 1)
                if product:
                    self_product(1, i, "self_k", ("q_evac", "q_evac"), (2 * i + 1, 2 * i + 2))
                if attn:
                    for j in range(4):
                        pe.wait_ge(sem["s_probs"], 4 * a + j + 1)
                        for g4 in range(4):
                            ins = pe.transpose(A[j][0:ST, g4 * ST:(g4 + 1) * ST],
                                               m.probs[:, j, g4 * ST:(g4 + 1) * ST], con[0:ST, C_IDENT:C_IDENT + ST])
                        ins.then_inc(sem["self_pt"], 1)
                if product:
                    self_product(2, i, "self_v", ("k_evac", "k_evac"), (2 * i + 1, 2 * i + 2))
                if attn:
                    pe.wait_ge(sem["vt_evac"], 2 * a + 2)
                    for gh in range(2):
                        for e in range(2):
                            j = 2 * e + gh
                            pe.wait_ge(sem["pt_evac"], 4 * a + j + 1)
                            for g4 in range(4):
                                ins = pe.matmul(C[gh][64 * e:64 * e + 64, g4 * ST:(g4 + 1) * ST],
                                                m.v_tok[:, 4 * gh + g4, 64 * e:64 * e + 64],
                                                m.probs_t[:, j, g4 * ST:(g4 + 1) * ST], start=True, stop=True)
                    ins.then_inc(sem["self_pv"], 1)
                if product:
                    stripe(S_SELF + 3, i, 4, 1)
                    pe.wait_ge(sem["set_lo"], KC + 1)
                    pe.wait_ge(sem["v_evac"], 2 * i + 1)
                    for kc in range(KC):
                        ins = pe.matmul(G[0][:, 0:RA], m.w32[:, kc, :], m.a_raw[:, kc, :], start=(kc == 0),
                                        stop=(kc == KC - 1))
                    ins.then_inc(sem["self_wo"], 1)

            self_pe(0, True, False)
            pe.wait_ge(sem["con_loaded"], 16)
            pe.wait_ge(sem["aux_loaded"], 64)
            for kc in range(KC):
                for c in range(2):
                    ins = pe.matmul(C[0][:, kc * RR:(kc + 1) * RR], m.kvc_t[:, c, kc * P:(kc + 1) * P],
                                    m.kr_raw[:, c, :], start=(c == 0), stop=(c == 1))
            ins.then_inc(sem["fold_done"], 1)
            self_pe(1, True, True)
            with pe.Fori(2, HP) as i:
                self_pe(i, True, True)
            self_pe(HP, False, True)

            pe.wait_ge(sem["ao_lo"], 3 * HP)
            pe.wait_ge(sem["wa_done"], 2 * HP)
            aoh, aol = m.aoh.rearrange("p k b s -> p k (b s)"), m.aol.rearrange("p k b s -> p k (b s)")

            def out_pe(i):
                first = isinstance(i, int) and i == 0
                stripe(S_OUT, i, 2)
                for u in range(2):
                    if not first:
                        pe.wait_ge(sem["y1_read"], 2 * i + u - 1)
                    chunks(G[u][:, 0:HT], S_OUT, i, 2, aoh, aol, u).then_inc(sem["out_done"], 1)
                stripe(S_OUT + 1, i, 2, 1)
                if first:
                    pe.wait_ge(sem["pt_evac"], 4 * HP)
                else:
                    pe.wait_ge(sem["g_evac"], i)
                for ec in range(KC):
                    ins = pe.matmul(A[3][:, ec * 2 * RA:(ec + 1) * 2 * RA], m.w32[:, ec, :], m.wa[:, i, :],
                                    start=True, stop=True)
                ins.then_inc(sem["wv_done"], 1)

            out_pe(0)
            with pe.Fori(1, HP) as i:
                out_pe(i)

            def sum_up(u, b0, b1):
                pe.matmul(b0[:, 0:HT], ones, half(m.sums[:, 0, :], u), start=True, stop=True)
                pe.matmul(b1[:, 0:HT], ones, half(m.sums[:, 1, :], u), start=True, stop=True)\
                  .then_inc(sem["stat_sums"], 1)

            pe.wait_ge(sem["set_lo"], KC + 3)

            def kv_pe(b):
                for ti in range(KT):
                    k, n = S_KV + ti, KT * b + ti
                    stripe(k, b, KT)
                    if isinstance(b, int) and b == 0 and ti < 2:
                        pe.wait_ge(sem["y1_read"], 2 * HP - 1 + ti)
                    else:
                        pe.wait_ge(sem["kv_copied"], n - 1)
                        pe.wait_ge(sem["kv_read"], n - 1)
                    for kc in range(KC):
                        if kc == KC // 2:
                            stripe(k, b, KT, 1)
                        ins = three(G[ti % 2][:, 0:KVC + RR], tile(k, kc), m.kvh[:, kc, :], m.kvl[:, kc, :],
                                    kc == 0, kc == KC - 1)
                    ins.then_inc(sem["kv_done"], 1)
                    if isinstance(b, int) and b == 0 and ti == 0:
                        pe.wait_ge(sem["g_evac"], HP)
                        pe.wait_ge(sem["square_added"], 2 * HP)
                        sum_up(0, A[0], A[1])
                        sum_up(1, A[2], A[3])

            kv_pe(0)
            with pe.Fori(1, NB) as b:
                kv_pe(b)
            pe.wait_ge(sem["kv_copied"], N_KV)
            pe.wait_ge(sem["kv_read"], N_KV)
            for b in range(NB):
                ins = pe.matmul(G[0][0:NB, 0:KVC], con[:, C_BATCH + NB * b:C_BATCH + NB * (b + 1)], m.kv_sum[:, b, :],
                                start=(b == 0), stop=(b == NB - 1))
            ins.then_inc(sem["mean_done"], 1)

            for k in range(3):
                stripe(S_DQ + k)
                for u in range(2):
                    n = 2 * k + u
                    if k == 0:
                        pe.wait_ge(sem["ln1_lo"], 2 * KC)
                        pe.wait_ge(sem["mean_ready"], 2 - u)
                    if positive(n - 1):
                        pe.wait_ge(sem["qc_lo"], n - 1)
                    chunks(G[u][:, 0:HT], S_DQ + k, 0, 0, m.x1h, m.x1l, u).then_inc(sem["dq_done"], 1)
            pe.wait_ge(sem["qc_lo"], 6)

            for hf in range(2):
                p_pair, p_win, p_out = HALF[hf]
                s0 = S_HALF + hf * N_HALF
                q = m.qn[p_pair]
                if hf:
                    pe.wait_ge(sem["lat_lo"], 2 * UH)
                    pe.wait_ge(sem["y2_done"], HP)

                def pair_pe(hp):
                    n = HP * hf + hp
                    later = not (isinstance(n, int) and n == 0)
                    stripe(s0, hp, 2)
                    for u in range(2):
                        if u:
                            stripe(s0, hp, 2, 1)
                        if later:
                            pe.wait_ge(sem["qn_lo"], 2 * n)
                        for c in range(3):
                            ins = three(G[u][:, 0:HT], tile(s0, 3 * u + c), m.qch[hf][:, c, :], m.qcl[hf][:, c, :],
                                        c == 0, c == 2)
                        ins.then_inc(sem["uq_done"], 1)
                    if hf and isinstance(hp, int):
                        pe.wait_ge(sem["square_added"], 3 * HP)
                        sum_up(0, C[0], C[1])
                    if later:
                        pe.wait_ge(sem["qr_raw"], n)
                    for c in range(2):
                        ins = three(A[0][:, 0:HT], tile(s0, 6 + c), m.qch[hf][:, c, :], m.qcl[hf][:, c, :], c == 0, False)
                    ins.then_inc(sem["qr_half"], 1)
                    stripe(s0 + 1, hp, 2)
                    three(A[0][:, 0:HT], tile(s0 + 1, 0), m.qch[hf][:, 2, :], m.qcl[hf][:, 2, :], False, True)\
                        .then_inc(sem["qr_done"], 1)
                    for e, banks, done, evac in ((0, A[2:4], "ukA_done", "qa_act"), (1, C, "ukB_done", "qa_dve")):
                        if e:
                            stripe(s0 + 1, hp, 2, 1)
                        pe.wait_ge(sem["qn_lo"], 2 * n + e + 1)
                        if later:
                            pe.wait_ge(sem[evac], 2 * n)
                        if hf and e and isinstance(hp, int):
                            pe.wait_ge(sem["stat_taken"], 3)
                        for c in range(2):
                            three(banks[c][:, 0:HT], tile(s0 + 1, 1 + 2 * e + c), q["h"][:, e, :], q["l"][:, e, :],
                                  True, True).then_inc(sem[done], 1)
                    pe.wait_ge(sem["qr_raw"], n + 1)
                    if later:
                        pe.wait_ge(sem["q_rot"], 2 * n)
                    pe.matmul(A[1][:, 0:HT], con[:, C_PERM:C_PERM + P], q["r"][:, :], start=True, stop=True)\
                      .then_inc(sem["perm_done"], 1)

                pair_pe(0)
                with pe.Fori(1, HP) as hp:
                    pair_pe(hp)

                n = HP * (hf + 1)
                for name, count in (("qa_act", 2 * n), ("qa_dve", 2 * n), ("q_rot", 2 * n), ("qr_zero", 2 * hf + 2), ("qn_lo", 2 * n)):
                    pe.wait_ge(sem[name], count)
                w = m.sp[p_win]
                for v in range(UH + 3):
                    if v < UH:
                        u, n = v, UH * hf + v
                        if positive(n - 1):
                            pe.wait_ge(sem["wt_evac"], n - 1)
                        for gi in range(UG):
                            r = (UG * u + gi) % RING
                            pe.wait_ge(sem[f"gathered_{r}"], 16 * (NG // 2 // RING * hf + (UG * u + gi) // RING + 1))
                            for c in range(3):
                                at = (3 * gi + c) * GK
                                ins = pe.transpose(G[u % 2][:, at:at + GK], w["win"][r][:, c * P:(c + 1) * P],
                                                   con[0:GK, C_IDENT:C_IDENT + GK])
                        ins.then_inc(sem["wt_done"], 1)
                    if 1 <= v < UH + 1:
                        u, n = v - 1, UH * hf + v - 1
                        pe.wait_ge(sem["wt_evac"], n + 1)
                        if positive(n - 1):
                            pe.wait_ge(sem["win_taken"], n - 1)
                        for gi in range(UG):
                            for c, src in enumerate((m.qa[:, 0], m.qa[:, 1], m.qr[:, 0])):
                                src = src[:, UG * u + gi, :, :].rearrange("p h q -> p (h q)")
                                ins = pe.matmul(A[u % 2][:, gi * GK:(gi + 1) * GK], src, w["wt"][u % 2][:, 3 * gi + c, :],
                                                start=(c == 0), stop=(c == 2))
                        ins.then_inc(sem["win_s"], 1)
                    if 2 <= v < UH + 2:
                        u, n = v - 2, UH * hf + v - 2
                        pe.wait_ge(sem["win_probs"], n + 1)
                        if positive(n - 1):
                            pe.wait_ge(sem["win_pt_evac"], n - 1)
                        for gi in range(UG):
                            ins = pe.transpose(A[2 + u % 2][0:GK, gi * P:(gi + 1) * P], w["pr"][u % 2][:, gi, :], ident)
                        ins.then_inc(sem["win_pt"], 1)
                    if v >= 3:
                        u, n = v - 3, UH * hf + v - 3
                        pe.wait_ge(sem["win_pt_evac"], n + 1)
                        if positive(2 * (n - 1)):
                            pe.wait_ge(sem["lat_lo"], 2 * (n - 1))
                        for gi in range(UG):
                            for c in range(2):
                                at = (2 * gi + c) * P
                                ins = pe.matmul(C[u % 2][:, at:at + P],
                                                w["win"][(UG * u + gi) % RING][:, c * P:(c + 1) * P],
                                                w["pt"][u % 2][:, gi, :], start=True, stop=True)
                        ins.then_inc(sem["win_lat"], 1)

                pe.wait_ge(sem["lat_lo"], 2 * UH * (hf + 1))
                pe.wait_ge(sem["wt_evac"], UH * (hf + 1))
                pe.wait_ge(sem["win_taken"], UH * (hf + 1))
                pe.wait_ge(sem["win_pt_evac"], UH * (hf + 1))
                for i in range(N_UV):
                    k = s0 + N_PAIR + i
                    stripe(k)
                    for h in range(4 * i, 4 * i + 4):
                        if h % 4 == 2:
                            stripe(k, 0, 0, 1)
                        if h >= 4:
                            pe.wait_ge(sem["vo_lo"], H * hf + h - 3)
                        for c in range(2):
                            ins = three(A[h % 4][:, 0:HT], tile(k, 2 * (h % 4) + c), m.lath[:, c, :, h, :], m.latl[:, c, :, h, :],
                                        c == 0, c == 1)
                        ins.then_inc(sem["uv_done"], 1)

                def wo_pe(i):
                    first = isinstance(i, int) and i == 0
                    for k in range(2):
                        n = HP * hf + 2 * i + k
                        if first and k == 0:
                            pe.wait_ge(sem["vo_lo"], H * (hf + 1))
                        if not first:
                            pe.wait_ge(sem["y2_done"], n - 1)
                        for kk in range(2):
                            s = s0 + N_PAIR + N_UV + 2 * k + kk
                            stripe(s, i, 4)
                            for c in range(KC):
                                h = KC * kk + c
                                if c == KC // 2:
                                    stripe(s, i, 4, 1)
                                ins = three(G[k][:, 0:HT], tile(s, c), m.lath[:, 0, :, h, :], m.latl[:, 0, :, h, :],
                                            h == 0, h == H - 1)
                            ins.then_inc(sem[("wo_half", "wo_done")[kk]], 1)

                wo_pe(0)
                with pe.Fori(1, HP // 2) as i:
                    wo_pe(i)
                if hf:
                    pe.wait_ge(sem["square_added"], 4 * HP)
                    sum_up(1, A[0], A[1])

            pe.wait_ge(sem["y2_done"], 2 * HP)

            def ffn_product(j, i, u):
                if u == 0:
                    stripe(S_QK + j, i, 2)
                pe.wait_ge(sem[("fk_evac", "fq_evac")[j]], 2 * i + u + (1 if j else -1))
                chunks(G[u][:, 0:HT], S_QK + j, i, 2, m.xah, m.xal, u).then_inc(sem[("fq_done", "fk_done")[j]], 1)

            def values(a):
                for j in range(4):
                    e, gh = j // 2, j % 2
                    pe.wait_ge(sem["f_pt_evac"], 4 * a + j + 1)
                    for g4 in range(4):
                        g = 4 * gh + g4
                        at = bass.ds((2 * a + e) * RA, RA) if not isinstance(a, int) \
                            else slice((2 * a + e) * RA, (2 * a + e + 1) * RA)
                        ins = pe.matmul(C[0][0:NS, g * RA:(g + 1) * RA], m.fprobs_t[:, j, g4 * NS:(g4 + 1) * NS],
                                        m.z_tok[:, g, at], start=False, stop=False, skip_group_check=True)
                ins.then_inc(sem["f_pv"], 1)

            def ffn_pe(i, product, attn, average):
                a = i - 1
                if attn:
                    pe.wait_ge(sem["fq_evac"], 2 * a + 2)
                    pe.wait_ge(sem["fk_evac"], 2 * a + 2)
                    for j in range(4):
                        e, gh = j // 2, j % 2
                        rows = slice(64 * e, 64 * e + 64)
                        if isinstance(a, int) and a == 0:
                            pe.wait_ge(sem["stat_taken"], 4)
                        else:
                            pe.wait_ge(sem["f_pt_evac"], 4 * a - 3 + j)
                        for g4 in range(4):
                            t0 = NS * (4 * gh + g4)
                            ins = pe.matmul(A[j][0:NS, g4 * NS:(g4 + 1) * NS], m.qk[0][rows, t0:t0 + NS],
                                            m.qk[1][rows, t0:t0 + NS], start=True, stop=True)
                        ins.then_inc(sem["f_s"], 1)
                if product:
                    ffn_product(0, i, 0)
                    ffn_product(0, i, 1)
                if average:
                    values(i - 2)
                if product:
                    ffn_product(1, i, 0)
                if attn:
                    for j in range(4):
                        pe.wait_ge(sem["f_probs"], 4 * a + j + 1)
                        for g4 in range(4):
                            ins = pe.transpose(A[j][0:NS, g4 * NS:(g4 + 1) * NS], m.fprobs[:, j, g4 * NS:(g4 + 1) * NS],
                                               con[0:NS, C_IDENT:C_IDENT + NS])
                        ins.then_inc(sem["f_pt"], 1)
                if product:
                    ffn_product(1, i, 1)

            for u in range(2):
                for j in range(2):
                    if u == 0:
                        stripe(S_QK + j, 0, 0, 1)
                    else:
                        pe.wait_ge(sem["z_evac"], 3 + j)
                    for kc in range(KC):
                        if j == 0:
                            pe.wait_ge(sem["in_low_odd" if kc % 2 else "in_low_even"], KC // 2 * u + kc // 2 + 1)
                        ins = three(G[j][:, 0:HT], tile(S_QK + j, kc), half(m.xah[:, kc, :], u),
                                    half(m.xal[:, kc, :], u), kc == 0, kc == KC - 1)
                    ins.then_inc(sem[("fq_done", "fk_done")[j]], 1)
                pe.wait_ge(sem["g_lo"], 1)
                for b in range(NB // 2 * u, NB // 2 * (u + 1)):
                    if b % (NB // 2) < 2:
                        pe.wait_ge(sem[("fq_evac", "fk_evac")[b % 2]], u + 1)
                    else:
                        pe.wait_ge(sem["z_evac"], b - 1)
                    for kc in range(KC):
                        t = slice(b * NS, (b + 1) * NS)
                        ins = three(G[b % 2][0:NS, 0:H * RA], (m.xah[:, kc, t], m.xal[:, kc, t]), m.gh[:, kc, :],
                                    m.gl[:, kc, :], kc == 0, kc == KC - 1)
                    ins.then_inc(sem["z_done"], 1)
            zero = con[:, C_ZERO:C_ZERO + P]
            pe.wait_ge(sem["lat_lo"], 4 * UH)
            pe.matmul(C[0][0:NS, 0:NB * RA], zero[:, 0:NS], zero, start=True, stop=True)
            pe.wait_ge(sem["z_evac"], NB)
            ffn_pe(1, True, True, False)
            with pe.Fori(2, HP) as i:
                ffn_pe(i, True, True, True)
            ffn_pe(HP, False, True, True)
            values(HP - 1)

            pe.wait_ge(sem["fk_evac"], 2 * HP)
            for u in range(2):
                for kc in range(KC):
                    pe.wait_ge(sem["in_low_odd" if kc % 2 else "in_low_even"], KC + KC // 2 * u + kc // 2 + 1)
                    ins = three(G[u][0:RA, 0:HT], (m.ah[:, kc, :], m.al[:, kc, :]), half(m.hh[:, kc, :], u),
                                half(m.hl[:, kc, :], u), kc == 0, kc == KC - 1)
                ins.then_inc(sem["ha_done"], 1)
                if u == 0:
                    pe.wait_ge(sem["m_evac"], 1)
                    pe.wait_ge(sem["f_pt_evac"], 4 * HP)
                    for g in range(NB):
                        ins = pe.transpose(A[g // 4][0:RA, (g % 4) * NS:(g % 4 + 1) * NS], m.m_tok[:, g, :],
                                           con[0:NS, C_IDENT:C_IDENT + NS])
                        if g % 4 == 3:
                            ins.then_inc(sem["mt_done"], 1)

            def up_pe(fb, fm):
                f = FM * fb + fm
                first = isinstance(f, int) and f == 0
                k = S_MLP
                pe.wait_ge(sem["w_lo"], 2 * k + 48 * fb + 4 * fm + 1)
                for u in range(2):
                    if first:
                        pe.wait_ge(sem["u_ready"], 2)
                    else:
                        pe.wait_ge(sem["silu_done"], 2 * f - 1 + u)
                    for kc in range(KC):
                        if u == 0 and kc == KC // 2:
                            pe.wait_ge(sem["w_lo"], 2 * k + 48 * fb + 4 * fm + 2)
                        three(G[u][:, 0:HT], tile(k, kc), half(m.hh[:, kc, :], u), half(m.hl[:, kc, :], u), kc == 0, False)
                    if first:
                        pe.wait_ge(sem["u_lo"], 2)
                    pe.wait_ge(sem["b_lo"], f + 1)
                    pe.matmul(G[u][:, 0:HT], m.bstk[:, :], half(m.ustk[:, :], u), start=False, stop=True)\
                      .then_inc(sem["ff_gate"], 1)
                pe.wait_ge(sem["w_lo"], 2 * k + 48 * fb + 4 * fm + 4)
                for u in range(2):
                    if first:
                        pe.wait_ge(sem["m_tanh"], 2)
                    else:
                        pe.wait_ge(sem["ff_prod"], 2 * f - 1 + u)
                    for kc in range(KC):
                        ins = three(A[u][:, 0:HT], tile(k + 1, kc), half(m.hh[:, kc, :], u), half(m.hl[:, kc, :], u),
                                    kc == 0, kc == KC - 1)
                    ins.then_inc(sem["ff_up"], 1)

            def down_pe(fb, i, c, static_first):
                n = FM * fb + 2 * i + c
                k = S_MLP + 2 * FM + c
                pe.wait_ge(sem["w_lo"], 2 * k + 48 * fb + 4 * i + 2)
                for u in range(2):
                    if isinstance(n, int) and n == 0:
                        pe.wait_ge(sem["m_evac"], 1)
                    else:
                        pe.wait_ge(sem["down_added"], 2 * n - 1 + u)
                    for kc in range(KC):
                        if static_first:
                            pe.wait_ge(sem["ff_lo"], 2 * (FM * fb + kc) + u + 1)
                        ins = three(C[u][:, 0:HT], tile(k, kc), half(m.ffh[:, kc, :], u), half(m.ffl[:, kc, :], u),
                                    kc == 0, kc == KC - 1)
                    ins.then_inc(sem["down_done"], 1)

            def block_pe(fb):
                up_pe(fb, 0)
                with pe.Fori(1, FM) as fm:
                    up_pe(fb, fm)
                down_pe(fb, 0, 0, True)
                down_pe(fb, 0, 1, False)
                with pe.Fori(1, KC // 2) as i:
                    for c in range(2):
                        down_pe(fb, i, c, False)

            block_pe(0)
            with pe.Fori(1, FB) as fb:
                block_pe(fb)
            pe.wait_ge(sem["square_added"], 4 * HP + 2 * KC - 1)
            sum_up(0, A[0], A[1])
            pe.wait_ge(sem["square_added"], 4 * HP + 2 * KC)
            sum_up(1, A[2], A[3])


def tiles(w):
    k, n = w.shape
    return w.reshape(k // P, P, n // P, P).transpose(0, 2, 1, 3)


def stripe_of(ts):
    out = np.zeros((P, KC, P), np.float32)
    for i, t in enumerate(ts):
        out[:, i] = t
    return out


def constants(ln1, ln2):
    c = np.zeros((P, N_CONST), np.float32)
    c[:, C_IDENT:C_IDENT + P] = np.eye(P)
    c[:, C_ONES:C_ONES + P] = 1.0 / D
    r = np.arange(P)
    c[r, C_PERM + (r ^ 32)] = 1.0
    nq, lq = np.divmod(np.arange(ST), NB)
    ok = (nq[:, None] == nq[None]) & (lq[None] <= lq[:, None])
    c[:ST, C_SMASK:C_SMASK + ST] = np.where(ok, 0, NEG)
    t = np.arange(NS)
    c[:NS, C_FMASK:C_FMASK + NS] = np.where(t[None] <= t[:, None], 0, NEG)
    c[:, C_BMASK:C_BMASK + GK] = np.where((r % GQ)[:, None] == (np.arange(GK) // WIN)[None], 0, NEG)
    half_r = RR // 2
    freq = np.float32(1.0) / np.float32(10000.0) ** (np.arange(half_r, dtype=np.float32) / np.float32(half_r))
    ang = np.arange(KPAD, dtype=np.float32)[:, None] * freq
    cos, sin = np.cos(ang), np.sin(ang)
    f = r % half_r
    c[:, C_QCOS:C_QCOS + NS] = cos[:NS, f].T
    c[:, C_QSIN:C_QSIN + NS] = sin[:NS, f].T * np.where(r % RR < half_r, -1, 1)[:, None]
    c[:, C_KCOS:C_KCOS + KT * RR] = np.concatenate([cos, cos], 1).reshape(KT, P, RR).transpose(1, 0, 2).reshape(P, -1)
    c[:, C_KSIN:C_KSIN + KT * RR] = np.concatenate([-sin, sin], 1).reshape(KT, P, RR).transpose(1, 0, 2).reshape(P, -1)
    j = np.arange(GK) % WIN
    c[:GK, C_SHIFT] = j - (WIN - 2)
    c[:GK, C_ISMEAN] = j == WIN - 1
    batch = (np.arange(NG)[None] * GQ + (np.arange(GK) // WIN)[:, None]) // NS
    c[:GK, C_ROW0:C_ROW0 + NG] = batch * KPAD
    c[:GK, C_MEANROW:C_MEANROW + NG] = NB * KPAD + batch
    c[:, C_LN1:C_LN1 + KC] = ln1.reshape(KC, P).T
    c[:, C_LN2:C_LN2 + KC] = ln2.reshape(KC, P).T
    c[:, C_WSHIFT:C_WSHIFT + WIN] = np.arange(WIN) - (WIN - 2)
    for b in range(NB):
        c[:, C_BATCH + NB * b + b] = 1.0
    return c


def kernel(**inputs):
    import concourse.bacc as bacc
    from concourse.bass_utils import run_bass_kernel_spmd as run

    a = {k: np.asarray(v) for k, v in inputs.items()}
    x = a["x"].reshape(T, D)
    fm = lambda w: np.ascontiguousarray(w.reshape(-1, P, w.shape[1]).transpose(1, 0, 2))
    s = np.zeros((N_STRIPES, P, KC, P), np.float32)
    at = 0

    def put(ts):
        nonlocal at
        s[at] = stripe_of(ts)
        at += 1

    qkv, wo = tiles(a["L0_attn_weight_qkv"].T), tiles(a["L0_attn_weight_out"].T)
    ffo, ffv = tiles(a["L0_ffn_Wo"]), tiles(a["L0_ffn_Wv"])
    for i in range(HP):
        for part in range(3):
            put(qkv[:, KC * part + i])
        put(ffo[:, i])
    for i in range(HP):
        put(wo[:, i])
        put(ffv[i])
    c = a["ctx_2048"]
    pad = np.zeros((NB, KPAD, D), np.float32)
    pad[:, :LK] = c
    for b in range(NB):
        ct = tiles(pad[b].T)
        for ti in range(KT):
            put(ct[:, ti])
    dq, uq, qr = (tiles(a["L0_xattn_W_" + n]) for n in ("dq", "uq", "qr"))
    uk, uv, xo = tiles(a["L0_xattn_W_uk"].T), tiles(a["L0_xattn_W_uv"]), tiles(a["L0_xattn_W_o"])
    for i in range(3):
        put(dq[:, i])
    for hf in range(2):
        for hp in range(HP):
            put([*uq[:, 2 * hp], *uq[:, 2 * hp + 1], qr[0, hp], qr[1, hp]])
            put([qr[2, hp], *uk[2 * hp], *uk[2 * hp + 1]])
        for i in range(N_UV):
            put([uv[k, h] for h in range(4 * i, 4 * i + 4) for k in range(2)])
        for i in range(KC):
            put(xo[:KC, i])
            put(xo[KC:, i])
    fq, fk = tiles(a["L0_ffn_Wq"].T), tiles(a["L0_ffn_Wk"].T)
    for i in range(HP):
        put(fq[:, i])
        put(fk[:, i])
    fin, fup, fdn = (tiles(a["L0_ffn_" + n].T) for n in ("W_in_base", "W_up_base", "W_down"))
    for fb in range(FB):
        for i in range(FM):
            put(fin[:, FM * fb + i])
            put(fup[:, FM * fb + i])
        for i in range(KC):
            put(fdn[FM * fb:FM * (fb + 1), i])
    assert at == N_STRIPES

    seg = a["itok_BxS_0_1023"].reshape(NG, GQ).astype(np.int32)
    arrays = {
        "xT": fm(x.T), "stripes": s, "w_kvc": fm(a["L0_xattn_W_kvc"]), "w_kvcT": fm(a["L0_xattn_W_kvc"].T),
        "w_kr": fm(a["L0_xattn_W_kr"]), "mod_a": fm(a["L0_ffn_A"]), "mod_b": np.ascontiguousarray(a["L0_ffn_B"]),
        "seg_rows": np.ascontiguousarray(np.tile(seg.T, (H, 1))),
        "seg_keys": np.ascontiguousarray(np.repeat(seg.T, WIN, axis=0)),
        "const": constants(a["L0_ffn_ln1_w"], a["L0_ffn_ln2_w"]),
    }
    nc = bacc.Bacc("TRN2", target_bir_lowering=False, num_devices=1)
    args = [nc.dram_tensor(n, v.shape, mybir.dt.from_np(v.dtype), kind="ExternalInput").ap() for n, v in arrays.items()]
    args += [nc.dram_tensor(n, shape, F32, kind="Internal").ap() for n, shape in
             (("key_table", (NB * KPAD + NB, ROW)), ("x1_dram", (P, KC, T)), ("g_dram", (P, KC, H * RA)))]
    args.append(nc.dram_tensor("out", (P, KC, T), F32, kind="ExternalOutput").ap())
    build(nc, *args)
    r = run(nc, [arrays], core_ids=[0])
    return np.ascontiguousarray(r.results[0]["out"].transpose(2, 1, 0).reshape(NB, NS, D))
```
